# Optimizing a Trainium2 kernel written in Bass

```python
import numpy as np
import jax
import jax.numpy as jnp

def _softmax(x, axis=-1):
    return jax.nn.softmax(x, axis=axis)

def _gelu(x):
    return jax.nn.gelu(x, approximate=True)

def _silu(x):
    return jax.nn.silu(x)

def _sigmoid(x):
    return jax.nn.sigmoid(x)

def _layernorm(x, axis=-1, eps=1e-05):
    m = jnp.mean(x, axis=axis, keepdims=True)
    v = jnp.var(x, axis=axis, keepdims=True)
    return (x - m) / jnp.sqrt(v + eps)

def _scatter_add(tgt, idx, src, axis=0):
    return tgt.at[idx].add(src)

def _segment_sum(src, seg, n):
    return jax.ops.segment_sum(src, seg, n)
kernel_name = 'mk_seq_preln_d2_jaxref_r8_6cd992'

def setup_inputs(seed: int=0):
    np.random.seed(seed)
    _w = jnp.asarray

    def _L0_attn_setup():
        import math
        import jax, jax.numpy as jnp
        import numpy as np
        B, S, HID = (2, 128, 256)
        H, D, R = (16, 128, 64)
        KVC, QC = (64, 192)
        MAX_POS = 512

        def _lin(x, w, b):
            return x @ w.T + b

        def _rotate_half(x):
            x1, x2 = (x[..., :x.shape[-1] // 2], x[..., x.shape[-1] // 2:])
            return jnp.concatenate([-x2, x1], axis=-1)

        def _rope_tables(dim, end, theta=10000.0):
            freqs = 1.0 / theta ** (jnp.arange(0, dim, 2)[:dim // 2].astype(jnp.float32) / dim)
            f = jnp.outer(jnp.arange(end, dtype=jnp.float32), freqs)
            cos, sin = (jnp.cos(f), jnp.sin(f))
            return (jnp.concatenate([cos, cos], -1), jnp.concatenate([sin, sin], -1))

        def _reference_tuple_inner(hidden_states, W_DKV_w, W_DKV_b, W_UK_w, W_UK_b, W_UV_w, W_UV_b, W_KR_w, W_KR_b, W_DQ_w, W_DQ_b, W_UQ_w, W_UQ_b, W_QR_w, W_QR_b, W_O_w, W_O_b):
            b, s = hidden_states.shape[:2]
            c_kv = _lin(hidden_states, W_DKV_w, W_DKV_b)
            k = _lin(c_kv, W_UK_w, W_UK_b).reshape(b, s, H, D)
            v = _lin(c_kv, W_UV_w, W_UV_b).reshape(b, s, H, D)
            c_q = _lin(hidden_states, W_DQ_w, W_DQ_b)
            q = _lin(c_q, W_UQ_w, W_UQ_b).reshape(b, s, H, D)
            k_r = _lin(k, W_KR_w, W_KR_b)
            q_r = _lin(q, W_QR_w, W_QR_b)
            cos, sin = _rope_tables(R, MAX_POS)
            cos_p = cos[:s][:, None, :]
            sin_p = sin[:s][:, None, :]
            q_r = q_r * cos_p + _rotate_half(q_r) * sin_p
            k_r = k_r * cos_p + _rotate_half(k_r) * sin_p
            scale = 1.0 / math.sqrt(D)
            scores = jnp.einsum('bqhd,bkhd->bhqk', q, k) * scale
            probs = jax.nn.softmax(scores, axis=-1)
            attn = jnp.einsum('bhqk,bkhd->bqhd', probs, v).reshape(b, s, H * D)
            output = _lin(attn, W_O_w, W_O_b)
            return (output, c_kv, k_r)
        key = jax.random.key(seed)
        ks = jax.random.split(key, 17)
        w = lambda k, shape: jax.random.normal(k, shape, jnp.float32) * 0.02
        return {'hidden_states': jax.random.normal(ks[0], (B, S, HID), jnp.float32), 'W_DKV_w': w(ks[1], (KVC, HID)), 'W_DKV_b': w(ks[2], (KVC,)), 'W_UK_w': w(ks[3], (H * D, KVC)), 'W_UK_b': w(ks[4], (H * D,)), 'W_UV_w': w(ks[5], (H * D, KVC)), 'W_UV_b': w(ks[6], (H * D,)), 'W_KR_w': w(ks[7], (R, D)), 'W_KR_b': w(ks[8], (R,)), 'W_DQ_w': w(ks[9], (QC, HID)), 'W_DQ_b': w(ks[10], (QC,)), 'W_UQ_w': w(ks[11], (H * D, QC)), 'W_UQ_b': w(ks[12], (H * D,)), 'W_QR_w': w(ks[13], (R, D)), 'W_QR_b': w(ks[14], (R,)), 'W_O_w': w(ks[15], (HID, H * D)), 'W_O_b': w(ks[16], (HID,))}
    _L0_attn_in = _L0_attn_setup()

    def _L0_ffn_setup():
        import jax, jax.numpy as jnp
        import numpy as np
        from jax import lax
        B, S, H = (1, 256, 256)
        E, I, TOP_K = (64, 64, 8)
        SHARED_I = 64
        key = jax.random.key(seed)
        ks = jax.random.split(key, 8)
        sc = 0.02
        return {'hidden_states': jax.random.normal(ks[0], (B, S, H), jnp.float32), 'router_w': jax.random.normal(ks[1], (E, H), jnp.float32) * sc, 'gate_up_proj': jax.random.normal(ks[2], (E, 2 * I, H), jnp.float32) * sc, 'down_proj': jax.random.normal(ks[3], (E, H, I), jnp.float32) * sc, 'shared_gate_w': jax.random.normal(ks[4], (SHARED_I, H), jnp.float32) * sc, 'shared_up_w': jax.random.normal(ks[5], (SHARED_I, H), jnp.float32) * sc, 'shared_down_w': jax.random.normal(ks[6], (H, SHARED_I), jnp.float32) * sc, 'shared_expert_gate_w': jax.random.normal(ks[7], (1, H), jnp.float32) * sc}
    _L0_ffn_in = _L0_ffn_setup()

    def _L1_attn_setup():
        import jax, jax.numpy as jnp
        import numpy as np
        import math
        N_EMBD = 256
        N_HEADS = 16
        HEAD_DIM = N_EMBD // N_HEADS
        CTX = 256

        def alibi_bias(seq_len: int, n_heads: int) -> jnp.ndarray:
            i = jnp.arange(seq_len)[:, None]
            j = jnp.arange(seq_len)[None, :]
            pos = jnp.where(j <= i, (j - i).astype(jnp.float32), 0.0)
            slopes = 2.0 ** (-8.0 / jnp.arange(1, n_heads + 1, dtype=jnp.float32))
            return slopes[:, None, None] * pos[None, :, :]

        def causal_mask(seq_len: int) -> jnp.ndarray:
            i = jnp.arange(seq_len)[:, None]
            j = jnp.arange(seq_len)[None, :]
            return jnp.where(j > i, -jnp.inf, 0.0).astype(jnp.float32)
        key = jax.random.key(seed)
        k_x, k_qkv, k_o = jax.random.split(key, 3)
        scale = 1.0 / math.sqrt(N_EMBD)
        x = jax.random.normal(k_x, (2, CTX, N_EMBD), dtype=jnp.float32)
        W_qkv = jax.random.normal(k_qkv, (N_EMBD, 3 * N_EMBD), dtype=jnp.float32) * scale
        W_o = jax.random.normal(k_o, (N_EMBD, N_EMBD), dtype=jnp.float32) * scale
        return {'x': x, 'W_qkv': W_qkv, 'W_o': W_o}
    _L1_attn_in = _L1_attn_setup()

    def _L1_ffn_setup():
        import jax, jax.numpy as jnp
        import numpy as np
        import math
        D_MODEL = 256
        D_FF = 1024
        NUM_EXPERTS = 8
        TOP_K = 2
        CAPACITY_FACTOR = 1.25
        BATCH, SEQ = (4, 256)

        def _moe_forward(x, Wg, w1, w2):
            B, T, d = x.shape
            S = B * T
            E, K = (NUM_EXPERTS, TOP_K)
            C = math.ceil(CAPACITY_FACTOR * S * K / E)
            xr = x.reshape(S, d)
            probs = jax.nn.softmax(xr @ Wg, axis=-1)
            gate_vals, expert_idx = jax.lax.top_k(probs, K)
            flat_e = expert_idx.reshape(-1)
            oh = jax.nn.one_hot(flat_e, E, dtype=jnp.int32)
            pos = jnp.sum((jnp.cumsum(oh, axis=0) - 1) * oh, axis=1)
            kept = pos < C
            i = jnp.arange(S * K)
            slot = i % K * S + i // K
            sentinel = S * K
            pos_w = jnp.where(kept, pos, C)
            dispatch_mask = jnp.full((E, C), sentinel, dtype=jnp.int32)
            dispatch_mask = dispatch_mask.at[flat_e, pos_w].set(slot.astype(jnp.int32), mode='drop')
            combine_weights = (gate_vals * kept.reshape(S, K)).T
            dispatched = xr[dispatch_mask.reshape(-1) % S].reshape(E, C, d)
            h = jax.nn.relu(jnp.einsum('ecd,edf->ecf', dispatched, w1))
            expert_out = jnp.einsum('ecf,efd->ecd', h, w2)
            rerouted = jnp.zeros((S * K + 1, d), dtype=expert_out.dtype)
            rerouted = rerouted.at[dispatch_mask.reshape(-1)].set(expert_out.reshape(-1, d))
            rerouted = rerouted[:-1].reshape(K, S, d)
            out = jnp.einsum('ks,ksm->sm', combine_weights, rerouted)
            return out.reshape(B, T, d)
        key = jax.random.key(seed)
        k1, k2, k3, k4 = jax.random.split(key, 4)
        x = jax.random.normal(k1, (BATCH, SEQ, D_MODEL), dtype=jnp.float32)
        Wg = jax.random.normal(k2, (D_MODEL, NUM_EXPERTS), dtype=jnp.float32) * 0.02
        w1 = jax.random.normal(k3, (NUM_EXPERTS, D_MODEL, D_FF), dtype=jnp.float32) * 0.02
        w2 = jax.random.normal(k4, (NUM_EXPERTS, D_FF, D_MODEL), dtype=jnp.float32) * 0.02
        return {'x': x, 'Wg': Wg, 'w1': w1, 'w2': w2}
    _L1_ffn_in = _L1_ffn_setup()
    _d = {'L0_attn_hidden_states': _L0_attn_in['hidden_states'], 'L0_attn_W_DKV_w': _L0_attn_in['W_DKV_w'], 'L0_attn_W_DKV_b': _L0_attn_in['W_DKV_b'], 'L0_attn_W_UK_w': _L0_attn_in['W_UK_w'], 'L0_attn_W_UK_b': _L0_attn_in['W_UK_b'], 'L0_attn_W_UV_w': _L0_attn_in['W_UV_w'], 'L0_attn_W_UV_b': _L0_attn_in['W_UV_b'], 'L0_attn_W_KR_w': _L0_attn_in['W_KR_w'], 'L0_attn_W_KR_b': _L0_attn_in['W_KR_b'], 'L0_attn_W_DQ_w': _L0_attn_in['W_DQ_w'], 'L0_attn_W_DQ_b': _L0_attn_in['W_DQ_b'], 'L0_attn_W_UQ_w': _L0_attn_in['W_UQ_w'], 'L0_attn_W_UQ_b': _L0_attn_in['W_UQ_b'], 'L0_attn_W_QR_w': _L0_attn_in['W_QR_w'], 'L0_attn_W_QR_b': _L0_attn_in['W_QR_b'], 'L0_attn_W_O_w': _L0_attn_in['W_O_w'], 'L0_attn_W_O_b': _L0_attn_in['W_O_b'], 'L0_ffn_router_w': _L0_ffn_in['router_w'], 'L0_ffn_gate_up_proj': _L0_ffn_in['gate_up_proj'], 'L0_ffn_down_proj': _L0_ffn_in['down_proj'], 'L0_ffn_shared_gate_w': _L0_ffn_in['shared_gate_w'], 'L0_ffn_shared_up_w': _L0_ffn_in['shared_up_w'], 'L0_ffn_shared_down_w': _L0_ffn_in['shared_down_w'], 'L0_ffn_shared_expert_gate_w': _L0_ffn_in['shared_expert_gate_w'], 'L1_attn_W_qkv': _L1_attn_in['W_qkv'], 'L1_attn_W_o': _L1_attn_in['W_o'], 'L1_ffn_Wg': _L1_ffn_in['Wg'], 'L1_ffn_w1': _L1_ffn_in['w1'], 'L1_ffn_w2': _L1_ffn_in['w2']}
    _x0 = _d['L0_attn_hidden_states']
    _d['L0_attn_hidden_states'] = jax.random.normal(jax.random.fold_in(jax.random.key(seed), 1), (4, 512, 256), dtype=_x0.dtype)
    del _x0
    return _d

def reference(L0_attn_hidden_states, L0_attn_W_DKV_w, L0_attn_W_DKV_b, L0_attn_W_UK_w, L0_attn_W_UK_b, L0_attn_W_UV_w, L0_attn_W_UV_b, L0_attn_W_KR_w, L0_attn_W_KR_b, L0_attn_W_DQ_w, L0_attn_W_DQ_b, L0_attn_W_UQ_w, L0_attn_W_UQ_b, L0_attn_W_QR_w, L0_attn_W_QR_b, L0_attn_W_O_w, L0_attn_W_O_b, L0_ffn_router_w, L0_ffn_gate_up_proj, L0_ffn_down_proj, L0_ffn_shared_gate_w, L0_ffn_shared_up_w, L0_ffn_shared_down_w, L0_ffn_shared_expert_gate_w, L1_attn_W_qkv, L1_attn_W_o, L1_ffn_Wg, L1_ffn_w1, L1_ffn_w2):

    def _L0_attn_ref(hidden_states, W_DKV_w, W_DKV_b, W_UK_w, W_UK_b, W_UV_w, W_UV_b, W_KR_w, W_KR_b, W_DQ_w, W_DQ_b, W_UQ_w, W_UQ_b, W_QR_w, W_QR_b, W_O_w, W_O_b):
        import math
        import jax, jax.numpy as jnp
        import numpy as np
        B, S, HID = (2, 128, 256)
        H, D, R = (16, 128, 64)
        KVC, QC = (64, 192)
        MAX_POS = 512

        def _lin(x, w, b):
            return x @ w.T + b

        def _rotate_half(x):
            x1, x2 = (x[..., :x.shape[-1] // 2], x[..., x.shape[-1] // 2:])
            return jnp.concatenate([-x2, x1], axis=-1)

        def _rope_tables(dim, end, theta=10000.0):
            freqs = 1.0 / theta ** (jnp.arange(0, dim, 2)[:dim // 2].astype(jnp.float32) / dim)
            f = jnp.outer(jnp.arange(end, dtype=jnp.float32), freqs)
            cos, sin = (jnp.cos(f), jnp.sin(f))
            return (jnp.concatenate([cos, cos], -1), jnp.concatenate([sin, sin], -1))

        def _reference_tuple_inner(hidden_states, W_DKV_w, W_DKV_b, W_UK_w, W_UK_b, W_UV_w, W_UV_b, W_KR_w, W_KR_b, W_DQ_w, W_DQ_b, W_UQ_w, W_UQ_b, W_QR_w, W_QR_b, W_O_w, W_O_b):
            b, s = hidden_states.shape[:2]
            c_kv = _lin(hidden_states, W_DKV_w, W_DKV_b)
            k = _lin(c_kv, W_UK_w, W_UK_b).reshape(b, s, H, D)
            v = _lin(c_kv, W_UV_w, W_UV_b).reshape(b, s, H, D)
            c_q = _lin(hidden_states, W_DQ_w, W_DQ_b)
            q = _lin(c_q, W_UQ_w, W_UQ_b).reshape(b, s, H, D)
            k_r = _lin(k, W_KR_w, W_KR_b)
            q_r = _lin(q, W_QR_w, W_QR_b)
            cos, sin = _rope_tables(R, MAX_POS)
            cos_p = cos[:s][:, None, :]
            sin_p = sin[:s][:, None, :]
            q_r = q_r * cos_p + _rotate_half(q_r) * sin_p
            k_r = k_r * cos_p + _rotate_half(k_r) * sin_p
            scale = 1.0 / math.sqrt(D)
            scores = jnp.einsum('bqhd,bkhd->bhqk', q, k) * scale
            probs = jax.nn.softmax(scores, axis=-1)
            attn = jnp.einsum('bhqk,bkhd->bqhd', probs, v).reshape(b, s, H * D)
            output = _lin(attn, W_O_w, W_O_b)
            return (output, c_kv, k_r)
        return _reference_tuple_inner(hidden_states, W_DKV_w, W_DKV_b, W_UK_w, W_UK_b, W_UV_w, W_UV_b, W_KR_w, W_KR_b, W_DQ_w, W_DQ_b, W_UQ_w, W_UQ_b, W_QR_w, W_QR_b, W_O_w, W_O_b)[0]

    def _L0_ffn_ref(hidden_states, router_w, gate_up_proj, down_proj, shared_gate_w, shared_up_w, shared_down_w, shared_expert_gate_w):
        import jax, jax.numpy as jnp
        import numpy as np
        from jax import lax
        B, S, H = (1, 256, 256)
        E, I, TOP_K = (64, 64, 8)
        SHARED_I = 64
        b, s, h_dim = hidden_states.shape
        h = hidden_states.reshape(-1, h_dim)
        T = h.shape[0]
        shared = jnp.dot(jax.nn.silu(jnp.dot(h, shared_gate_w.T)) * jnp.dot(h, shared_up_w.T), shared_down_w.T)
        shared = jax.nn.sigmoid(jnp.dot(h, shared_expert_gate_w.T)) * shared
        logits = jnp.dot(h, router_w.T)
        probs = jax.nn.softmax(logits.astype(jnp.float32), axis=-1)
        top_vals, top_idx = lax.top_k(probs, TOP_K)
        top_vals = top_vals / jnp.sum(top_vals, axis=-1, keepdims=True)
        top_vals = top_vals.astype(h.dtype)
        comb = jnp.zeros((T, E), h.dtype).at[jnp.arange(T)[:, None], top_idx].add(top_vals)

        def body(acc, xs):
            wgu, wd, w_e = xs
            g, u = jnp.split(jnp.dot(h, wgu.T), 2, axis=-1)
            eo = jnp.dot(jax.nn.silu(g) * u, wd.T)
            return (acc + eo * w_e[:, None], None)
        expert_out, _ = lax.scan(body, jnp.zeros_like(h), (gate_up_proj, down_proj, comb.T))
        return (expert_out + shared).reshape(b, s, h_dim)

    def _L1_attn_ref(x, W_qkv, W_o):
        import jax, jax.numpy as jnp
        import numpy as np
        import math
        N_EMBD = 256
        N_HEADS = 16
        HEAD_DIM = N_EMBD // N_HEADS
        CTX = 256

        def alibi_bias(seq_len: int, n_heads: int) -> jnp.ndarray:
            i = jnp.arange(seq_len)[:, None]
            j = jnp.arange(seq_len)[None, :]
            pos = jnp.where(j <= i, (j - i).astype(jnp.float32), 0.0)
            slopes = 2.0 ** (-8.0 / jnp.arange(1, n_heads + 1, dtype=jnp.float32))
            return slopes[:, None, None] * pos[None, :, :]

        def causal_mask(seq_len: int) -> jnp.ndarray:
            i = jnp.arange(seq_len)[:, None]
            j = jnp.arange(seq_len)[None, :]
            return jnp.where(j > i, -jnp.inf, 0.0).astype(jnp.float32)
        bsz, seq_len, n_embd = x.shape
        qkv = jnp.einsum('bsd,de->bse', x, W_qkv)
        q, k, v = jnp.split(qkv, 3, axis=-1)

        def to_heads(t):
            return t.reshape(bsz, seq_len, N_HEADS, HEAD_DIM).transpose(0, 2, 1, 3)
        q, k, v = (to_heads(q), to_heads(k), to_heads(v))
        attn = jnp.einsum('bhqd,bhkd->bhqk', q, k) / math.sqrt(HEAD_DIM)
        attn = attn + alibi_bias(seq_len, N_HEADS)[None] + causal_mask(seq_len)[None, None]
        attn = jax.nn.softmax(attn, axis=-1)
        y = jnp.einsum('bhqk,bhkd->bhqd', attn, v)
        y = y.transpose(0, 2, 1, 3).reshape(bsz, seq_len, n_embd)
        return jnp.einsum('bsd,de->bse', y, W_o)

    def _L1_ffn_ref(x, Wg, w1, w2):
        import jax, jax.numpy as jnp
        import numpy as np
        import math
        D_MODEL = 256
        D_FF = 1024
        NUM_EXPERTS = 8
        TOP_K = 2
        CAPACITY_FACTOR = 1.25
        BATCH, SEQ = (4, 256)

        def _moe_forward(x, Wg, w1, w2):
            B, T, d = x.shape
            S = B * T
            E, K = (NUM_EXPERTS, TOP_K)
            C = math.ceil(CAPACITY_FACTOR * S * K / E)
            xr = x.reshape(S, d)
            probs = jax.nn.softmax(xr @ Wg, axis=-1)
            gate_vals, expert_idx = jax.lax.top_k(probs, K)
            flat_e = expert_idx.reshape(-1)
            oh = jax.nn.one_hot(flat_e, E, dtype=jnp.int32)
            pos = jnp.sum((jnp.cumsum(oh, axis=0) - 1) * oh, axis=1)
            kept = pos < C
            i = jnp.arange(S * K)
            slot = i % K * S + i // K
            sentinel = S * K
            pos_w = jnp.where(kept, pos, C)
            dispatch_mask = jnp.full((E, C), sentinel, dtype=jnp.int32)
            dispatch_mask = dispatch_mask.at[flat_e, pos_w].set(slot.astype(jnp.int32), mode='drop')
            combine_weights = (gate_vals * kept.reshape(S, K)).T
            dispatched = xr[dispatch_mask.reshape(-1) % S].reshape(E, C, d)
            h = jax.nn.relu(jnp.einsum('ecd,edf->ecf', dispatched, w1))
            expert_out = jnp.einsum('ecf,efd->ecd', h, w2)
            rerouted = jnp.zeros((S * K + 1, d), dtype=expert_out.dtype)
            rerouted = rerouted.at[dispatch_mask.reshape(-1)].set(expert_out.reshape(-1, d))
            rerouted = rerouted[:-1].reshape(K, S, d)
            out = jnp.einsum('ks,ksm->sm', combine_weights, rerouted)
            return out.reshape(B, T, d)
        return _moe_forward(x, Wg, w1, w2)
    x = L0_attn_hidden_states
    x = x + _L0_attn_ref(_layernorm(x, axis=-1), L0_attn_W_DKV_w, L0_attn_W_DKV_b, L0_attn_W_UK_w, L0_attn_W_UK_b, L0_attn_W_UV_w, L0_attn_W_UV_b, L0_attn_W_KR_w, L0_attn_W_KR_b, L0_attn_W_DQ_w, L0_attn_W_DQ_b, L0_attn_W_UQ_w, L0_attn_W_UQ_b, L0_attn_W_QR_w, L0_attn_W_QR_b, L0_attn_W_O_w, L0_attn_W_O_b)
    x = x + _L0_ffn_ref(_layernorm(x, axis=-1), L0_ffn_router_w, L0_ffn_gate_up_proj, L0_ffn_down_proj, L0_ffn_shared_gate_w, L0_ffn_shared_up_w, L0_ffn_shared_down_w, L0_ffn_shared_expert_gate_w)
    x = x + _L1_attn_ref(_layernorm(x, axis=-1), L1_attn_W_qkv, L1_attn_W_o)
    x = x + _L1_ffn_ref(_layernorm(x, axis=-1), L1_ffn_Wg, L1_ffn_w1, L1_ffn_w2)
    return x

_drawn_inputs = setup_inputs


def setup_inputs(seed=0):
    import zlib

    import numpy as np

    out = dict(_drawn_inputs(seed))
    spreads = {}
    factors = {'L0_attn_W_DKV_w': 8.0,
     'L0_attn_W_DKV_b': 8.0,
     'L0_attn_W_UK_w': 8.0,
     'L0_attn_W_UK_b': 64.0,
     'L0_attn_W_UV_w': 8.0,
     'L0_attn_W_DQ_w': 8.0,
     'L0_attn_W_DQ_b': 8.0,
     'L0_attn_W_UQ_w': 8.0,
     'L0_attn_W_UQ_b': 8.0,
     'L0_ffn_router_w': 8.0,
     'L0_ffn_gate_up_proj': 8.0,
     'L0_ffn_down_proj': 8.0,
     'L0_ffn_shared_gate_w': 8.0,
     'L0_ffn_shared_up_w': 8.0,
     'L0_ffn_shared_down_w': 8.0,
     'L0_ffn_shared_expert_gate_w': 8.0,
     'L0_attn_W_UV_b': 4.76,
     'L0_attn_W_O_b': 4.705,
     'L1_ffn_Wg': 8.0,
     'L1_ffn_w1': 8.0,
     'L1_ffn_w2': 8.0}
    for name, (base, spread) in spreads.items():
        noise = np.random.default_rng([zlib.crc32(name.encode()), seed]).standard_normal(out[name].shape)
        drawn = base * np.exp(spread * noise) if base else spread * noise
        out[name] = jnp.asarray(drawn.astype(out[name].dtype))
    for name, factor in factors.items():
        out[name] = (out[name] * factor).astype(out[name].dtype)
    return out
```

```python
from contextlib import ExitStack

import numpy as np

import concourse.bass as bass
import concourse.mybir as mybir
from concourse.alu_op_type import AluOpType as ALU

F32 = mybir.dt.float32
U32 = mybir.dt.uint32
ACT = mybir.ActivationFunctionType
AX = mybir.AxisListType

P = 128
B, S, D = 4, 512, 256
NT = B * S // P
QT = S // P
DC = D // P
EPS = 1e-5

H0, HD0, KV, QC = 16, 128, 64, 192
KA = KV + 1

E0, I0 = 64, 64
TOP0 = 8

H1, HD1 = 16, 16
HG = 4
NG = H1 // HG
VA = HD1 + 1

E1, F1 = 8, 1024
CAP = 640
CT = CAP // P
NEG = -1.0e30

CREDIT = 16


def done(n):
    return n + 1 + CREDIT


def reuse(n, depth):
    return n - depth + 1 + CREDIT


def credit(eng, *sems):
    for s in sems:
        eng.sem_inc(s, CREDIT)


def phase_semaphores(nc, ctx, prefix=""):
    taken = []

    def give_back():
        nc.clear_and_free_semaphores(taken)
        nc.all_engine_barrier()

    ctx.callback(give_back)

    def sem(name):
        taken.append(nc.alloc_semaphore(prefix + name))
        return taken[-1]

    return sem


def identity_matrix(pool, ident, made):
    pool.memset(ident[:, :], 0.0).then_inc(made, 1)
    pool.wait_ge(made, 1)
    pool.affine_select(out=ident[:, :], in_=ident[:, :], compare_op=ALU.not_equal, fill=1.0, base=0,
                       pattern=[[-1, P]], channel_multiplier=1).then_inc(made, 1)


class Norm:

    def __init__(self, nc, ctx, name, x, ident, ps_t, eps):
        sb = lambda n, s: ctx.enter_context(nc.sbuf_tensor(f"{name}_{n}", s, F32))
        sem = phase_semaphores(nc, ctx, name + "_")
        self.x, self.ident, self.ps_t, self.eps = x, ident, ps_t, eps
        self.stats = sb("stats", [P, NT, 6])
        self.meanvar = sb("meanvar", [P, NT, 2])
        self.std = sb("std", [P, NT])
        self.rstd = sb("rstd", [P, NT])
        self.xn = sb("xn", [P, 2, D])
        self.xnT = sb("xnT", [P, 2, DC, P])
        self.x_ready = sem("x_ready")
        self.stats_done = sem("stats_done")
        self.meanvar_done = sem("meanvar_done")
        self.std_done = sem("std_done")
        self.rstd_done = sem("rstd_done")
        self.xn_done = sem("xn_done")
        self.turned = sem("turned")
        self.xnT_done = sem("xnT_done")
        self.used = sem("used")
        self.copied = sem("copied")

    def vector_stats(self, dve):
        for t in range(NT):
            dve.bn_stats(self.stats[:, t, :], self.x[:, t, :]).then_inc(self.stats_done, 1)
        for t in range(NT):
            dve.wait_ge(self.stats_done, t + 1)
            dve.bn_aggr(self.meanvar[:, t, :], self.stats[:, t, :]).then_inc(self.meanvar_done, 1)
        dve.wait_ge(self.std_done, 1)
        dve.reciprocal(self.rstd[:, :], self.std[:, :]).then_inc(self.rstd_done, 1)
        dve.wait_ge(self.rstd_done, 1)

    def scalar_std(self, act):
        act.wait_ge(self.meanvar_done, NT)
        act.activation(self.std[:, :], self.meanvar[:, :, 1], ACT.Sqrt,
                       bias=self.eps[:, 0:1]).then_inc(self.std_done, 1)

    def vector_tile(self, dve, t, u, copied=False):
        dve.wait_ge(self.turned, reuse(t, 2))
        if copied:
            dve.wait_ge(self.copied, reuse(t, 2))
        dve.tensor_scalar(self.xn[:, u, :], self.x[:, t, :], self.meanvar[:, t, 0:1],
                          self.rstd[:, bass.ts(t, 1)], ALU.subtract, ALU.mult).then_inc(self.xn_done, 1)

    def tensor_turn(self, pe, t, u):
        pe.wait_ge(self.xn_done, done(t))
        pe.wait_ge(self.xnT_done, reuse(t, 2))
        for c in range(DC):
            m = pe.transpose(self.ps_t[u][:, c * P:(c + 1) * P], self.xn[:, u, c * P:(c + 1) * P],
                             self.ident[:, :])
        m.then_inc(self.turned, 1)

    def scalar_tile(self, act, t, u, copied=False):
        act.wait_ge(self.turned, done(t))
        if copied:
            act.wait_ge(self.copied, reuse(t, 2))
        act.wait_ge(self.used, reuse(t, 2))
        act.copy(self.xnT[:, u, :, :], self.ps_t[u][:, 0:D].rearrange("p (c k) -> p c k", c=DC)) \
            .then_inc(self.xnT_done, 1)


def tiles(eng, step):
    with eng.Fori(0, NT // 2) as tt:
        for u in range(2):
            step(2 * tt + u, u)


def ahead(eng, first, second):
    first(0, 0)
    with eng.Fori(0, NT // 2 - 1) as tt:
        for u in range(2):
            first(2 * tt + u + 1, 1 - u)
            second(2 * tt + u, u)
    first(NT - 1, 1)
    second(NT - 2, 0)
    second(NT - 1, 1)


def latent_prepare(nc, x, ident, eps, banks, c_aug, cT, cqT, A_all, N_all, bias_out, ins):
    with ExitStack() as ctx:
        sb = lambda n, s: ctx.enter_context(nc.sbuf_tensor(n, s, F32))
        sem = phase_semaphores(nc, ctx, "latent_prepare_")
        w_dkv = sb("w_dkv", [P, DC, KV])
        w_dq = sb("w_dq", [P, DC, QC])
        b_dkv_row = sb("b_dkv_row", [1, KV])
        b_dkv_col = sb("b_dkv_col", [KV, 1])
        b_dq = sb("b_dq", [P, 2])
        w_uq = sb("w_uq", [P, H0, QC + 1])
        w_uk = sb("w_uk", [P, H0, KA])
        w_uv = sb("w_uv", [P, H0, KA])
        w_o = sb("w_o", [P, H0, D])
        b_o = sb("b_o", [1, D])
        ones_row = sb("ones_row", [1, P])
        norm = Norm(nc, ctx, "n1", x, ident, banks[0:2], eps)
        ps_cq, ps_a, ps_c = banks[2:4], banks[4:6], banks[6:8]
        x_loaded, small_loaded, uqk_loaded, uvo_loaded = (
            sem(n) for n in ("x_loaded", "small_loaded", "uqk_loaded", "uvo_loaded"))
        made, consts = sem("made"), sem("consts")
        a_mm, a_out, n_mm, n_out = (sem(n) for n in ("a_mm", "a_out", "n_mm", "n_out"))
        c_out, cq_out = sem("c_out"), sem("cq_out")

        with nc.Block() as block:
            @block.sync
            def _(sp):
                xv = ins["hidden"].rearrange("b (t p) d -> p (b t) d", p=P)
                for g in range(4):
                    sp.dma_start(x[:, 4 * g:4 * g + 4, :], xv[:, 4 * g:4 * g + 4, :]).then_inc(x_loaded, 16)
                sp.dma_start(w_uq[:, :, :], ins["w_uq"].rearrange("(h p) k -> p h k", p=P)).then_inc(uqk_loaded, 16)
                sp.dma_start(w_uk[:, :, :], ins["w_uk"].rearrange("(h p) k -> p h k", p=P)).then_inc(uqk_loaded, 16)

            @block.scalar
            def _(act):
                small = [(w_dkv[:, :, :], ins["w_dkv"].rearrange("(c p) k -> p c k", p=P)),
                         (w_dq[:, :, :], ins["w_dq"].rearrange("(c p) k -> p c k", p=P)),
                         (b_dkv_row[:, :], ins["b_dkv"].rearrange("(a k) -> a k", a=1)),
                         (b_dkv_col[:, :], ins["b_dkv"].rearrange("(k a) -> k a", a=1)),
                         (b_dq[:, 0:1], ins["b_dq"][0:P].rearrange("(k a) -> k a", a=1)),
                         (b_dq[0:QC - P, 1:2], ins["b_dq"][P:QC].rearrange("(k a) -> k a", a=1)),
                         (b_o[:, :], ins["b_o"].rearrange("(a k) -> a k", a=1))]
                for to, of in small:
                    act.dma_start(to, of).then_inc(small_loaded, 16)
                act.dma_start(w_uv[:, :, :], ins["w_uv"].rearrange("(h p) k -> p h k", p=P)).then_inc(uvo_loaded, 16)
                act.dma_start(w_o[:, :, :], ins["w_o"].rearrange("(h p) k -> p h k", p=P)).then_inc(uvo_loaded, 16)
                credit(act, norm.xnT_done, cq_out)
                act.wait_ge(consts, 3)
                norm.scalar_std(act)
                scale = float(1.0 / np.sqrt(np.float32(HD0)))
                act.wait_ge(consts, 4)
                for j in range(H0 // 2):
                    act.wait_ge(a_mm, j + 1)
                    v = ps_a[j % 2][:, 0:4 * KA].rearrange("p (h c k) -> p h c k", h=2, c=2)
                    act.mul(A_all[:, 2 * j:2 * j + 2, 0, :], v[:, :, 0, :], scale).then_inc(a_out, 1)
                    act.mul(A_all[0:KA, 2 * j:2 * j + 2, 1, :], v[0:KA, :, 1, :], scale).then_inc(a_out, 1)
                act.wait_ge(small_loaded, 16 * 7)

                def step(t, u):
                    norm.scalar_tile(act, t, u)

                def latents(t, u):
                    act.wait_ge(norm.used, done(t))
                    m = ps_cq[u]
                    act.activation(cqT[:, 0, bass.ts(t, P)], m[:, 0:P], ACT.Identity, bias=b_dq[:, 0:1])
                    act.activation(cqT[0:QC - P, 1, bass.ts(t, P)], m[0:QC - P, P:2 * P], ACT.Identity,
                                   bias=b_dq[0:QC - P, 1:2]).then_inc(cq_out, 1)

                ahead(act, step, latents)

            @block.gpsimd
            def _(pool):
                pool.memset(c_aug[:, :, KV:KA], 1.0).then_inc(consts, 1)
                pool.memset(ones_row[:, :], 1.0).then_inc(consts, 1)
                pool.memset(eps[:, :], EPS).then_inc(consts, 1)
                pool.memset(A_all[:, :, :, :], 0.0).then_inc(consts, 1)
                identity_matrix(pool, ident, made)

            @block.vector
            def _(dve):
                credit(dve, norm.xn_done, c_out)
                dve.memset(cT[KV:KA, :], 1.0)
                dve.memset(cqT[QC - P:QC - P + 1, 1, :], 1.0)
                dve.wait_ge(x_loaded, 64)
                norm.vector_stats(dve)
                for j in range(H0 // 2):
                    dve.wait_ge(n_mm, j + 1)
                    dve.tensor_copy(N_all[:, j, :], ps_a[j % 2][:, 0:D]).then_inc(n_out, 1)
                dve.wait_ge(n_mm, H0 // 2 + 1)
                dve.tensor_copy(bias_out[:, :], ps_a[0][0:1, 0:D]).then_inc(n_out, 1)

                def latents(t, u):
                    dve.wait_ge(norm.used, done(t))
                    m = ps_c[u]
                    dve.tensor_copy(c_aug[:, t, 0:KV], m[:, 0:KV])
                    dve.tensor_scalar(cT[0:KV, bass.ts(t, P)], m[0:KV, KV:KV + P], b_dkv_col[:, 0:1],
                                      None, ALU.add).then_inc(c_out, 1)

                ahead(dve, lambda t, u: norm.vector_tile(dve, t, u), latents)

            @block.tensor
            def _(pe):
                credit(pe, norm.turned, norm.used)
                pe.wait_ge(uqk_loaded, 32)
                for j in range(H0 // 2):
                    if j >= 2:
                        pe.wait_ge(a_out, 2 * (j - 1))
                    v = ps_a[j % 2][:, 0:4 * KA].rearrange("p (h c k) -> p h c k", h=2, c=2)
                    for i in range(2):
                        h = 2 * j + i
                        pe.matmul(v[:, i, 0, :], w_uq[:, h, 0:P], w_uk[:, h, :], start=True, stop=True)
                        m = pe.matmul(v[0:KA, i, 1, :], w_uq[:, h, P:QC + 1], w_uk[:, h, :],
                                      start=True, stop=True)
                    m.then_inc(a_mm, 1)
                pe.wait_ge(uvo_loaded, 32)
                pe.wait_ge(a_out, H0)
                for j in range(H0 // 2):
                    if j >= 2:
                        pe.wait_ge(n_out, j - 1)
                    for i in range(2):
                        h = 2 * j + i
                        m = pe.matmul(ps_a[j % 2][i * KV:(i + 1) * KV, 0:D], w_uv[:, h, 0:KV], w_o[:, h, :],
                                      start=True, stop=True)
                    m.then_inc(n_mm, 1)
                pe.wait_ge(n_out, H0 // 2)
                pe.wait_ge(small_loaded, 16 * 7)
                pe.wait_ge(consts, 4)
                for h in range(H0):
                    pe.matmul(ps_a[0][0:1, 0:D], w_uv[:, h, KV:KA], w_o[:, h, :], start=(h == 0), stop=False)
                pe.matmul(ps_a[0][0:1, 0:D], ones_row[:, 0:1], b_o[:, :], start=False, stop=True).then_inc(n_mm, 1)
                pe.wait_ge(made, 2)

                def latents(t, u):
                    pe.wait_ge(norm.xnT_done, done(t))
                    pe.wait_ge(c_out, reuse(t, 2))
                    pe.wait_ge(cq_out, reuse(t, 2))
                    m, mq = ps_c[u], ps_cq[u]
                    xs = norm.xnT
                    for c in range(DC):
                        pe.matmul(m[:, 0:KV], xs[:, u, c, :], w_dkv[:, c, :], start=(c == 0), stop=False)
                    pe.matmul(m[:, 0:KV], ones_row[:, :], b_dkv_row[:, :], start=False, stop=True)
                    for to, w in ((m[0:KV, KV:KV + P], w_dkv[:, :, :]), (mq[:, 0:P], w_dq[:, :, 0:P]),
                                  (mq[0:QC - P, P:2 * P], w_dq[:, :, P:QC])):
                        for c in range(DC):
                            mm = pe.matmul(to, w[:, c, :], xs[:, u, c, :], start=(c == 0), stop=(c == DC - 1))
                    mm.then_inc(norm.used, 1)

                ahead(pe, lambda t, u: norm.tensor_turn(pe, t, u), latents)


def latent_attention(nc, ident, banks, c_aug, cT, cqT, A_all, U_all, dispatched):
    with ExitStack() as ctx:
        sb = lambda n, s: ctx.enter_context(nc.sbuf_tensor(n, s, F32))
        sem = phase_semaphores(nc, ctx, "latent_")
        A_now = sb("A_now", [P, 2, KA])
        q_now = sb("q_now", [KA, S])
        neg_max = sb("neg_max", [P, QT])
        probs = sb("probs", [P, 2, S])
        probsT = sb("probsT", [P, 2, S])
        recip = sb("recip", [P, QT, 1])
        ps_s, ps_t, ps_u, ps_q = banks[0:4], banks[4:6], banks[6], banks[7]
        mix = ps_u[:, 0:QT * KA].rearrange("p (q k) -> p q k", q=QT)
        A_staged, q_made, q_out = sem("A_staged"), sem("q_made"), sem("q_out")
        scored, maxed, exped, turned = sem("scored"), sem("maxed"), sem("exped"), sem("turned")
        copied = [sem("copied_even"), sem("copied_odd")]
        mixed, normed, recips = sem("mixed"), sem("normed"), sem("recips")
        zeros = sb("zeros", [P, CT * D])
        zero_set, cleared = sem("zero_set"), sem("cleared")

        def heads(eng, b, head):
            head(b, 0, True, False)
            with eng.Fori(1, H0 - 1) as h:
                head(b, h, False, False)
            head(b, H0 - 1, False, True)

        def unit(b, h, q):
            return (b * H0 + h) * QT + q

        def pair(b, h, q):
            return (b * H0 + h) * (QT // 2) + q // 2

        with nc.Block() as block:
            @block.sync
            def _(sp):
                sp.wait_ge(zero_set, 1)
                for e in range(E1):
                    sp.dma_start(dispatched[e * CAP:(e + 1) * CAP, :].rearrange("(p r) d -> p (r d)", p=P),
                                 zeros[:, :]).then_inc(cleared, 16)
                sp.wait_ge(cleared, 16 * E1)

            @block.gpsimd
            def _(pool):
                credit(pool, A_staged)
                pool.memset(zeros[:, :], 0.0).then_inc(zero_set, 1)
                with pool.Fori(0, B) as b:
                    with pool.Fori(0, H0) as h:
                        m = b * H0 + h
                        pool.wait_ge(q_made, reuse(m, 1))
                        pool.tensor_copy(A_now[:, :, :], A_all[:, h, :, :]).then_inc(A_staged, 1)

            @block.tensor
            def _(pe):
                credit(pe, q_made, scored, turned, mixed)

                def queries(b, h):
                    m = b * H0 + h
                    pe.wait_ge(A_staged, done(m))
                    pe.wait_ge(q_out, reuse(m, 1))
                    pe.matmul(ps_q[0:KA, :], A_now[:, 0, :], cqT[:, 0, bass.ts(b, S)], start=True, stop=False)
                    pe.matmul(ps_q[0:KA, :], A_now[0:KA, 1, :], cqT[0:KA, 1, bass.ts(b, S)],
                              start=False, stop=True).then_inc(q_made, 1)

                def scores(b, h, q):
                    if q == 0:
                        pe.wait_ge(q_out, done(b * H0 + h))
                    pe.wait_ge(exped, reuse(unit(b, h, q), 4))
                    pe.matmul(ps_s[q][:, :], q_now[:, bass.ts(q, P)], cT[:, bass.ts(b, S)],
                              start=True, stop=True).then_inc(scored, 1)

                def turn(b, h, q):
                    pe.wait_ge(exped, done(unit(b, h, q)))
                    pe.wait_ge(copied[q % 2], reuse(pair(b, h, q), 1))
                    for k in range(QT):
                        m = pe.transpose(ps_t[q % 2][:, bass.ts(k, P)], probs[:, q % 2, bass.ts(k, P)],
                                         ident[:, :])
                    m.then_inc(turned, 1)

                def mixes(b, h, q):
                    if q == 0:
                        pe.wait_ge(normed, reuse(b * H0 + h, 1))
                    pe.wait_ge(copied[q % 2], done(pair(b, h, q)))
                    for k in range(QT):
                        m = pe.matmul(mix[:, q, :], probsT[:, q % 2, bass.ts(k, P)], c_aug[:, b * QT + k, :],
                                      start=(k == 0), stop=(k == QT - 1))
                    m.then_inc(mixed, 1)

                def head(b, h, first, last):
                    scores(b, h, 2)
                    if not last:
                        queries(b, h + 1)
                    turn(b, h, 0)
                    if not first:
                        mixes(b, h - 1, 3)
                    scores(b, h, 3)
                    turn(b, h, 1)
                    mixes(b, h, 0)
                    turn(b, h, 2)
                    mixes(b, h, 1)
                    if not last:
                        scores(b, h + 1, 0)
                    turn(b, h, 3)
                    mixes(b, h, 2)
                    if not last:
                        scores(b, h + 1, 1)

                with pe.Fori(0, B) as b:
                    queries(b, 0)
                    scores(b, 0, 0)
                    scores(b, 0, 1)
                    heads(pe, b, head)
                    mixes(b, H0 - 1, 3)

            @block.scalar
            def _(act):
                credit(act, q_out, exped, copied[1])

                def queries(b, h):
                    m = b * H0 + h
                    act.wait_ge(q_made, done(m))
                    act.wait_ge(scored, done(m * QT - 1))
                    act.copy(q_now[:, :], ps_q[0:KA, :]).then_inc(q_out, 1)

                def exps(b, h, q):
                    n = unit(b, h, q)
                    act.wait_ge(maxed, done(n))
                    act.wait_ge(turned, reuse(n, 2))
                    act.activation(probs[:, q % 2, :], ps_s[q][:, :], ACT.Exp,
                                   bias=neg_max[:, q:q + 1]).then_inc(exped, 1)

                def copy(b, h, q):
                    n = unit(b, h, q)
                    act.wait_ge(turned, done(n))
                    act.wait_ge(mixed, reuse(n, 2))
                    act.copy(probsT[:, q % 2, :], ps_t[q % 2][:, :]).then_inc(copied[1], 1)

                def head(b, h, first, last):
                    exps(b, h, 1)
                    exps(b, h, 2)
                    copy(b, h, 1)
                    if not last:
                        queries(b, h + 1)
                    exps(b, h, 3)
                    if not last:
                        exps(b, h + 1, 0)
                    copy(b, h, 3)

                with act.Fori(0, B) as b:
                    queries(b, 0)
                    exps(b, 0, 0)
                    heads(act, b, head)

            @block.vector
            def _(dve):
                credit(dve, maxed, copied[0], normed)

                def maxes(b, h, q):
                    dve.wait_ge(scored, done(unit(b, h, q)))
                    dve.tensor_reduce(neg_max[:, q:q + 1], ps_s[q][:, :], AX.X, ALU.max,
                                      negate=True).then_inc(maxed, 1)

                def copy(b, h, q):
                    n = unit(b, h, q)
                    dve.wait_ge(turned, done(n))
                    dve.wait_ge(mixed, reuse(n, 2))
                    dve.tensor_copy(probsT[:, q % 2, :], ps_t[q % 2][:, :]).then_inc(copied[0], 1)

                def norms(b, h):
                    m = b * H0 + h
                    dve.wait_ge(mixed, done(m * QT + QT - 1))
                    dve.reciprocal(recip[:, :, :], mix[:, :, KV:KA]).then_inc(recips, 1)
                    dve.wait_ge(recips, m + 1)
                    dve.tensor_tensor(U_all[:, bass.ts(b, QT), h, :], mix[:, :, 0:KV],
                                      recip[:, :, :].to_broadcast([P, QT, KV]), ALU.mult).then_inc(normed, 1)

                def head(b, h, first, last):
                    maxes(b, h, 2)
                    copy(b, h, 0)
                    if not first:
                        norms(b, h - 1)
                    maxes(b, h, 3)
                    copy(b, h, 2)
                    if not last:
                        maxes(b, h + 1, 0)
                        maxes(b, h + 1, 1)

                with dve.Fori(0, B) as b:
                    maxes(b, 0, 0)
                    maxes(b, 0, 1)
                    heads(dve, b, head)
                    norms(b, H0 - 1)


def project_out(nc, name, x, ident, psum, mixes, chunks, w, bias_row=None):
    with ExitStack() as ctx:
        sb = lambda n, s: ctx.enter_context(nc.sbuf_tensor(f"{name}_{n}", s, F32))
        sem = phase_semaphores(nc, ctx, name + "_")
        W = chunks * P
        rows = sb("rows", [P, 2, W])
        turned_rows = sb("turned_rows", [P, 2, W])
        ones_row = sb("ones_row", [1, P])
        half = min(W, 512)
        wide = W > 512
        ps_t = [[psum[:, (2 * u + i) * 512:(2 * u + i) * 512 + half] for i in range(1 + wide)] for u in range(2)]
        ps_o = [psum[:, (4 + u) * 512:(4 + u) * 512 + D] for u in range(2)]
        ones_set, staged, turned = sem("ones_set"), sem("staged"), sem("turned")
        copied, copied_right, projected, added = sem("copied"), sem("copied_right"), sem("projected"), sem("added")

        with nc.Block() as block:
            @block.gpsimd
            def _(pool):
                credit(pool, staged)
                pool.memset(ones_row[:, :], 1.0).then_inc(ones_set, 1)

                def stage(t, u):
                    pool.wait_ge(turned, reuse(t, 2))
                    pool.tensor_copy(rows[:, u, :], mixes[:, t, :]).then_inc(staged, 1)

                tiles(pool, stage)

            @block.tensor
            def _(pe):
                credit(pe, turned, projected)
                pe.wait_ge(ones_set, 1)

                def turn(t, u):
                    pe.wait_ge(staged, done(t))
                    pe.wait_ge(copied, reuse(t, 2))
                    if wide:
                        pe.wait_ge(copied_right, reuse(t, 2))
                    for k in range(chunks):
                        m = pe.transpose(ps_t[u][k // 4][:, (k % 4) * P:(k % 4 + 1) * P],
                                         rows[:, u, k * P:(k + 1) * P], ident[:, :])
                    m.then_inc(turned, 1)

                def project(t, u):
                    pe.wait_ge(copied, done(t))
                    if wide:
                        pe.wait_ge(copied_right, done(t))
                    pe.wait_ge(added, reuse(t, 2))
                    for k in range(chunks):
                        m = pe.matmul(ps_o[u], turned_rows[:, u, k * P:(k + 1) * P], w[:, k, :],
                                      start=(k == 0), stop=(k == chunks - 1 and bias_row is None))
                    if bias_row is not None:
                        m = pe.matmul(ps_o[u], ones_row[:, :], bias_row[:, :], start=False, stop=True)
                    m.then_inc(projected, 1)

                ahead(pe, turn, project)

            @block.scalar
            def _(act):
                credit(act, copied)

                def copy(t, u):
                    act.wait_ge(turned, done(t))
                    act.wait_ge(projected, reuse(t, 2))
                    act.copy(turned_rows[:, u, 0:half], ps_t[u][0]).then_inc(copied, 1)

                tiles(act, copy)

            @block.vector
            def _(dve):
                credit(dve, copied_right, added)

                def copy(t, u):
                    if wide:
                        dve.wait_ge(turned, done(t))
                        dve.wait_ge(projected, reuse(t, 2))
                        dve.tensor_copy(turned_rows[:, u, half:W], ps_t[u][1]).then_inc(copied_right, 1)

                def add(t, u):
                    dve.wait_ge(projected, done(t))
                    dve.tensor_tensor(x[:, t, :], ps_o[u], x[:, t, :], ALU.add).then_inc(added, 1)

                ahead(dve, copy, add)


def experts_prepare(nc, x, ident, eps, banks, xT, comb_dram, ins):
    with ExitStack() as ctx:
        sb = lambda n, s: ctx.enter_context(nc.sbuf_tensor(n, s, F32))
        sem = phase_semaphores(nc, ctx, "experts_prepare_")
        norm = Norm(nc, ctx, "n2", x, ident, banks[0:2], eps)
        ps_l = banks[2:4]
        EA = E0 + 2
        w_r = sb("w_r", [P, DC, E0 + 1])
        logits = sb("logits", [P, NT, E0 + 1])
        top = sb("top", [P, NT, 8])
        rest = sb("rest", [P, NT, E0])
        shifted = sb("shifted", [P, NT, E0])
        chosen = sb("chosen", [P, NT, E0])
        total = sb("total", [P, NT, 1])
        comb = sb("comb", [P, NT, EA])
        combT = sb("combT", [EA, NT * P])
        w_loaded, routed = sem("w_loaded"), sem("routed")
        logit_out, max_done, rest_done, step_done = sem("logit_out"), sem("max_done"), sem("rest_done"), sem("step_done")
        exp_done, comb_done = sem("exp_done"), sem("comb_done")
        comb_turned, combT_done, stored = sem("comb_turned"), sem("combT_done"), sem("stored")

        with nc.Block() as block:
            @block.sync
            def _(sp):
                sp.dma_start(w_r[:, :, :], ins["w_router"].rearrange("(c p) k -> p c k", p=P)).then_inc(w_loaded, 16)
                sp.wait_ge(combT_done, NT // 4)
                sp.dma_start(comb_dram[:, :], combT[:, :]).then_inc(stored, 16)
                sp.wait_ge(stored, 16)

            @block.gpsimd
            def _(pool):
                credit(pool, norm.copied)

                def copy(t, u):
                    pool.wait_ge(norm.xnT_done, done(t))
                    pool.tensor_copy(xT[:, :, bass.ts(t, P)], norm.xnT[:, u, :, :]).then_inc(norm.copied, 1)

                tiles(pool, copy)

            @block.scalar
            def _(act):
                credit(act, norm.xnT_done)
                norm.scalar_std(act)
                tiles(act, lambda t, u: norm.scalar_tile(act, t, u, copied=True))
                act.wait_ge(step_done, 2)
                act.activation(shifted[:, :, :], shifted[:, :, :], ACT.Exp).then_inc(exp_done, 1)
                act.activation(comb[:, :, E0:E0 + 1], logits[:, :, E0:E0 + 1], ACT.Sigmoid).then_inc(exp_done, 1)
                for g in range(NT // 4):
                    act.wait_ge(comb_turned, g + 1)
                    act.copy(combT[:, g * 512:(g + 1) * 512], banks[4 + g][0:EA, :]).then_inc(combT_done, 1)

            @block.vector
            def _(dve):
                credit(dve, norm.xn_done, logit_out)
                norm.vector_stats(dve)

                def logit(t, u):
                    dve.wait_ge(norm.used, done(t))
                    dve.tensor_copy(logits[:, t, :], ps_l[u][:, 0:E0 + 1]).then_inc(logit_out, 1)

                ahead(dve, lambda t, u: norm.vector_tile(dve, t, u), logit)
                dve.wait_ge(logit_out, done(NT - 1))
                dve.memset(comb[:, :, E0 + 1:EA], 0.0).then_inc(step_done, 1)
                for t in range(NT):
                    dve.max(top[:, t, :], logits[:, t, 0:E0]).then_inc(max_done, 1)
                dve.wait_ge(max_done, NT)
                dve.tensor_tensor(shifted[:, :, :], logits[:, :, 0:E0], top[:, :, 0:1].to_broadcast([P, NT, E0]),
                                  ALU.subtract).then_inc(step_done, 1)
                for t in range(NT):
                    dve.match_replace(rest[:, t, :], top[:, t, :], logits[:, t, 0:E0], -3.0e38).then_inc(rest_done, 1)
                dve.wait_ge(rest_done, NT)
                dve.tensor_tensor(chosen[:, :, :], rest[:, :, :], logits[:, :, 0:E0],
                                  ALU.not_equal).then_inc(step_done, 1)
                dve.wait_ge(step_done, 3)
                dve.wait_ge(exp_done, 1)
                dve.tensor_tensor(chosen[:, :, :], chosen[:, :, :], shifted[:, :, :], ALU.mult).then_inc(step_done, 1)
                dve.wait_ge(step_done, 4)
                dve.tensor_reduce(total[:, :, 0], chosen[:, :, :], AX.X, ALU.add).then_inc(step_done, 1)
                dve.wait_ge(step_done, 5)
                dve.reciprocal(total[:, :, :], total[:, :, :]).then_inc(step_done, 1)
                dve.wait_ge(step_done, 6)
                dve.tensor_tensor(comb[:, :, 0:E0], chosen[:, :, :], total[:, :, :].to_broadcast([P, NT, E0]),
                                  ALU.mult).then_inc(comb_done, 1)

            @block.tensor
            def _(pe):
                credit(pe, norm.turned, norm.used)
                pe.wait_ge(w_loaded, 16)

                def route(t, u):
                    pe.wait_ge(norm.xnT_done, done(t))
                    pe.wait_ge(logit_out, reuse(t, 2))
                    for c in range(DC):
                        m = pe.matmul(ps_l[u][:, 0:E0 + 1], norm.xnT[:, u, c, :], w_r[:, c, :],
                                      start=(c == 0), stop=(c == DC - 1))
                    m.then_inc(norm.used, 1)

                ahead(pe, lambda t, u: norm.tensor_turn(pe, t, u), route)
                pe.wait_ge(comb_done, 1)
                pe.wait_ge(exp_done, 2)
                for t in range(NT):
                    m = pe.transpose(banks[4 + t // 4][0:EA, (t % 4) * P:(t % 4 + 1) * P], comb[:, t, :], ident[:, :])
                    if t % 4 == 3:
                        m.then_inc(comb_turned, 1)


def experts(nc, x, psum, xT, comb_dram, ins):
    with ExitStack() as ctx:
        sb = lambda n, s: ctx.enter_context(nc.sbuf_tensor(n, s, F32))
        sem = phase_semaphores(nc, ctx, "experts_")
        PR = 4
        TURNS = E0 // 2 // PR
        UNITS = PR * B
        w_gu = sb("w_gu", [P, PR, 2, DC, P])
        w_d = sb("w_d", [P, PR, D])
        weight = sb("weight", [P, 4, S])
        gate = sb("gate", [P, 2, S])
        scaled = sb("scaled", [P, 2, S])
        hidden = sb("hidden", [P, 2, S])
        ps_g = [psum[:, u * 512:(u + 1) * 512] for u in range(2)]
        ps_u = [psum[:, (2 + u) * 512:(3 + u) * 512] for u in range(2)]
        ps_o = [psum[:, (4 + 2 * u) * 512:(6 + 2 * u) * 512] for u in range(2)]
        w_loaded = [sem(f"w_loaded{p}") for p in range(PR)]
        weight_loaded = [sem(f"weight_loaded{k}") for k in range(4)]
        gu_done, silu_done, scaled_done, hidden_done = (
            sem(n) for n in ("gu_done", "silu_done", "scaled_done", "hidden_done"))
        down_done, added = sem("down_done"), sem("added")

        def unit(g, k):
            return B + g * UNITS + k

        with nc.Block() as block:
            @block.sync
            def _(sp):
                def load_weights(p, pair):
                    sp.dma_start(w_gu[:, p, :, :, :], ins["w_gu0"][pair]
                                 .rearrange("g (c k) m -> k g c m", k=P)).then_inc(w_loaded[p], 16)
                    sp.dma_start(w_d[:, p, :], ins["w_d0"][pair]).then_inc(w_loaded[p], 16)

                def load_weight(n, k, pair, b):
                    sp.wait_ge(scaled_done, reuse(n, 4))
                    for i in range(2):
                        sp.dma_start(weight[i * I0:(i + 1) * I0, k % 4, :],
                                     comb_dram[bass.ds(2 * pair + i, 1), b * S:(b + 1) * S].to_broadcast([I0, S])) \
                            .then_inc(weight_loaded[k % 4], 16)

                def turn(g, last):
                    for k in range(UNITS):
                        if k == 0 or k > UNITS - PR and not last:
                            sp.wait_ge(down_done, done(unit(g, k) - 1))
                            load_weights((k - 1) % PR, g * PR + PR - 1 if k == 0 else (g + 1) * PR + (k - 1) % PR)
                        if k + 4 < UNITS:
                            load_weight(unit(g, k) + 4, k + 4, g * PR + k % PR, (k + 4) // PR)
                        elif not last:
                            load_weight(unit(g, k) + 4, k + 4, (g + 1) * PR + k % PR, 0)

                load_weights(PR - 1, E0 // 2)
                for b in range(B):
                    load_weight(b, b, E0 // 2, b)
                for p in range(PR - 1):
                    load_weights(p, p)
                for p in range(PR):
                    load_weight(B + p, p, p, 0)
                with sp.Fori(0, TURNS - 1) as g:
                    turn(g, False)
                turn(TURNS - 1, True)

            @block.tensor
            def _(pe):
                credit(pe, gu_done, down_done)

                def gates_ups(n, p, b, u):
                    pe.wait_ge(silu_done, reuse(n, 2))
                    pe.wait_ge(hidden_done, reuse(n, 2))
                    for i, to in ((0, ps_g[u]), (1, ps_u[u])):
                        for c in range(DC):
                            m = pe.matmul(to, w_gu[:, p, i, c, :], xT[:, c, b * S:(b + 1) * S],
                                          start=(c == 0), stop=(c == DC - 1))
                    m.then_inc(gu_done, 1)

                def down(n, p, b, u, first, last, add):
                    pe.wait_ge(hidden_done, done(n))
                    if first:
                        pe.wait_ge(added, reuse(add, 2))
                    for q in range(QT):
                        m = pe.matmul(ps_o[b % 2][:, q * D:(q + 1) * D], hidden[:, u, q * P:(q + 1) * P],
                                      w_d[:, p, :], start=(first and q % 2 == 0), stop=last,
                                      skip_group_check=True)
                    m.then_inc(down_done, 1)

                pe.wait_ge(w_loaded[PR - 1], 32)
                for b in range(B):
                    gates_ups(b, PR - 1, b, b % 2)
                    if b > 0:
                        down(b - 1, PR - 1, b - 1, (b - 1) % 2, True, True, b - 1)
                down(B - 1, PR - 1, B - 1, 1, True, True, B - 1)
                with pe.Fori(0, TURNS) as g:
                    def down_k(k):
                        b, p = k // PR, k % PR
                        down(unit(g, k), p, b, k % 2, p == 0, p == PR - 1, B + g * B + b)

                    for k in range(UNITS):
                        b, p = k // PR, k % PR
                        if b == 0:
                            pe.wait_ge(w_loaded[p], 32 * g + (64 if p == PR - 1 else 32))
                        gates_ups(unit(g, k), p, b, k % 2)
                        if k > 0:
                            down_k(k - 1)
                    down_k(UNITS - 1)

            @block.scalar
            def _(act):
                credit(act, silu_done)

                def silu(n, u):
                    act.wait_ge(gu_done, done(n))
                    act.wait_ge(scaled_done, reuse(n, 2))
                    act.activation(gate[:, u, :], ps_g[u], ACT.Silu).then_inc(silu_done, 1)

                for b in range(B):
                    silu(b, b % 2)
                with act.Fori(0, TURNS) as g:
                    for k in range(UNITS):
                        silu(unit(g, k), k % 2)

            @block.gpsimd
            def _(pool):
                credit(pool, scaled_done)

                def scale(n, u, buffer, loads):
                    pool.wait_ge(silu_done, done(n))
                    pool.wait_ge(weight_loaded[buffer], 16 * loads)
                    pool.wait_ge(hidden_done, reuse(n, 2))
                    pool.tensor_tensor(scaled[:, u, :], gate[:, u, :], weight[:, buffer, :],
                                       ALU.mult).then_inc(scaled_done, 1)

                for b in range(B):
                    scale(b, b % 2, b, 2)
                with pool.Fori(0, TURNS) as g:
                    for k in range(UNITS):
                        scale(unit(g, k), k % 2, k % 4, 2 * (g * (UNITS // 4) + k // 4 + 2))

            @block.vector
            def _(dve):
                credit(dve, hidden_done, added)

                def hide(n, u):
                    dve.wait_ge(scaled_done, done(n))
                    dve.wait_ge(down_done, reuse(n, 2))
                    dve.tensor_tensor(hidden[:, u, :], ps_u[u], scaled[:, u, :], ALU.mult).then_inc(hidden_done, 1)

                def add(n, b):
                    dve.wait_ge(down_done, done(n))
                    xb = x[:, b * QT:(b + 1) * QT, :].rearrange("p t d -> p (t d)")
                    dve.tensor_tensor(xb, ps_o[b % 2], xb, ALU.add).then_inc(added, 1)

                for b in range(B):
                    hide(b, b % 2)
                    if b > 0:
                        add(b - 1, b - 1)
                add(B - 1, B - 1)
                with dve.Fori(0, TURNS) as g:
                    for k in range(UNITS):
                        hide(unit(g, k), k % 2)
                        if k % PR == 0 and k > 0:
                            add(unit(g, k) - 1, k // PR - 1)
                    add(unit(g, UNITS - 1), B - 1)


def alibi_prepare(nc, x, ident, eps, banks, xT, v_aug, biases, w_out, ins):
    with ExitStack() as ctx:
        sb = lambda n, s, d=F32: ctx.enter_context(nc.sbuf_tensor(n, s, d))
        sem = phase_semaphores(nc, ctx, "alibi_prepare_")
        norm = Norm(nc, ctx, "n3", x, ident, banks[0:2], eps)
        ps_v = banks[2:4]
        w_v = sb("w_v", [P, DC, D])
        distance_int = sb("distance_int", [P, S], mybir.dt.int32)
        distance = sb("distance", [P, S])
        w_loaded, w_out_loaded, v_out, far = sem("w_loaded"), sem("w_out_loaded"), sem("v_out"), sem("far")

        with nc.Block() as block:
            @block.sync
            def _(sp):
                sp.dma_start(w_v[:, :, :], ins["w_v"].rearrange("(c p) k -> p c k", p=P)).then_inc(w_loaded, 16)
                sp.dma_start(w_out[:, :, :], ins["w_out1"].rearrange("(c p) k -> p c k", p=P)).then_inc(w_out_loaded, 16)
                sp.wait_ge(w_out_loaded, 16)

            @block.gpsimd
            def _(pool):
                credit(pool, norm.copied)
                pool.iota(distance_int[:, :], pattern=[[1, S]], base=-(QT - 1) * P, channel_multiplier=-1).then_inc(far, 1)
                pool.wait_ge(far, 1)
                pool.tensor_copy(distance[:, :], distance_int[:, :]).then_inc(far, 1)
                pool.wait_ge(far, 2)
                pool.affine_select(out=distance[:, :], in_=distance[:, :], compare_op=ALU.is_ge, fill=NEG,
                                   base=(QT - 1) * P, pattern=[[-1, S]], channel_multiplier=1).then_inc(far, 1)

                def copy(t, u):
                    pool.wait_ge(norm.xnT_done, done(t))
                    pool.tensor_copy(xT[:, :, bass.ts(t, P)], norm.xnT[:, u, :, :]).then_inc(norm.copied, 1)

                tiles(pool, copy)

            @block.scalar
            def _(act):
                credit(act, norm.xnT_done)
                norm.scalar_std(act)
                tiles(act, lambda t, u: norm.scalar_tile(act, t, u, copied=True))

            @block.vector
            def _(dve):
                credit(dve, norm.xn_done, v_out)
                norm.vector_stats(dve)
                dve.memset(v_aug[:, :, :, HD1:VA], 1.0)

                def values(t, u):
                    dve.wait_ge(norm.used, done(t))
                    dve.tensor_copy(v_aug[:, t, :, 0:HD1], ps_v[u][:, 0:D].rearrange("p (h d) -> p h d", h=H1)) \
                        .then_inc(v_out, 1)

                ahead(dve, lambda t, u: norm.vector_tile(dve, t, u), values)
                dve.wait_ge(far, 3)
                slopes = np.float32(2.0) ** (np.float32(-8.0) / np.arange(1, H1 + 1, dtype=np.float32))
                for h in range(H1):
                    dve.tensor_scalar(biases[:, h, :], distance[:, :], float(slopes[h]), None, ALU.mult)

            @block.tensor
            def _(pe):
                credit(pe, norm.turned, norm.used)
                pe.wait_ge(w_loaded, 16)

                def values(t, u):
                    pe.wait_ge(norm.xnT_done, done(t))
                    pe.wait_ge(v_out, reuse(t, 2))
                    for c in range(DC):
                        m = pe.matmul(ps_v[u][:, 0:D], norm.xnT[:, u, c, :], w_v[:, c, :],
                                      start=(c == 0), stop=(c == DC - 1))
                    m.then_inc(norm.used, 1)

                ahead(pe, lambda t, u: norm.tensor_turn(pe, t, u), values)


def alibi_attention(nc, ident, banks, xT, v_aug, biases, Y_all, ins):
    with ExitStack() as ctx:
        sb = lambda n, s: ctx.enter_context(nc.sbuf_tensor(n, s, F32))
        sem = phase_semaphores(nc, ctx, "alibi_")
        UNITS = QT * HG
        w_qk = sb("w_qk", [P, NG, 2, DC, P])
        w_now = sb("w_now", [P, 2, DC, P])
        bias_now = sb("bias_now", [P, HG, S])
        q_now = sb("q_now1", [P, S])
        k_now = sb("k_now1", [P, S])
        neg_scores = sb("neg_scores", [P, 3, S])
        neg_max = sb("neg_max1", [P, UNITS])
        probs = sb("probs1", [P, 2, S])
        probsT = sb("probsT1", [P, 2, S])
        recip = sb("recip1", [P, UNITS, 1])
        carrier = sb("carrier", [1, UNITS])
        ps_s, ps_t, ps_y, ps_q, ps_k = banks[0:3], banks[3:5], banks[5], banks[6], banks[7]
        mix = ps_y[:, 0:UNITS * VA].rearrange("p (n k) -> p n k", n=UNITS)
        w_loaded, w_staged, bias_staged = sem("w_loaded"), sem("w_staged"), sem("bias_staged")
        qk_made, q_out, k_out = sem("qk_made"), sem("q_out"), sem("k_out")
        scored, maxed, exped, turned = sem("scored"), sem("maxed"), sem("exped"), sem("turned")
        copied = [sem("copied_even"), sem("copied_odd")]
        mixed, recips, normed = sem("mixed"), sem("recips"), sem("normed")

        def turns(eng, turn):
            with eng.Fori(0, NG) as g:
                with eng.Fori(0, B) as b:
                    turn(g, b, g * B + b)

        def unit(a, k):
            return a * UNITS + k

        def pair(a, k):
            return a * (UNITS // 2) + k // 2

        def keys(k):
            return (k // HG + 1) * P

        with nc.Block() as block:
            @block.sync
            def _(sp):
                sp.dma_start(w_qk[:, :, :, :, :], ins["w_qk"].rearrange("g a (c p) m -> p g a c m", p=P)).then_inc(w_loaded, 16)

            @block.gpsimd
            def _(pool):
                credit(pool, w_staged, bias_staged)
                pool.wait_ge(w_loaded, 16)
                with pool.Fori(0, NG) as g:
                    pool.wait_ge(normed, g * B + CREDIT)
                    pool.tensor_copy(w_now[:, :, :, :], w_qk[:, g, :, :, :]).then_inc(w_staged, 1)
                    pool.tensor_copy(bias_now[:, :, :], biases[:, bass.ts(g, HG), :]).then_inc(bias_staged, 1)

            @block.tensor
            def _(pe):
                credit(pe, qk_made, scored, turned, mixed)

                def queries_keys(g, b, a):
                    pe.wait_ge(w_staged, done(g))
                    pe.wait_ge(q_out, reuse(a, 1))
                    pe.wait_ge(k_out, reuse(a, 1))
                    for i, to in ((0, ps_q), (1, ps_k)):
                        for c in range(DC):
                            m = pe.matmul(to, w_now[:, i, c, :], xT[:, c, bass.ts(b, S)],
                                          start=(c == 0), stop=(c == DC - 1))
                    m.then_inc(qk_made, 1)

                def scores(a, k):
                    if k < 3:
                        pe.wait_ge(normed, reuse(a, 1))
                    else:
                        pe.wait_ge(maxed, done(unit(a, k) - 3))
                    r, q = k % HG * 32, k // HG
                    pe.matmul(ps_s[k % 3][:, 0:keys(k)], q_now[r:r + HD1, q * P:(q + 1) * P],
                              k_now[r:r + HD1, 0:keys(k)], start=True, stop=True).then_inc(scored, 1)

                def turn_probs(a, k):
                    pe.wait_ge(exped, done(unit(a, k)))
                    pe.wait_ge(copied[k % 2], reuse(pair(a, k), 1))
                    for j in range(k // HG + 1):
                        m = pe.transpose(ps_t[k % 2][:, j * P:(j + 1) * P], probs[:, k % 2, j * P:(j + 1) * P],
                                         ident[:, :])
                    m.then_inc(turned, 1)

                def mixes(g, b, a, k):
                    pe.wait_ge(copied[k % 2], done(pair(a, k)))
                    for j in range(k // HG + 1):
                        m = pe.matmul(mix[:, k, :], probsT[:, k % 2, j * P:(j + 1) * P],
                                      v_aug[:, b * QT + j, g * HG + k % HG, :], start=(j == 0), stop=(j == k // HG))
                    m.then_inc(mixed, 1)

                def turn(g, b, a):
                    queries_keys(g, b, a)
                    pe.wait_ge(q_out, done(a))
                    pe.wait_ge(k_out, done(a))
                    scores(a, 0)
                    scores(a, 1)
                    for k in range(UNITS):
                        if k + 2 < UNITS:
                            scores(a, k + 2)
                        turn_probs(a, k)
                        if k > 0:
                            mixes(g, b, a, k - 1)
                    mixes(g, b, a, UNITS - 1)

                turns(pe, turn)

            @block.scalar
            def _(act):
                credit(act, q_out, exped, copied[1])

                def exps(a, k):
                    n = unit(a, k)
                    act.wait_ge(maxed, done(n))
                    act.wait_ge(turned, reuse(n, 2))
                    act.activation(probs[:, k % 2, 0:keys(k)], neg_scores[:, k % 3, 0:keys(k)], ACT.Exp,
                                   bias=neg_max[:, k:k + 1], scale=-1.0).then_inc(exped, 1)

                def copy(a, k):
                    n = unit(a, k)
                    act.wait_ge(turned, done(n))
                    act.wait_ge(mixed, reuse(n, 2))
                    act.copy(probsT[:, k % 2, 0:keys(k)], ps_t[k % 2][:, 0:keys(k)]).then_inc(copied[1], 1)

                def turn(g, b, a):
                    act.wait_ge(qk_made, done(a))
                    act.wait_ge(scored, done(unit(a, 0) - 1))
                    act.mul(q_now[:, :], ps_q, 1.0 / float(np.sqrt(HD1))).then_inc(q_out, 1)
                    exps(a, 0)
                    for k in range(UNITS):
                        if k + 1 < UNITS:
                            exps(a, k + 1)
                        if k % 2:
                            copy(a, k)

                turns(act, turn)

            @block.vector
            def _(dve):
                credit(dve, k_out, maxed, copied[0], normed)

                def maxes(g, a, k):
                    n = unit(a, k)
                    dve.wait_ge(scored, done(n))
                    dve.wait_ge(exped, reuse(n, 3))
                    dve.memset(carrier[:, k:k + 1], 0.0)
                    at = (QT - 1 - k // HG) * P
                    dve.tensor_tensor_reduce(neg_scores[:, k % 3, 0:keys(k)], ps_s[k % 3][:, 0:keys(k)],
                                             bias_now[:, k % HG, at:at + keys(k)], -1.0, 3.0e38, ALU.add, ALU.min,
                                             neg_max[:, k:k + 1]).then_inc(maxed, 1)

                def copy(a, k):
                    n = unit(a, k)
                    dve.wait_ge(turned, done(n))
                    dve.wait_ge(mixed, reuse(n, 2))
                    dve.tensor_copy(probsT[:, k % 2, 0:keys(k)], ps_t[k % 2][:, 0:keys(k)]).then_inc(copied[0], 1)

                def turn(g, b, a):
                    dve.wait_ge(qk_made, done(a))
                    dve.wait_ge(scored, done(unit(a, 0) - 1))
                    dve.tensor_copy(k_now[:, :], ps_k).then_inc(k_out, 1)
                    dve.wait_ge(bias_staged, done(g))
                    maxes(g, a, 0)
                    maxes(g, a, 1)
                    for k in range(UNITS):
                        if k + 2 < UNITS:
                            maxes(g, a, k + 2)
                        if k % 2 == 0:
                            copy(a, k)
                    dve.wait_ge(mixed, done(unit(a, UNITS - 1)))
                    dve.reciprocal(recip[:, :, :], mix[:, :, HD1:VA]).then_inc(recips, 1)
                    dve.wait_ge(recips, a + 1)
                    out = Y_all[:, bass.ts(b, QT), g, :].rearrange("p q (j d) -> p q j d", j=HG)
                    dve.tensor_tensor(out, mix[:, :, 0:HD1].rearrange("p (q j) d -> p q j d", j=HG),
                                      recip[:, :, :].to_broadcast([P, UNITS, HD1])
                                      .rearrange("p (q j) d -> p q j d", j=HG), ALU.mult).then_inc(normed, 1)

                turns(dve, turn)


def capacity_route(nc, x, ident, eps, banks, dispatched, slots, gates, ins):
    with ExitStack() as ctx:
        sb = lambda n, s, d=F32: ctx.enter_context(nc.sbuf_tensor(n, s, d))
        sem = phase_semaphores(nc, ctx, "capacity_route_")
        norm = Norm(nc, ctx, "n4", x, ident, banks[0:2], eps)
        ps_l, ps_before, ps_total = banks[2:4], banks[4], banks[5]
        w_g = sb("w_g", [P, DC, E1])
        xn_all = sb("xn_all", [P, NT, D])
        logits = sb("logits1", [P, NT, E1])
        top = sb("top1", [P, NT, 8])
        which = sb("which", [P, NT, 8], U32)
        which_f = sb("which_f", [P, NT, 2])
        expert_int = sb("expert_int", [P, E1], mybir.dt.int32)
        expert = sb("expert", [P, E1])
        onehot = sb("onehot", [P, 2, NT, E1])
        both = sb("both", [P, NT, E1])
        earlier = sb("earlier", [P, P])
        ones = sb("ones", [P, P])
        before = sb("before", [P, NT, E1])
        totals = sb("totals", [P, 2, NT, E1])
        placed = sb("placed", [P, 2, NT, E1])
        shifted = sb("shifted1", [P, NT, E1])
        total = sb("total1", [P, NT, 1])
        position = sb("position", [P, 2, NT])
        kept = sb("kept", [P, 2, NT])
        slot_f = sb("slot_f", [P, 2, NT])
        send = sb("send", [P, 2, NT], U32)
        w_loaded, logit_out, made = sem("w_loaded"), sem("logit_out"), sem("made")
        topped, step, counted, exped, sent = sem("topped"), sem("step"), sem("counted"), sem("exped"), sem("sent")

        with nc.Block() as block:
            @block.sync
            def _(sp):
                sp.dma_start(w_g[:, :, :], ins["w_g"].rearrange("(c p) k -> p c k", p=P)).then_inc(w_loaded, 16)

            @block.gpsimd
            def _(pool):
                credit(pool, norm.copied)
                pool.memset(ones[:, :], 1.0).then_inc(made, 1)
                pool.iota(expert_int[:, :], pattern=[[1, E1]], base=0, channel_multiplier=0).then_inc(made, 1)
                pool.wait_ge(made, 2)
                pool.tensor_copy(expert[:, :], expert_int[:, :]).then_inc(made, 1)
                pool.affine_select(out=earlier[:, :], in_=ones[:, :], compare_op=ALU.is_gt, fill=0.0, base=0,
                                   pattern=[[1, P]], channel_multiplier=-1).then_inc(made, 1)

                def copy(t, u):
                    pool.wait_ge(norm.xn_done, done(t))
                    pool.tensor_copy(xn_all[:, t, :], norm.xn[:, u, :]).then_inc(norm.copied, 1)

                tiles(pool, copy)
                pool.wait_ge(norm.copied, done(NT - 1))
                pool.wait_ge(step, 9)
                for t in range(NT):
                    for i in range(2):
                        pool.indirect_dma_start(dispatched[:, :], bass.IndirectOffsetOnAxis(ap=send[:, i, t:t + 1], axis=0),
                                                xn_all[:, t, :], None, bounds_check=E1 * CAP - 1,
                                                oob_is_err=False).then_inc(sent, 16)
                pool.wait_ge(sent, 16 * 2 * NT)

            @block.scalar
            def _(act):
                credit(act, norm.xnT_done)
                norm.scalar_std(act)
                tiles(act, lambda t, u: norm.scalar_tile(act, t, u))
                act.wait_ge(step, 1)
                act.activation(shifted[:, :, :], shifted[:, :, :], ACT.Exp).then_inc(exped, 1)

            @block.vector
            def _(dve):
                credit(dve, norm.xn_done, logit_out)
                norm.vector_stats(dve)

                def logit(t, u):
                    dve.wait_ge(norm.used, done(t))
                    dve.tensor_copy(logits[:, t, :], ps_l[u][:, 0:E1]).then_inc(logit_out, 1)

                ahead(dve, lambda t, u: norm.vector_tile(dve, t, u, copied=True), logit)
                dve.wait_ge(logit_out, done(NT - 1))
                for t in range(NT):
                    dve.max(top[:, t, :], logits[:, t, :]).then_inc(topped, 1)
                dve.wait_ge(topped, NT)
                dve.tensor_tensor(shifted[:, :, :], logits[:, :, :], top[:, :, 0:1].to_broadcast([P, NT, E1]),
                                  ALU.subtract).then_inc(step, 1)
                for t in range(NT):
                    dve.max_index(which[:, t, :], top[:, t, :], logits[:, t, :]).then_inc(topped, 1)
                dve.wait_ge(topped, 2 * NT)
                dve.tensor_copy(which_f[:, :, :], which[:, :, 0:2]).then_inc(step, 1)
                dve.wait_ge(step, 2)
                dve.wait_ge(made, 4)
                for i in range(2):
                    dve.tensor_tensor(onehot[:, i, :, :], which_f[:, :, i:i + 1].to_broadcast([P, NT, E1]),
                                      expert[:, :].unsqueeze(1).to_broadcast([P, NT, E1]), ALU.is_equal).then_inc(step, 1)
                dve.wait_ge(step, 4)
                dve.tensor_tensor(both[:, :, :], onehot[:, 0, :, :], onehot[:, 1, :, :], ALU.add).then_inc(step, 1)
                dve.wait_ge(counted, 1)
                dve.memset(totals[:, 0, 0, :], 0.0)
                dve.tensor_copy(totals[:, 0, 1:NT, :],
                                ps_total[:, 0:(NT - 1) * E1].rearrange("p (t e) -> p t e", e=E1)).then_inc(topped, 1)
                n, at, lag = 2 * NT + 1, 0, 1
                dve.wait_ge(topped, n)
                while lag < NT:
                    dve.tensor_copy(totals[:, 1 - at, 0:lag, :], totals[:, at, 0:lag, :])
                    dve.tensor_tensor(totals[:, 1 - at, lag:NT, :], totals[:, at, lag:NT, :],
                                      totals[:, at, 0:NT - lag, :], ALU.add).then_inc(topped, 1)
                    n, at, lag = n + 1, 1 - at, 2 * lag
                    dve.wait_ge(topped, n)
                dve.tensor_tensor(before[:, :, :], ps_before[:, 0:NT * E1].rearrange("p (t e) -> p t e", e=E1),
                                  totals[:, at, :, :], ALU.add).then_inc(step, 1)
                dve.wait_ge(step, 6)
                for i in range(2):
                    dve.tensor_tensor(placed[:, i, :, :], onehot[:, i, :, :], before[:, :, :], ALU.mult).then_inc(topped, 1)
                dve.wait_ge(topped, n + 2)
                dve.tensor_reduce(position[:, :, :], placed[:, :, :, :], AX.X, ALU.add).then_inc(step, 1)
                dve.wait_ge(step, 7)
                dve.tensor_scalar(kept[:, :, :], position[:, :, :], float(CAP), None, ALU.is_lt).then_inc(topped, 1)
                dve.scalar_tensor_tensor(out=slot_f[:, :, :], in0=which_f[:, :, :].rearrange("p t i -> p i t"),
                                         scalar=float(CAP), in1=position[:, :, :], op0=ALU.mult, op1=ALU.add) \
                    .then_inc(topped, 1)
                dve.wait_ge(topped, n + 4)
                dve.tensor_tensor(slot_f[:, :, :], slot_f[:, :, :], kept[:, :, :], ALU.mult).then_inc(topped, 1)
                dve.tensor_scalar(position[:, :, :], kept[:, :, :], -float(2 * E1 * CAP), float(2 * E1 * CAP),
                                  ALU.mult, ALU.add).then_inc(topped, 1)
                dve.wait_ge(topped, n + 6)
                dve.tensor_copy(slots[:, :, :], slot_f[:, :, :]).then_inc(step, 1)
                dve.tensor_tensor(send[:, :, :], slot_f[:, :, :], position[:, :, :], ALU.add).then_inc(step, 1)
                dve.wait_ge(exped, 1)
                dve.tensor_reduce(total[:, :, 0], shifted[:, :, :], AX.X, ALU.add).then_inc(topped, 1)
                dve.wait_ge(topped, n + 7)
                dve.reciprocal(total[:, :, :], total[:, :, :]).then_inc(topped, 1)
                for i in range(2):
                    dve.tensor_tensor(placed[:, i, :, :], onehot[:, i, :, :], shifted[:, :, :], ALU.mult).then_inc(topped, 1)
                dve.wait_ge(topped, n + 10)
                dve.tensor_reduce(gates[:, :, :], placed[:, :, :, :], AX.X, ALU.add).then_inc(topped, 1)
                dve.wait_ge(topped, n + 11)
                dve.tensor_tensor(gates[:, :, :], gates[:, :, :], kept[:, :, :], ALU.mult).then_inc(topped, 1)
                dve.wait_ge(topped, n + 12)
                dve.tensor_tensor(gates[:, :, :], gates[:, :, :],
                                  total[:, :, 0].unsqueeze(1).to_broadcast([P, 2, NT]), ALU.mult)

            @block.tensor
            def _(pe):
                credit(pe, norm.turned, norm.used)
                pe.wait_ge(w_loaded, 16)

                def route(t, u):
                    pe.wait_ge(norm.xnT_done, done(t))
                    pe.wait_ge(logit_out, reuse(t, 2))
                    for c in range(DC):
                        m = pe.matmul(ps_l[u][:, 0:E1], norm.xnT[:, u, c, :], w_g[:, c, :],
                                      start=(c == 0), stop=(c == DC - 1))
                    m.then_inc(norm.used, 1)

                ahead(pe, lambda t, u: norm.tensor_turn(pe, t, u), route)
                pe.wait_ge(step, 5)
                pe.wait_ge(made, 4)
                rows = both[:, :, :].rearrange("p t e -> p (t e)")
                pe.matmul(ps_before[:, 0:NT * E1], earlier[:, :], rows, start=True, stop=True)
                pe.matmul(ps_total[:, 0:NT * E1], ones[:, :], rows, start=True, stop=True).then_inc(counted, 1)


def capacity_experts(nc, ident, banks, dispatched, returned, ins):
    with ExitStack() as ctx:
        sb = lambda n, s: ctx.enter_context(nc.sbuf_tensor(n, s, F32))
        sem = phase_semaphores(nc, ctx, "capacity_")
        FC = F1 // P
        HALF = CAP // 2
        w1 = sb("w1", [P, 2, DC, F1])
        w2 = sb("w2", [P, 2, FC, D])
        rows = sb("rows1", [P, 2, CT, D])
        rowsT = sb("rowsT", [P, 2, DC, CAP])
        hidden = sb("hidden1", [P, FC, CAP])
        outs = sb("outs", [P, 2, CT, D])
        ps_t, ps_h, ps_o = banks[0:2], banks[2:6], banks[6:8]
        w1_loaded = [sem(f"w1_loaded{u}") for u in range(2)]
        w2_loaded = [sem(f"w2_loaded{u}") for u in range(2)]
        rows_loaded = [sem(f"rows_loaded{u}") for u in range(2)]
        stored, outs_free = sem("stored"), sem("outs_free")
        turned, rowsT_done, up_done = sem("turned"), sem("rowsT_done"), sem("up_done")
        relu_left, relu_right, down_done, out_done = sem("relu_left"), sem("relu_right"), sem("down_done"), sem("out_done")

        def turns(eng, turn):
            with eng.Fori(0, E1 // 2) as ee:
                for u in range(2):
                    turn(2 * ee + u, ee, u)

        with nc.Block() as block:
            @block.sync
            def _(sp):
                def load(e, ee, u):
                    sp.wait_ge(turned, reuse(e * CT + CT - 1, 2 * CT))
                    sp.dma_start(rows[:, u, :, :], dispatched[bass.ds(e * CAP, CAP), :]
                                 .rearrange("(t p) d -> p t d", p=P)).then_inc(rows_loaded[u], 16)
                    sp.wait_ge(up_done, reuse(e * FC + FC - 1, 2 * FC))
                    sp.dma_start(w1[:, u, :, :], ins["w1"][bass.ds(e, 1)].rearrange("a (c p) f -> p (a c) f", p=P)) \
                        .then_inc(w1_loaded[u], 16)
                    sp.wait_ge(down_done, reuse(e * CT + CT - 1, 2 * CT))
                    sp.dma_start(w2[:, u, :, :], ins["w2"][bass.ds(e, 1)].rearrange("a (c p) d -> p (a c) d", p=P)) \
                        .then_inc(w2_loaded[u], 16)

                turns(sp, load)

            @block.gpsimd
            def _(pool):
                credit(pool, outs_free)

                def store(e, ee, u):
                    pool.wait_ge(out_done, done(e * CT + CT - 1))
                    pool.dma_start(returned[bass.ds(e * CAP, CAP), :].rearrange("(t p) d -> p t d", p=P),
                                   outs[:, u, :, :]).then_inc(stored, 16)
                    pool.wait_ge(stored, 16 * (e + 1))
                    pool.sem_inc(outs_free, 1)

                turns(pool, store)

            @block.tensor
            def _(pe):
                credit(pe, turned, up_done, down_done)

                def turn_rows(e, ee, u):
                    pe.wait_ge(rows_loaded[u], 16 * (ee + 1))
                    for t in range(CT):
                        n = e * CT + t
                        pe.wait_ge(rowsT_done, reuse(n, 2))
                        for c in range(DC):
                            m = pe.transpose(ps_t[t % 2][:, c * P:(c + 1) * P], rows[:, u, t, c * P:(c + 1) * P],
                                             ident[:, :])
                        m.then_inc(turned, 1)

                def up(e, ee, u):
                    pe.wait_ge(w1_loaded[u], 16 * (ee + 1))
                    pe.wait_ge(rowsT_done, done(e * CT + CT - 1))
                    for f in range(FC):
                        n = e * FC + f
                        pe.wait_ge(relu_left, reuse(n, 2))
                        pe.wait_ge(relu_right, reuse(n, 2))
                        for i in range(2):
                            for c in range(DC):
                                m = pe.matmul(ps_h[2 * (f % 2) + i][:, 0:HALF], w1[:, u, c, f * P:(f + 1) * P],
                                              rowsT[:, u, c, i * HALF:(i + 1) * HALF],
                                              start=(c == 0), stop=(c == DC - 1))
                        m.then_inc(up_done, 1)

                def down(e, ee, u):
                    pe.wait_ge(w2_loaded[u], 16 * (ee + 1))
                    pe.wait_ge(relu_left, done(e * FC + FC - 1))
                    pe.wait_ge(relu_right, done(e * FC + FC - 1))
                    for t in range(CT):
                        n = e * CT + t
                        pe.wait_ge(out_done, reuse(n, 2))
                        for f in range(FC):
                            m = pe.matmul(ps_o[t % 2][:, 0:D], hidden[:, f, t * P:(t + 1) * P], w2[:, u, f, :],
                                          start=(f == 0), stop=(f == FC - 1))
                        m.then_inc(down_done, 1)

                def turn(e, ee, u):
                    turn_rows(e, ee, u)
                    up(e, ee, u)
                    down(e, ee, u)

                turns(pe, turn)

            @block.scalar
            def _(act):
                credit(act, relu_left)

                def turn(e, ee, u):
                    for f in range(FC):
                        act.wait_ge(up_done, done(e * FC + f))
                        if f == 0:
                            act.wait_ge(down_done, reuse(e * CT, 1))
                        act.activation(hidden[:, f, 0:HALF], ps_h[2 * (f % 2)][:, 0:HALF], ACT.Relu).then_inc(relu_left, 1)

                turns(act, turn)

            @block.vector
            def _(dve):
                credit(dve, rowsT_done, relu_right, out_done)

                def turn(e, ee, u):
                    for t in range(CT):
                        n = e * CT + t
                        dve.wait_ge(turned, done(n))
                        if t == 0:
                            dve.wait_ge(up_done, reuse(e * FC, 1))
                        dve.tensor_copy(rowsT[:, u, :, t * P:(t + 1) * P],
                                        ps_t[t % 2][:, 0:D].rearrange("p (c k) -> p c k", c=DC)).then_inc(rowsT_done, 1)
                    for f in range(FC):
                        dve.wait_ge(up_done, done(e * FC + f))
                        if f == 0:
                            dve.wait_ge(down_done, reuse(e * CT, 1))
                        dve.tensor_scalar(hidden[:, f, HALF:CAP], ps_h[2 * (f % 2) + 1][:, 0:HALF], 0.0, None,
                                          ALU.max).then_inc(relu_right, 1)
                    for t in range(CT):
                        n = e * CT + t
                        dve.wait_ge(down_done, done(n))
                        if t == 0:
                            dve.wait_ge(outs_free, reuse(e, 2))
                        dve.tensor_copy(outs[:, u, t, :], ps_o[t % 2][:, 0:D]).then_inc(out_done, 1)

                turns(dve, turn)


def combine(nc, x, returned, slots, gates, out):
    with ExitStack() as ctx:
        sem = phase_semaphores(nc, ctx, "combine_")
        first = ctx.enter_context(nc.sbuf_tensor("first", [P, NT, D], F32))
        second = ctx.enter_context(nc.sbuf_tensor("second", [P, NT, D], F32))
        RING = 8
        fetched = [[sem(f"fetched{i}_{t}") for t in range(RING)] for i in range(2)]
        half, summed, stored = sem("half"), sem("summed"), sem("stored")

        with nc.Block() as block:
            @block.gpsimd
            def _(pool):
                for t in range(NT):
                    if t >= RING:
                        pool.wait_ge(summed, t - RING + 1)
                    for i, rows in ((0, first), (1, second)):
                        pool.indirect_dma_start(rows[:, t, :], None, returned[:, :],
                                                bass.IndirectOffsetOnAxis(ap=slots[:, i, t:t + 1], axis=0),
                                                bounds_check=E1 * CAP - 1, oob_is_err=False) \
                            .then_inc(fetched[i][t % RING], 16)

            @block.vector
            def _(dve):
                for t in range(NT):
                    dve.wait_ge(fetched[0][t % RING], 16 * (t // RING + 1))
                    dve.scalar_tensor_tensor(out=x[:, t, :], in0=first[:, t, :], scalar=gates[:, 0, t:t + 1],
                                             in1=x[:, t, :], op0=ALU.mult, op1=ALU.add).then_inc(half, 1)
                    dve.wait_ge(half, t + 1)
                    dve.wait_ge(fetched[1][t % RING], 16 * (t // RING + 1))
                    dve.scalar_tensor_tensor(out=x[:, t, :], in0=second[:, t, :], scalar=gates[:, 1, t:t + 1],
                                             in1=x[:, t, :], op0=ALU.mult, op1=ALU.add).then_inc(summed, 1)

            @block.sync
            def _(sp):
                outv = out.rearrange("b (t p) d -> p (b t) d", p=P)
                for g in range(NT // 2):
                    sp.wait_ge(summed, 2 * g + 2)
                    sp.dma_start(outv[:, 2 * g:2 * g + 2, :], x[:, 2 * g:2 * g + 2, :]).then_inc(stored, 16)
                sp.wait_ge(stored, 16 * (NT // 2))


def two_layers(nc, ins, out):
    with ExitStack() as ctx:
        sb = lambda n, s, d=F32: ctx.enter_context(nc.sbuf_tensor(n, s, d))
        x = sb("x", [P, NT, D])
        ident = sb("ident", [P, P])
        eps = sb("eps", [P, 1])
        psum = ctx.enter_context(nc.psum_tensor("psum", [P, 8 * 512], F32))
        banks = [psum[:, k * 512:(k + 1) * 512] for k in range(8)]
        comb_dram = nc.dram_tensor("comb_dram", [E0 + 2, NT * P], F32, kind="Internal").ap()
        dispatched = nc.dram_tensor("dispatched_dram", [E1 * CAP, D], F32, kind="Internal").ap()
        returned = nc.dram_tensor("returned_dram", [E1 * CAP, D], F32, kind="Internal").ap()

        with ExitStack() as latent:
            sl = lambda n, s: latent.enter_context(nc.sbuf_tensor(n, s, F32))
            U_all = sl("U_all", [P, NT, H0, KV])
            N_all = sl("N_all", [P, H0 // 2, D])
            bias_out = sl("bias_out", [1, D])
            c_aug = sl("c_aug", [P, NT, KA])
            cT = sl("cT", [KA, B * S])
            cqT = sl("cqT", [P, 2, B * S])
            A_all = sl("A_all", [P, H0, 2, KA])
            latent_prepare(nc, x, ident, eps, banks, c_aug, cT, cqT, A_all, N_all, bias_out, ins)
            latent_attention(nc, ident, banks, c_aug, cT, cqT, A_all, U_all, dispatched)
            project_out(nc, "out0", x, ident, psum, U_all[:, :, :, :].rearrange("p t h k -> p t (h k)"),
                        H0 * KV // P, N_all, bias_out)

        with ExitStack() as mixture:
            xT = mixture.enter_context(nc.sbuf_tensor("xT0", [P, DC, B * S], F32))
            experts_prepare(nc, x, ident, eps, banks, xT, comb_dram, ins)
            experts(nc, x, psum, xT, comb_dram, ins)

        with ExitStack() as alibi:
            sl = lambda n, s: alibi.enter_context(nc.sbuf_tensor(n, s, F32))
            xT = sl("xT1", [P, DC, B * S])
            v_aug = sl("v_aug", [P, NT, H1, VA])
            biases = sl("biases", [P, H1, S])
            Y_all = sl("Y_all", [P, NT, NG, HG * HD1])
            w_out1 = sl("w_out1", [P, DC, D])
            alibi_prepare(nc, x, ident, eps, banks, xT, v_aug, biases, w_out1, ins)
            alibi_attention(nc, ident, banks, xT, v_aug, biases, Y_all, ins)
            project_out(nc, "out1", x, ident, psum, Y_all[:, :, :, :].rearrange("p t g k -> p t (g k)"), DC, w_out1)

        slots = sb("slots", [P, 2, NT], U32)
        gates = sb("gates", [P, 2, NT])
        capacity_route(nc, x, ident, eps, banks, dispatched, slots, gates, ins)
        capacity_experts(nc, ident, banks, dispatched, returned, ins)
        combine(nc, x, returned, slots, gates, out)


def layout(**w):
    a = {n: np.asarray(v) for n, v in w.items()}
    at, f0 = "L0_attn_", "L0_ffn_"
    out = {"hidden": a[at + "hidden_states"]}
    out["w_dkv"], out["w_dq"] = a[at + "W_DKV_w"].T, a[at + "W_DQ_w"].T
    out["b_dkv"], out["b_dq"], out["b_o"] = a[at + "W_DKV_b"], a[at + "W_DQ_b"], a[at + "W_O_b"]
    for k in ("UQ", "UK", "UV"):
        out["w_" + k.lower()] = np.concatenate([a[f"{at}W_{k}_w"], a[f"{at}W_{k}_b"][:, None]], 1)
    out["w_o"] = a[at + "W_O_w"].T
    out["w_router"] = np.concatenate([a[f0 + "router_w"], a[f0 + "shared_expert_gate_w"]], 0).T
    gate_up = a[f0 + "gate_up_proj"].reshape(E0, 2, I0, D)
    shared = np.stack([a[f0 + "shared_gate_w"], a[f0 + "shared_up_w"]])[None]
    gate_up = np.concatenate([gate_up, shared, np.zeros_like(shared)], 0)
    out["w_gu0"] = gate_up.reshape(E0 // 2 + 1, 2, 2, I0, D).transpose(0, 2, 4, 1, 3).reshape(E0 // 2 + 1, 2, D, P)
    down = np.concatenate([a[f0 + "down_proj"], a[f0 + "shared_down_w"][None],
                           np.zeros_like(a[f0 + "shared_down_w"][None])], 0)
    out["w_d0"] = down.transpose(0, 2, 1).reshape(E0 // 2 + 1, P, D)
    qkv = a["L1_attn_W_qkv"]
    qk = qkv[:, 0:2 * D].reshape(D, 2, NG, HG, HD1).transpose(2, 1, 0, 3, 4)
    out["w_qk"] = np.concatenate([qk, np.zeros_like(qk)], -1).reshape(NG, 2, D, P)
    out["w_v"], out["w_out1"] = qkv[:, 2 * D:], a["L1_attn_W_o"]
    out["w_g"], out["w1"], out["w2"] = a["L1_ffn_Wg"], a["L1_ffn_w1"], a["L1_ffn_w2"]
    return {n: np.ascontiguousarray(v) for n, v in out.items()}


def kernel(**inputs):
    import concourse.bacc as bacc
    from concourse.bass_utils import run_bass_kernel_spmd

    nc = bacc.Bacc("TRN2", target_bir_lowering=False, num_devices=1)
    arrays = layout(**inputs)
    ins = {n: nc.dram_tensor("in_" + n, a.shape, mybir.dt.from_np(a.dtype), kind="ExternalInput").ap()
           for n, a in arrays.items()}
    out = nc.dram_tensor("out", (B, S, D), F32, kind="ExternalOutput").ap()
    two_layers(nc, ins, out)
    r = run_bass_kernel_spmd(nc, [{"in_" + n: a for n, a in arrays.items()}], core_ids=[0])
    return r.results[0]["out"]
```

```python
from contextlib import ExitStack

import numpy as np

import concourse.bass as bass
import concourse.mybir as mybir
from concourse.alu_op_type import AluOpType as ALU

F32 = mybir.dt.float32
F32R = mybir.dt.float32r
U32 = mybir.dt.uint32
ACT = mybir.ActivationFunctionType
AX = mybir.AxisListType

P = 128
B, S, D = 4, 512, 256
NT = B * S // P
QT = S // P
DC = D // P
EPS = 1e-5

H0, HD0, KV, QC = 16, 128, 64, 192
KA = KV + 1

E0, I0 = 64, 64
TOP0 = 8

H1, HD1 = 16, 16
HG = 4
NG = H1 // HG
SLOT = 32

E1, F1 = 8, 1024
CAP = 640
CT = CAP // P
NEG = -1.0e30

CREDIT = 16


def done(n):
    return n + 1 + CREDIT


def reuse(n, depth):
    return n - depth + 1 + CREDIT


def credit(eng, *sems):
    for s in sems:
        eng.sem_inc(s, CREDIT)


def phase_semaphores(nc, ctx, prefix=""):
    taken = []

    def give_back():
        nc.clear_and_free_semaphores(taken)
        nc.all_engine_barrier()

    ctx.callback(give_back)

    def sem(name):
        taken.append(nc.alloc_semaphore(prefix + name))
        return taken[-1]

    return sem


def identity_matrix(pool, ident, made):
    pool.memset(ident[:, :], 0.0).then_inc(made, 1)
    pool.wait_ge(made, 1)
    pool.affine_select(out=ident[:, :], in_=ident[:, :], compare_op=ALU.not_equal, fill=1.0, base=0,
                       pattern=[[-1, P]], channel_multiplier=1).then_inc(made, 1)


class Norm:

    def __init__(self, nc, ctx, name, x, ident, ps_t, eps):
        sb = lambda n, s: ctx.enter_context(nc.sbuf_tensor(f"{name}_{n}", s, F32))
        sem = phase_semaphores(nc, ctx, name + "_")
        self.x, self.ident, self.ps_t, self.eps = x, ident, ps_t, eps
        self.stats = sb("stats", [P, NT, 6])
        self.meanvar = sb("meanvar", [P, NT, 2])
        self.std = sb("std", [P, NT])
        self.rstd = sb("rstd", [P, NT])
        self.xn = sb("xn", [P, 2, D])
        self.xnT = sb("xnT", [P, 2, DC, P])
        self.x_ready = sem("x_ready")
        self.stats_done = sem("stats_done")
        self.meanvar_done = sem("meanvar_done")
        self.std_done = sem("std_done")
        self.rstd_done = sem("rstd_done")
        self.xn_done = sem("xn_done")
        self.turned = sem("turned")
        self.xnT_done = sem("xnT_done")
        self.used = sem("used")
        self.copied = sem("copied")

    def vector_stats(self, dve):
        for t in range(NT):
            dve.bn_stats(self.stats[:, t, :], self.x[:, t, :]).then_inc(self.stats_done, 1)
        for t in range(NT):
            dve.wait_ge(self.stats_done, t + 1)
            dve.bn_aggr(self.meanvar[:, t, :], self.stats[:, t, :]).then_inc(self.meanvar_done, 1)
        dve.wait_ge(self.std_done, 1)
        dve.reciprocal(self.rstd[:, :], self.std[:, :]).then_inc(self.rstd_done, 1)
        dve.wait_ge(self.rstd_done, 1)

    def scalar_std(self, act):
        act.wait_ge(self.meanvar_done, NT)
        act.activation(self.std[:, :], self.meanvar[:, :, 1], ACT.Sqrt,
                       bias=self.eps[:, 0:1]).then_inc(self.std_done, 1)

    def vector_tile(self, dve, t, u, copied=False):
        dve.wait_ge(self.turned, reuse(t, 2))
        if copied:
            dve.wait_ge(self.copied, reuse(t, 2))
        dve.tensor_scalar(self.xn[:, u, :], self.x[:, t, :], self.meanvar[:, t, 0:1],
                          self.rstd[:, bass.ts(t, 1)], ALU.subtract, ALU.mult).then_inc(self.xn_done, 1)

    def tensor_turn(self, pe, t, u):
        pe.wait_ge(self.xn_done, done(t))
        pe.wait_ge(self.xnT_done, reuse(t, 2))
        for c in range(DC):
            m = pe.transpose(self.ps_t[u][:, c * P:(c + 1) * P], self.xn[:, u, c * P:(c + 1) * P],
                             self.ident[:, :])
        m.then_inc(self.turned, 1)

    def scalar_tile(self, act, t, u, copied=False):
        act.wait_ge(self.turned, done(t))
        if copied:
            act.wait_ge(self.copied, reuse(t, 2))
        act.wait_ge(self.used, reuse(t, 2))
        act.copy(self.xnT[:, u, :, :], self.ps_t[u][:, 0:D].rearrange("p (c k) -> p c k", c=DC)) \
            .then_inc(self.xnT_done, 1)


def tiles(eng, step):
    with eng.Fori(0, NT // 2) as tt:
        for u in range(2):
            step(2 * tt + u, u)


def ahead(eng, first, second):
    first(0, 0)
    with eng.Fori(0, NT // 2 - 1) as tt:
        for u in range(2):
            first(2 * tt + u + 1, 1 - u)
            second(2 * tt + u, u)
    first(NT - 1, 1)
    second(NT - 2, 0)
    second(NT - 1, 1)


def latent_prepare(nc, x, ident, eps, banks, c_aug, cT, cqT, A_all, N_all, bias_out, ins):
    with ExitStack() as ctx:
        sb = lambda n, s: ctx.enter_context(nc.sbuf_tensor(n, s, F32))
        sem = phase_semaphores(nc, ctx, "latent_prepare_")
        w_dkv = sb("w_dkv", [P, DC, KV])
        w_dq = sb("w_dq", [P, DC, QC])
        b_dkv_row = sb("b_dkv_row", [1, KV])
        b_dkv_col = sb("b_dkv_col", [KV, 1])
        b_dq = sb("b_dq", [P, 2])
        w_uq = sb("w_uq", [P, H0, QC + 1])
        w_uk = sb("w_uk", [P, H0, KA])
        w_uv = sb("w_uv", [P, H0, KA])
        w_o = sb("w_o", [P, H0, D])
        b_o = sb("b_o", [1, D])
        ones_row = sb("ones_row", [1, P])
        norm = Norm(nc, ctx, "n1", x, ident, banks[0:2], eps)
        ps_cq, ps_a, ps_c = banks[2:4], banks[4:6], banks[6:8]
        x_loaded, small_loaded, uqk_loaded, uvo_loaded = (
            sem(n) for n in ("x_loaded", "small_loaded", "uqk_loaded", "uvo_loaded"))
        made, consts = sem("made"), sem("consts")
        a_mm, a_out, n_mm, n_out = (sem(n) for n in ("a_mm", "a_out", "n_mm", "n_out"))
        c_out, cq_out = sem("c_out"), sem("cq_out")

        with nc.Block() as block:
            @block.sync
            def _(sp):
                xv = ins["hidden"].rearrange("b (t p) d -> p (b t) d", p=P)
                for g in range(4):
                    sp.dma_start(x[:, 4 * g:4 * g + 4, :], xv[:, 4 * g:4 * g + 4, :]).then_inc(x_loaded, 16)
                sp.dma_start(w_uq[:, :, :], ins["w_uq"].rearrange("(h p) k -> p h k", p=P)).then_inc(uqk_loaded, 16)
                sp.dma_start(w_uk[:, :, :], ins["w_uk"].rearrange("(h p) k -> p h k", p=P)).then_inc(uqk_loaded, 16)

            @block.scalar
            def _(act):
                small = [(w_dkv[:, :, :], ins["w_dkv"].rearrange("(c p) k -> p c k", p=P)),
                         (w_dq[:, :, :], ins["w_dq"].rearrange("(c p) k -> p c k", p=P)),
                         (b_dkv_row[:, :], ins["b_dkv"].rearrange("(a k) -> a k", a=1)),
                         (b_dkv_col[:, :], ins["b_dkv"].rearrange("(k a) -> k a", a=1)),
                         (b_dq[:, 0:1], ins["b_dq"][0:P].rearrange("(k a) -> k a", a=1)),
                         (b_dq[0:QC - P, 1:2], ins["b_dq"][P:QC].rearrange("(k a) -> k a", a=1)),
                         (b_o[:, :], ins["b_o"].rearrange("(a k) -> a k", a=1))]
                for to, of in small:
                    act.dma_start(to, of).then_inc(small_loaded, 16)
                act.dma_start(w_uv[:, :, :], ins["w_uv"].rearrange("(h p) k -> p h k", p=P)).then_inc(uvo_loaded, 16)
                act.dma_start(w_o[:, :, :], ins["w_o"].rearrange("(h p) k -> p h k", p=P)).then_inc(uvo_loaded, 16)
                credit(act, norm.xnT_done, cq_out)
                act.wait_ge(consts, 3)
                norm.scalar_std(act)
                scale = float(1.0 / np.sqrt(np.float32(HD0)))
                act.wait_ge(consts, 4)
                for j in range(H0 // 2):
                    act.wait_ge(a_mm, j + 1)
                    v = ps_a[j % 2][:, 0:4 * KA].rearrange("p (h c k) -> p h c k", h=2, c=2)
                    act.mul(A_all[:, 2 * j:2 * j + 2, 0, :], v[:, :, 0, :], scale).then_inc(a_out, 1)
                    act.mul(A_all[0:KA, 2 * j:2 * j + 2, 1, :], v[0:KA, :, 1, :], scale).then_inc(a_out, 1)
                act.wait_ge(small_loaded, 16 * 7)

                def step(t, u):
                    norm.scalar_tile(act, t, u)

                def latents(t, u):
                    act.wait_ge(norm.used, done(t))
                    m = ps_cq[u]
                    act.activation(cqT[:, 0, bass.ts(t, P)], m[:, 0:P], ACT.Identity, bias=b_dq[:, 0:1])
                    act.activation(cqT[0:QC - P, 1, bass.ts(t, P)], m[0:QC - P, P:2 * P], ACT.Identity,
                                   bias=b_dq[0:QC - P, 1:2]).then_inc(cq_out, 1)

                ahead(act, step, latents)

            @block.gpsimd
            def _(pool):
                pool.memset(c_aug[:, :, KV:KA], 1.0).then_inc(consts, 1)
                pool.memset(ones_row[:, :], 1.0).then_inc(consts, 1)
                pool.memset(eps[:, :], EPS).then_inc(consts, 1)
                pool.memset(A_all[:, :, :, :], 0.0).then_inc(consts, 1)
                identity_matrix(pool, ident, made)

            @block.vector
            def _(dve):
                credit(dve, norm.xn_done, c_out)
                dve.memset(cT[KV:KA, :], 1.0)
                dve.memset(cqT[QC - P:QC - P + 1, 1, :], 1.0)
                dve.wait_ge(x_loaded, 64)
                norm.vector_stats(dve)
                for j in range(H0 // 2):
                    dve.wait_ge(n_mm, j + 1)
                    dve.tensor_copy(N_all[:, j, :], ps_a[j % 2][:, 0:D]).then_inc(n_out, 1)
                dve.wait_ge(n_mm, H0 // 2 + 1)
                dve.tensor_copy(bias_out[:, :], ps_a[0][0:1, 0:D]).then_inc(n_out, 1)

                def latents(t, u):
                    dve.wait_ge(norm.used, done(t))
                    m = ps_c[u]
                    dve.tensor_copy(c_aug[:, t, 0:KV], m[:, 0:KV])
                    dve.tensor_scalar(cT[0:KV, bass.ts(t, P)], m[0:KV, KV:KV + P], b_dkv_col[:, 0:1],
                                      None, ALU.add).then_inc(c_out, 1)

                ahead(dve, lambda t, u: norm.vector_tile(dve, t, u), latents)

            @block.tensor
            def _(pe):
                credit(pe, norm.turned, norm.used)
                pe.wait_ge(uqk_loaded, 32)
                for j in range(H0 // 2):
                    if j >= 2:
                        pe.wait_ge(a_out, 2 * (j - 1))
                    v = ps_a[j % 2][:, 0:4 * KA].rearrange("p (h c k) -> p h c k", h=2, c=2)
                    for i in range(2):
                        h = 2 * j + i
                        pe.matmul(v[:, i, 0, :], w_uq[:, h, 0:P], w_uk[:, h, :], start=True, stop=True)
                        m = pe.matmul(v[0:KA, i, 1, :], w_uq[:, h, P:QC + 1], w_uk[:, h, :],
                                      start=True, stop=True)
                    m.then_inc(a_mm, 1)
                pe.wait_ge(uvo_loaded, 32)
                pe.wait_ge(a_out, H0)
                for j in range(H0 // 2):
                    if j >= 2:
                        pe.wait_ge(n_out, j - 1)
                    for i in range(2):
                        h = 2 * j + i
                        m = pe.matmul(ps_a[j % 2][i * KV:(i + 1) * KV, 0:D], w_uv[:, h, 0:KV], w_o[:, h, :],
                                      start=True, stop=True)
                    m.then_inc(n_mm, 1)
                pe.wait_ge(n_out, H0 // 2)
                pe.wait_ge(small_loaded, 16 * 7)
                pe.wait_ge(consts, 4)
                for h in range(H0):
                    pe.matmul(ps_a[0][0:1, 0:D], w_uv[:, h, KV:KA], w_o[:, h, :], start=(h == 0), stop=False)
                pe.matmul(ps_a[0][0:1, 0:D], ones_row[:, 0:1], b_o[:, :], start=False, stop=True).then_inc(n_mm, 1)
                pe.wait_ge(made, 2)

                def latents(t, u):
                    pe.wait_ge(norm.xnT_done, done(t))
                    pe.wait_ge(c_out, reuse(t, 2))
                    pe.wait_ge(cq_out, reuse(t, 2))
                    m, mq = ps_c[u], ps_cq[u]
                    xs = norm.xnT
                    for c in range(DC):
                        pe.matmul(m[:, 0:KV], xs[:, u, c, :], w_dkv[:, c, :], start=(c == 0), stop=False)
                    pe.matmul(m[:, 0:KV], ones_row[:, :], b_dkv_row[:, :], start=False, stop=True)
                    for to, w in ((m[0:KV, KV:KV + P], w_dkv[:, :, :]), (mq[:, 0:P], w_dq[:, :, 0:P]),
                                  (mq[0:QC - P, P:2 * P], w_dq[:, :, P:QC])):
                        for c in range(DC):
                            mm = pe.matmul(to, w[:, c, :], xs[:, u, c, :], start=(c == 0), stop=(c == DC - 1))
                    mm.then_inc(norm.used, 1)

                ahead(pe, lambda t, u: norm.tensor_turn(pe, t, u), latents)


def latent_attention(nc, ident, banks, c_aug, cT, cqT, A_all, U_all, dispatched):
    with ExitStack() as ctx:
        sb = lambda n, s: ctx.enter_context(nc.sbuf_tensor(n, s, F32))
        sem = phase_semaphores(nc, ctx, "latent_")
        A_now = sb("A_now", [P, 2, KA])
        q_now = sb("q_now", [KA, S])
        neg_max = sb("neg_max", [P, QT])
        probs = sb("probs", [P, 2, S])
        probsT = sb("probsT", [P, 2, S])
        recip = sb("recip", [P, QT, 1])
        ps_s, ps_t, ps_u, ps_q = banks[0:4], banks[4:6], banks[6], banks[7]
        mix = ps_u[:, 0:QT * KA].rearrange("p (q k) -> p q k", q=QT)
        A_staged, q_made, q_out = sem("A_staged"), sem("q_made"), sem("q_out")
        scored, maxed, exped, turned = sem("scored"), sem("maxed"), sem("exped"), sem("turned")
        copied = [sem("copied_even"), sem("copied_odd")]
        mixed, normed, recips = sem("mixed"), sem("normed"), sem("recips")
        zeros = sb("zeros", [P, CT * D])
        zero_set, cleared = sem("zero_set"), sem("cleared")

        def heads(eng, b, head):
            head(b, 0, True, False)
            with eng.Fori(1, H0 - 1) as h:
                head(b, h, False, False)
            head(b, H0 - 1, False, True)

        def unit(b, h, q):
            return (b * H0 + h) * QT + q

        def pair(b, h, q):
            return (b * H0 + h) * (QT // 2) + q // 2

        with nc.Block() as block:
            @block.sync
            def _(sp):
                sp.wait_ge(zero_set, 1)
                for e in range(E1):
                    sp.dma_start(dispatched[e * CAP:(e + 1) * CAP, :].rearrange("(p r) d -> p (r d)", p=P),
                                 zeros[:, :]).then_inc(cleared, 16)
                sp.wait_ge(cleared, 16 * E1)

            @block.gpsimd
            def _(pool):
                credit(pool, A_staged)
                pool.memset(zeros[:, :], 0.0).then_inc(zero_set, 1)
                with pool.Fori(0, B) as b:
                    with pool.Fori(0, H0) as h:
                        m = b * H0 + h
                        pool.wait_ge(q_made, reuse(m, 1))
                        pool.tensor_copy(A_now[:, :, :], A_all[:, h, :, :]).then_inc(A_staged, 1)

            @block.tensor
            def _(pe):
                credit(pe, q_made, scored, turned, mixed)

                def queries(b, h):
                    m = b * H0 + h
                    pe.wait_ge(A_staged, done(m))
                    pe.wait_ge(q_out, reuse(m, 1))
                    pe.matmul(ps_q[0:KA, :], A_now[:, 0, :], cqT[:, 0, bass.ts(b, S)], start=True, stop=False)
                    pe.matmul(ps_q[0:KA, :], A_now[0:KA, 1, :], cqT[0:KA, 1, bass.ts(b, S)],
                              start=False, stop=True).then_inc(q_made, 1)

                def scores(b, h, q):
                    if q == 0:
                        pe.wait_ge(q_out, done(b * H0 + h))
                    pe.wait_ge(exped, reuse(unit(b, h, q), 4))
                    pe.matmul(ps_s[q][:, :], q_now[:, bass.ts(q, P)], cT[:, bass.ts(b, S)],
                              start=True, stop=True).then_inc(scored, 1)

                def turn(b, h, q):
                    pe.wait_ge(exped, done(unit(b, h, q)))
                    pe.wait_ge(copied[q % 2], reuse(pair(b, h, q), 1))
                    for k in range(QT):
                        m = pe.transpose(ps_t[q % 2][:, bass.ts(k, P)], probs[:, q % 2, bass.ts(k, P)],
                                         ident[:, :])
                    m.then_inc(turned, 1)

                def mixes(b, h, q):
                    if q == 0:
                        pe.wait_ge(normed, reuse(b * H0 + h, 1))
                    pe.wait_ge(copied[q % 2], done(pair(b, h, q)))
                    for k in range(QT):
                        m = pe.matmul(mix[:, q, :], probsT[:, q % 2, bass.ts(k, P)], c_aug[:, b * QT + k, :],
                                      start=(k == 0), stop=(k == QT - 1))
                    m.then_inc(mixed, 1)

                def head(b, h, first, last):
                    scores(b, h, 2)
                    if not last:
                        queries(b, h + 1)
                    turn(b, h, 0)
                    if not first:
                        mixes(b, h - 1, 3)
                    scores(b, h, 3)
                    turn(b, h, 1)
                    mixes(b, h, 0)
                    turn(b, h, 2)
                    mixes(b, h, 1)
                    if not last:
                        scores(b, h + 1, 0)
                    turn(b, h, 3)
                    mixes(b, h, 2)
                    if not last:
                        scores(b, h + 1, 1)

                with pe.Fori(0, B) as b:
                    queries(b, 0)
                    scores(b, 0, 0)
                    scores(b, 0, 1)
                    heads(pe, b, head)
                    mixes(b, H0 - 1, 3)

            @block.scalar
            def _(act):
                credit(act, q_out, exped, copied[1])

                def queries(b, h):
                    m = b * H0 + h
                    act.wait_ge(q_made, done(m))
                    act.wait_ge(scored, done(m * QT - 1))
                    act.copy(q_now[:, :], ps_q[0:KA, :]).then_inc(q_out, 1)

                def exps(b, h, q):
                    n = unit(b, h, q)
                    act.wait_ge(maxed, done(n))
                    act.wait_ge(turned, reuse(n, 2))
                    act.activation(probs[:, q % 2, :], ps_s[q][:, :], ACT.Exp,
                                   bias=neg_max[:, q:q + 1]).then_inc(exped, 1)

                def copy(b, h, q):
                    n = unit(b, h, q)
                    act.wait_ge(turned, done(n))
                    act.wait_ge(mixed, reuse(n, 2))
                    act.copy(probsT[:, q % 2, :], ps_t[q % 2][:, :]).then_inc(copied[1], 1)

                def head(b, h, first, last):
                    exps(b, h, 1)
                    exps(b, h, 2)
                    copy(b, h, 1)
                    if not last:
                        queries(b, h + 1)
                    exps(b, h, 3)
                    if not last:
                        exps(b, h + 1, 0)
                    copy(b, h, 3)

                with act.Fori(0, B) as b:
                    queries(b, 0)
                    exps(b, 0, 0)
                    heads(act, b, head)

            @block.vector
            def _(dve):
                credit(dve, maxed, copied[0], normed)

                def maxes(b, h, q):
                    dve.wait_ge(scored, done(unit(b, h, q)))
                    dve.tensor_reduce(neg_max[:, q:q + 1], ps_s[q][:, :], AX.X, ALU.max,
                                      negate=True).then_inc(maxed, 1)

                def copy(b, h, q):
                    n = unit(b, h, q)
                    dve.wait_ge(turned, done(n))
                    dve.wait_ge(mixed, reuse(n, 2))
                    dve.tensor_copy(probsT[:, q % 2, :], ps_t[q % 2][:, :]).then_inc(copied[0], 1)

                def norms(b, h):
                    m = b * H0 + h
                    dve.wait_ge(mixed, done(m * QT + QT - 1))
                    dve.reciprocal(recip[:, :, :], mix[:, :, KV:KA]).then_inc(recips, 1)
                    dve.wait_ge(recips, m + 1)
                    dve.tensor_tensor(U_all[:, bass.ts(b, QT), h, :], mix[:, :, 0:KV],
                                      recip[:, :, :].to_broadcast([P, QT, KV]), ALU.mult).then_inc(normed, 1)

                def head(b, h, first, last):
                    maxes(b, h, 2)
                    copy(b, h, 0)
                    if not first:
                        norms(b, h - 1)
                    maxes(b, h, 3)
                    copy(b, h, 2)
                    if not last:
                        maxes(b, h + 1, 0)
                        maxes(b, h + 1, 1)

                with dve.Fori(0, B) as b:
                    maxes(b, 0, 0)
                    maxes(b, 0, 1)
                    heads(dve, b, head)
                    norms(b, H0 - 1)


def project_out(nc, name, x, ident, psum, mixes, chunks, w, bias_row=None):
    with ExitStack() as ctx:
        sb = lambda n, s: ctx.enter_context(nc.sbuf_tensor(f"{name}_{n}", s, F32))
        sem = phase_semaphores(nc, ctx, name + "_")
        W = chunks * P
        rows = sb("rows", [P, 2, W])
        turned_rows = sb("turned_rows", [P, 2, W])
        ones_row = sb("ones_row", [1, P])
        half = min(W, 512)
        wide = W > 512
        ps_t = [[psum[:, (2 * u + i) * 512:(2 * u + i) * 512 + half] for i in range(1 + wide)] for u in range(2)]
        ps_o = [psum[:, (4 + u) * 512:(4 + u) * 512 + D] for u in range(2)]
        ones_set, staged, turned = sem("ones_set"), sem("staged"), sem("turned")
        copied, copied_right, projected, added = sem("copied"), sem("copied_right"), sem("projected"), sem("added")

        with nc.Block() as block:
            @block.gpsimd
            def _(pool):
                credit(pool, staged)
                pool.memset(ones_row[:, :], 1.0).then_inc(ones_set, 1)

                def stage(t, u):
                    pool.wait_ge(turned, reuse(t, 2))
                    pool.tensor_copy(rows[:, u, :], mixes[:, t, :]).then_inc(staged, 1)

                tiles(pool, stage)

            @block.tensor
            def _(pe):
                credit(pe, turned, projected)
                pe.wait_ge(ones_set, 1)

                def turn(t, u):
                    pe.wait_ge(staged, done(t))
                    pe.wait_ge(copied, reuse(t, 2))
                    if wide:
                        pe.wait_ge(copied_right, reuse(t, 2))
                    for k in range(chunks):
                        m = pe.transpose(ps_t[u][k // 4][:, (k % 4) * P:(k % 4 + 1) * P],
                                         rows[:, u, k * P:(k + 1) * P], ident[:, :])
                    m.then_inc(turned, 1)

                def project(t, u):
                    pe.wait_ge(copied, done(t))
                    if wide:
                        pe.wait_ge(copied_right, done(t))
                    pe.wait_ge(added, reuse(t, 2))
                    for k in range(chunks):
                        m = pe.matmul(ps_o[u], turned_rows[:, u, k * P:(k + 1) * P], w[:, k, :],
                                      start=(k == 0), stop=(k == chunks - 1 and bias_row is None))
                    if bias_row is not None:
                        m = pe.matmul(ps_o[u], ones_row[:, :], bias_row[:, :], start=False, stop=True)
                    m.then_inc(projected, 1)

                ahead(pe, turn, project)

            @block.scalar
            def _(act):
                credit(act, copied)

                def copy(t, u):
                    act.wait_ge(turned, done(t))
                    act.wait_ge(projected, reuse(t, 2))
                    act.copy(turned_rows[:, u, 0:half], ps_t[u][0]).then_inc(copied, 1)

                tiles(act, copy)

            @block.vector
            def _(dve):
                credit(dve, copied_right, added)

                def copy(t, u):
                    if wide:
                        dve.wait_ge(turned, done(t))
                        dve.wait_ge(projected, reuse(t, 2))
                        dve.tensor_copy(turned_rows[:, u, half:W], ps_t[u][1]).then_inc(copied_right, 1)

                def add(t, u):
                    dve.wait_ge(projected, done(t))
                    dve.tensor_tensor(x[:, t, :], ps_o[u], x[:, t, :], ALU.add).then_inc(added, 1)

                ahead(dve, copy, add)


def experts_prepare(nc, x, ident, eps, banks, xT_hi, xT_lo, comb_dram, ins):
    with ExitStack() as ctx:
        sb = lambda n, s: ctx.enter_context(nc.sbuf_tensor(n, s, F32))
        sem = phase_semaphores(nc, ctx, "experts_prepare_")
        norm = Norm(nc, ctx, "n2", x, ident, banks[0:2], eps)
        ps_l = banks[2:4]
        EA = E0 + 2
        w_r = sb("w_r", [P, DC, E0 + 1])
        logits = sb("logits", [P, NT, E0 + 1])
        top = sb("top", [P, NT, 8])
        rest = sb("rest", [P, NT, E0])
        shifted = sb("shifted", [P, NT, E0])
        chosen = sb("chosen", [P, NT, E0])
        total = sb("total", [P, NT, 1])
        comb = sb("comb", [P, NT, EA])
        combT = sb("combT", [EA, NT * P])
        w_loaded, hi_done = sem("w_loaded"), sem("hi_done")
        logit_out, max_done, rest_done, step_done = sem("logit_out"), sem("max_done"), sem("rest_done"), sem("step_done")
        exp_done, comb_done = sem("exp_done"), sem("comb_done")
        comb_turned, combT_done, stored = sem("comb_turned"), sem("combT_done"), sem("stored")

        with nc.Block() as block:
            @block.sync
            def _(sp):
                sp.dma_start(w_r[:, :, :], ins["w_router"].rearrange("(c p) k -> p c k", p=P)).then_inc(w_loaded, 16)
                sp.wait_ge(combT_done, NT // 4)
                sp.dma_start(comb_dram[:, :], combT[:, :]).then_inc(stored, 16)
                sp.wait_ge(stored, 16)

            @block.gpsimd
            def _(pool):
                credit(pool, norm.copied)

                def copy(t, u):
                    pool.wait_ge(norm.xnT_done, done(t))
                    pool.tensor_copy(xT_hi[:, :, bass.ts(t, P)], norm.xnT[:, u, :, :]).then_inc(hi_done, 1)
                    pool.wait_ge(hi_done, t + 1)
                    pool.tensor_tensor(xT_lo[:, :, bass.ts(t, P)], norm.xnT[:, u, :, :],
                                       xT_hi[:, :, bass.ts(t, P)].bitcast(F32), ALU.subtract).then_inc(norm.copied, 1)

                tiles(pool, copy)

            @block.scalar
            def _(act):
                credit(act, norm.xnT_done)
                norm.scalar_std(act)
                tiles(act, lambda t, u: norm.scalar_tile(act, t, u, copied=True))
                act.wait_ge(step_done, 2)
                act.activation(shifted[:, :, :], shifted[:, :, :], ACT.Exp).then_inc(exp_done, 1)
                act.activation(comb[:, :, E0:E0 + 1], logits[:, :, E0:E0 + 1], ACT.Sigmoid).then_inc(exp_done, 1)
                for g in range(NT // 4):
                    act.wait_ge(comb_turned, g + 1)
                    act.copy(combT[:, g * 512:(g + 1) * 512], banks[4 + g][0:EA, :]).then_inc(combT_done, 1)

            @block.vector
            def _(dve):
                credit(dve, norm.xn_done, logit_out)
                norm.vector_stats(dve)

                def logit(t, u):
                    dve.wait_ge(norm.used, done(t))
                    dve.tensor_copy(logits[:, t, :], ps_l[u][:, 0:E0 + 1]).then_inc(logit_out, 1)

                ahead(dve, lambda t, u: norm.vector_tile(dve, t, u), logit)
                dve.wait_ge(logit_out, done(NT - 1))
                dve.memset(comb[:, :, E0 + 1:EA], 0.0).then_inc(step_done, 1)
                for t in range(NT):
                    dve.max(top[:, t, :], logits[:, t, 0:E0]).then_inc(max_done, 1)
                dve.wait_ge(max_done, NT)
                dve.tensor_tensor(shifted[:, :, :], logits[:, :, 0:E0], top[:, :, 0:1].to_broadcast([P, NT, E0]),
                                  ALU.subtract).then_inc(step_done, 1)
                for t in range(NT):
                    dve.match_replace(rest[:, t, :], top[:, t, :], logits[:, t, 0:E0], -3.0e38).then_inc(rest_done, 1)
                dve.wait_ge(rest_done, NT)
                dve.tensor_tensor(chosen[:, :, :], rest[:, :, :], logits[:, :, 0:E0],
                                  ALU.not_equal).then_inc(step_done, 1)
                dve.wait_ge(step_done, 3)
                dve.wait_ge(exp_done, 1)
                dve.tensor_tensor(chosen[:, :, :], chosen[:, :, :], shifted[:, :, :], ALU.mult).then_inc(step_done, 1)
                dve.wait_ge(step_done, 4)
                dve.tensor_reduce(total[:, :, 0], chosen[:, :, :], AX.X, ALU.add).then_inc(step_done, 1)
                dve.wait_ge(step_done, 5)
                dve.reciprocal(total[:, :, :], total[:, :, :]).then_inc(step_done, 1)
                dve.wait_ge(step_done, 6)
                dve.tensor_tensor(comb[:, :, 0:E0], chosen[:, :, :], total[:, :, :].to_broadcast([P, NT, E0]),
                                  ALU.mult).then_inc(comb_done, 1)

            @block.tensor
            def _(pe):
                credit(pe, norm.turned, norm.used)
                pe.wait_ge(w_loaded, 16)

                def route(t, u):
                    pe.wait_ge(norm.xnT_done, done(t))
                    pe.wait_ge(logit_out, reuse(t, 2))
                    for c in range(DC):
                        m = pe.matmul(ps_l[u][:, 0:E0 + 1], norm.xnT[:, u, c, :], w_r[:, c, :],
                                      start=(c == 0), stop=(c == DC - 1))
                    m.then_inc(norm.used, 1)

                ahead(pe, lambda t, u: norm.tensor_turn(pe, t, u), route)
                pe.wait_ge(comb_done, 1)
                pe.wait_ge(exp_done, 2)
                for t in range(NT):
                    m = pe.transpose(banks[4 + t // 4][0:EA, (t % 4) * P:(t % 4 + 1) * P], comb[:, t, :], ident[:, :])
                    if t % 4 == 3:
                        m.then_inc(comb_turned, 1)


def experts(nc, x, psum, xT_hi, xT_lo, comb_dram, ins):
    with ExitStack() as ctx:
        sb = lambda n, s, d=F32: ctx.enter_context(nc.sbuf_tensor(n, s, d))
        sem = phase_semaphores(nc, ctx, "experts_")
        PR = 4
        TURNS = E0 // 2 // PR
        UNITS = PR * B
        GU = 2 * DC * P
        w_raw = sb("w_raw", [P, PR, GU + D])
        w_hi = sb("w_hi", [P, PR, GU + D], F32R)
        w_lo = sb("w_lo", [P, PR, GU + D], F32R)
        weight = sb("weight", [P, 4, S])
        gate = sb("gate", [P, 2, S])
        scaled = sb("scaled", [P, 2, S])
        hidden = sb("hidden", [P, 2, S])
        hidden_hi = sb("hidden_hi", [P, 4, S], F32R)
        hidden_lo = sb("hidden_lo", [P, 4, S], F32R)
        ps_g = [psum[:, u * 512:(u + 1) * 512] for u in range(2)]
        ps_u = [psum[:, (2 + u) * 512:(3 + u) * 512] for u in range(2)]
        ps_o = [psum[:, (4 + 2 * u) * 512:(6 + 2 * u) * 512] for u in range(2)]
        w_loaded = [sem(f"w_loaded{p}") for p in range(PR)]
        weight_loaded = [sem(f"weight_loaded{k}") for k in range(4)]
        w_hi_done, w_split = sem("w_hi_done"), sem("w_split")
        gu_done, silu_done, scaled_done, hidden_done = (
            sem(n) for n in ("gu_done", "silu_done", "scaled_done", "hidden_done"))
        hi_done, lo_done = sem("hi_done"), sem("lo_done")
        down_done, added = sem("down_done"), sem("added")

        def unit(g, k):
            return B + g * UNITS + k

        def split(g, p):
            return 1 + g * PR + p

        def loads(g, p):
            return 32 * g + (64 if p == PR - 1 else 32)

        def splits_in_turn(g, last, split_pair):
            def at(k):
                if k < 2:
                    split_pair(g, k + 2, unit(g, k) - 2)
                elif k >= UNITS - 2 and not last:
                    split_pair(g + 1, k - (UNITS - 2), unit(g, k) - 2)
            return at

        with nc.Block() as block:
            @block.sync
            def _(sp):
                def load_weights(p, pair):
                    sp.dma_start(w_raw[:, p, 0:GU].rearrange("p (g c m) -> p g c m", g=2, c=DC),
                                 ins["w_gu0"][pair].rearrange("g (c k) m -> k g c m", k=P)).then_inc(w_loaded[p], 16)
                    sp.dma_start(w_raw[:, p, GU:GU + D], ins["w_d0"][pair]).then_inc(w_loaded[p], 16)

                def load_weight(n, k, pair, b):
                    sp.wait_ge(scaled_done, reuse(n, 4))
                    for i in range(2):
                        sp.dma_start(weight[i * I0:(i + 1) * I0, k % 4, :],
                                     comb_dram[bass.ds(2 * pair + i, 1), b * S:(b + 1) * S].to_broadcast([I0, S])) \
                            .then_inc(weight_loaded[k % 4], 16)

                def turn(g, last):
                    for k in range(UNITS):
                        if 2 <= k < 2 + PR and not last:
                            sp.wait_ge(w_split, done(split(g, k - 2)))
                            load_weights(k - 2, (g + 1) * PR + k - 2)
                        if k + 4 < UNITS:
                            load_weight(unit(g, k) + 4, k + 4, g * PR + k % PR, (k + 4) // PR)
                        elif not last:
                            load_weight(unit(g, k) + 4, k + 4, (g + 1) * PR + k % PR, 0)

                load_weights(PR - 1, E0 // 2)
                for p in range(PR - 1):
                    load_weights(p, p)
                for b in range(B):
                    load_weight(b, b, E0 // 2, b)
                sp.wait_ge(w_split, done(0))
                load_weights(PR - 1, PR - 1)
                for p in range(PR):
                    load_weight(B + p, p, p, 0)
                with sp.Fori(0, TURNS - 1) as g:
                    turn(g, False)
                turn(TURNS - 1, True)

            @block.tensor
            def _(pe):
                credit(pe, gu_done, down_done)

                def gates_ups(n, p, b, u):
                    pe.wait_ge(silu_done, reuse(n, 2))
                    pe.wait_ge(hidden_done, reuse(n, 2))
                    parts = ((w_hi, xT_hi), (w_hi, xT_lo), (w_lo, xT_hi))
                    for i, to in ((0, ps_g[u]), (1, ps_u[u])):
                        for w, xs in parts:
                            for c in range(DC):
                                at = (i * DC + c) * P
                                m = pe.matmul(to, w[:, p, at:at + P], xs[:, c, b * S:(b + 1) * S],
                                              start=(w is w_hi and xs is xT_hi and c == 0),
                                              stop=(w is w_lo and c == DC - 1))
                    m.then_inc(gu_done, 1)

                def down(n, p, b, u, first, last, add):
                    pe.wait_ge(lo_done, done(n))
                    if first:
                        pe.wait_ge(added, reuse(add, 2))
                    for q in range(QT):
                        for j, (hs, w) in enumerate(((hidden_hi, w_hi), (hidden_hi, w_lo), (hidden_lo, w_hi))):
                            m = pe.matmul(ps_o[b % 2][:, q * D:(q + 1) * D], hs[:, u, q * P:(q + 1) * P],
                                          w[:, p, GU:GU + D], start=(first and q % 2 == 0 and j == 0),
                                          stop=(last and j == 2), skip_group_check=True)
                    m.then_inc(down_done, 1)

                pe.wait_ge(w_split, done(0))
                for b in range(B):
                    gates_ups(b, PR - 1, b, b % 2)
                    if b > 1:
                        down(b - 2, PR - 1, b - 2, b - 2, True, True, b - 2)
                for b in range(B - 2, B):
                    down(b, PR - 1, b, b, True, True, b)

                def turn(g, first):
                    for k in range(UNITS):
                        b, p = k // PR, k % PR
                        if b == 0:
                            pe.wait_ge(w_split, done(split(g, p)))
                        gates_ups(unit(g, k), p, b, k % 2)
                        if k >= 2:
                            down_k(g, k - 2)
                        elif not first:
                            down_k(g - 1, UNITS + k - 2)

                def down_k(g, k):
                    b, p = k // PR, k % PR
                    down(unit(g, k), p, b, k % 4, p == 0, p == PR - 1, B + g * B + b)

                turn(0, True)
                with pe.Fori(1, TURNS) as g:
                    turn(g, False)
                for k in range(UNITS - 2, UNITS):
                    down_k(TURNS - 1, k)

            @block.scalar
            def _(act):
                credit(act, silu_done, hi_done, w_hi_done)

                def silu(n, u):
                    act.wait_ge(gu_done, done(n))
                    act.wait_ge(scaled_done, reuse(n, 2))
                    act.activation(gate[:, u, :], ps_g[u], ACT.Silu).then_inc(silu_done, 1)

                def high(n, u, v):
                    act.wait_ge(hidden_done, done(n))
                    act.wait_ge(down_done, reuse(n, 4))
                    act.copy(hidden_hi[:, v, :], hidden[:, u, :]).then_inc(hi_done, 1)

                def split_pair(g, p, used):
                    act.wait_ge(w_loaded[p], loads(g, p))
                    act.wait_ge(down_done, done(used))
                    act.copy(w_hi[:, p, :], w_raw[:, p, :]).then_inc(w_hi_done, 1)

                act.wait_ge(w_loaded[PR - 1], 32)
                act.copy(w_hi[:, PR - 1, :], w_raw[:, PR - 1, :]).then_inc(w_hi_done, 1)
                for b in range(B):
                    silu(b, b % 2)
                    if b > 0:
                        high(b - 1, (b - 1) % 2, b - 1)
                    if b < 2:
                        act.wait_ge(w_loaded[b], 32)
                        act.copy(w_hi[:, b, :], w_raw[:, b, :]).then_inc(w_hi_done, 1)
                high(B - 1, (B - 1) % 2, B - 1)

                def turn(g, last):
                    split_at = splits_in_turn(g, last, split_pair)
                    for k in range(UNITS):
                        silu(unit(g, k), k % 2)
                        if k > 0:
                            high(unit(g, k) - 1, (k - 1) % 2, (k - 1) % 4)
                        split_at(k)
                    high(unit(g, UNITS - 1), 1, 3)

                with act.Fori(0, TURNS - 1) as g:
                    turn(g, False)
                turn(TURNS - 1, True)

            @block.gpsimd
            def _(pool):
                credit(pool, scaled_done, w_split)

                def scale(n, u, buffer, loads):
                    pool.wait_ge(silu_done, done(n))
                    pool.wait_ge(weight_loaded[buffer], 16 * loads)
                    pool.wait_ge(hidden_done, reuse(n, 2))
                    pool.tensor_tensor(scaled[:, u, :], gate[:, u, :], weight[:, buffer, :],
                                       ALU.mult).then_inc(scaled_done, 1)

                def low(n, p):
                    pool.wait_ge(w_hi_done, done(n))
                    pool.tensor_tensor(w_lo[:, p, :], w_raw[:, p, :], w_hi[:, p, :].bitcast(F32),
                                       ALU.subtract).then_inc(w_split, 1)

                low(0, PR - 1)
                for b in range(B):
                    scale(b, b % 2, b, 2)
                    if b < 2:
                        low(split(0, b), b)

                def turn(g, last):
                    split_at = splits_in_turn(g, last, lambda g, p, used: low(split(g, p), p))
                    for k in range(UNITS):
                        scale(unit(g, k), k % 2, k % 4, 2 * (g * (UNITS // 4) + k // 4 + 2))
                        split_at(k)

                with pool.Fori(0, TURNS - 1) as g:
                    turn(g, False)
                turn(TURNS - 1, True)

            @block.vector
            def _(dve):
                credit(dve, hidden_done, lo_done, added)

                def hide(n, u, v):
                    dve.wait_ge(scaled_done, done(n))
                    dve.wait_ge(lo_done, reuse(n, 2))
                    dve.tensor_tensor(hidden[:, u, :], ps_u[u], scaled[:, u, :], ALU.mult).then_inc(hidden_done, 1)

                def low(n, u, v):
                    dve.wait_ge(hi_done, done(n))
                    dve.tensor_tensor(hidden_lo[:, v, :], hidden[:, u, :], hidden_hi[:, v, :].bitcast(F32),
                                      ALU.subtract).then_inc(lo_done, 1)

                def add(n, b):
                    dve.wait_ge(down_done, done(n))
                    xb = x[:, b * QT:(b + 1) * QT, :].rearrange("p t d -> p (t d)")
                    dve.tensor_tensor(xb, ps_o[b % 2], xb, ALU.add).then_inc(added, 1)

                for b in range(B):
                    hide(b, b % 2, b)
                    if b > 0:
                        low(b - 1, (b - 1) % 2, b - 1)
                    if b > 2:
                        add(b - 3, b - 3)
                low(B - 1, 1, B - 1)
                for b in range(B - 3, B):
                    add(b, b)

                def turn(g, first):
                    for k in range(UNITS):
                        hide(unit(g, k), k % 2, k % 4)
                        if k > 0:
                            low(unit(g, k) - 1, (k - 1) % 2, (k - 1) % 4)
                        if k % PR == 2 and (k > 2 or not first):
                            add(unit(g, k) - 3, (k // PR - 1) % B)
                    low(unit(g, UNITS - 1), 1, 3)

                turn(0, True)
                with dve.Fori(1, TURNS) as g:
                    turn(g, False)
                add(unit(TURNS - 1, UNITS - 1), B - 1)


def alibi_prepare(nc, x, ident, eps, banks, xT, v_all, biases, w_out, ins):
    with ExitStack() as ctx:
        sb = lambda n, s, d=F32: ctx.enter_context(nc.sbuf_tensor(n, s, d))
        sem = phase_semaphores(nc, ctx, "alibi_prepare_")
        norm = Norm(nc, ctx, "n3", x, ident, banks[0:2], eps)
        ps_v = banks[2:4]
        w_v = sb("w_v", [P, DC, D])
        distance_int = sb("distance_int", [P, S], mybir.dt.int32)
        distance = sb("distance", [P, S])
        w_loaded, w_out_loaded, v_out, far = sem("w_loaded"), sem("w_out_loaded"), sem("v_out"), sem("far")

        with nc.Block() as block:
            @block.sync
            def _(sp):
                sp.dma_start(w_v[:, :, :], ins["w_v"].rearrange("(c p) k -> p c k", p=P)).then_inc(w_loaded, 16)
                sp.dma_start(w_out[:, :, :], ins["w_out1"].rearrange("(c p) k -> p c k", p=P)).then_inc(w_out_loaded, 16)
                sp.wait_ge(w_out_loaded, 16)

            @block.gpsimd
            def _(pool):
                credit(pool, norm.copied)
                pool.iota(distance_int[:, :], pattern=[[1, S]], base=-(QT - 1) * P, channel_multiplier=-1).then_inc(far, 1)
                pool.wait_ge(far, 1)
                pool.tensor_copy(distance[:, :], distance_int[:, :]).then_inc(far, 1)
                pool.wait_ge(far, 2)
                pool.affine_select(out=distance[:, :], in_=distance[:, :], compare_op=ALU.is_ge, fill=NEG,
                                   base=(QT - 1) * P, pattern=[[-1, S]], channel_multiplier=1).then_inc(far, 1)

                def copy(t, u):
                    pool.wait_ge(norm.xnT_done, done(t))
                    pool.tensor_copy(xT[:, :, bass.ts(t, P)], norm.xnT[:, u, :, :]).then_inc(norm.copied, 1)

                tiles(pool, copy)

            @block.scalar
            def _(act):
                credit(act, norm.xnT_done)
                norm.scalar_std(act)
                tiles(act, lambda t, u: norm.scalar_tile(act, t, u, copied=True))

            @block.vector
            def _(dve):
                credit(dve, norm.xn_done, v_out)
                norm.vector_stats(dve)

                def values(t, u):
                    dve.wait_ge(norm.used, done(t))
                    dve.tensor_copy(v_all[:, t, :], ps_v[u][:, 0:D]).then_inc(v_out, 1)

                ahead(dve, lambda t, u: norm.vector_tile(dve, t, u), values)
                dve.wait_ge(far, 3)
                slopes = np.float32(2.0) ** (np.float32(-8.0) / np.arange(1, H1 + 1, dtype=np.float32))
                for h in range(H1):
                    dve.tensor_scalar(biases[:, h, :], distance[:, :], float(slopes[h]), None, ALU.mult)

            @block.tensor
            def _(pe):
                credit(pe, norm.turned, norm.used)
                pe.wait_ge(w_loaded, 16)

                def values(t, u):
                    pe.wait_ge(norm.xnT_done, done(t))
                    pe.wait_ge(v_out, reuse(t, 2))
                    for c in range(DC):
                        m = pe.matmul(ps_v[u][:, 0:D], norm.xnT[:, u, c, :], w_v[:, c, :],
                                      start=(c == 0), stop=(c == DC - 1))
                    m.then_inc(norm.used, 1)

                ahead(pe, lambda t, u: norm.tensor_turn(pe, t, u), values)


def alibi_attention(nc, ident, banks, xT, v_all, biases, Y_all, ins):
    with ExitStack() as ctx:
        sb = lambda n, s, d=F32: ctx.enter_context(nc.sbuf_tensor(n, s, d))
        sem = phase_semaphores(nc, ctx, "alibi_")
        GU = QT * HG
        UNITS = NG * GU
        w_qk = sb("w_qk", [P, NG, 2, DC, P])
        lo_rows = sb("lo_rows", [P, 1])
        q_hi = sb("q_hi", [P, 2, S], F32R)
        q_lo = sb("q_lo", [P, 2, S], F32R)
        k_masked = sb("k_masked", [P, S], F32R)
        k_split = sb("k_split", [P, 2, S], F32R)
        v_now = sb("v_now", [P, NG, QT, HG, SLOT])
        neg_scores = sb("neg_scores", [P, 3, S])
        neg_max = sb("neg_max1", [P, UNITS])
        probs = sb("probs1", [P, 2, S])
        probsT = sb("probsT1", [P, 2, S])
        yT = sb("yT", [P, S])
        recip = sb("recip1", [P, GU, 1])
        carrier = sb("carrier", [1, UNITS])
        ps_s, ps_t, ps_yT, ps_q, ps_k = banks[0:3], banks[3:5], banks[5], banks[6], banks[7]
        mix = ps_q.rearrange("p (n k) -> p n k", n=GU)
        w_loaded, padded, v_staged = sem("w_loaded"), sem("padded"), sem("v_staged")
        q_made, k_made, q_hi_out, k_masked_out = sem("q_made"), sem("k_made"), sem("q_hi_out"), sem("k_masked_out")
        q_out, k_out = sem("q_out"), sem("k_out")
        scored, maxed, exped, turned = sem("scored"), sem("maxed"), sem("exped"), sem("turned")
        copied = [sem("copied_even"), sem("copied_odd")]
        mixed, yT_out, turned_back, recips, normed = (
            sem(n) for n in ("mixed", "yT_out", "turned_back", "recips", "normed"))
        scale = 1.0 / float(np.sqrt(HD1))

        def unit(b, k):
            return b * UNITS + k

        def pair(b, k):
            return b * (UNITS // 2) + k // 2

        def group(b, g):
            return b * NG + g

        def head(k):
            return k // GU * HG + k % HG

        def tile(k):
            return k % GU // HG

        def keys(k):
            return (tile(k) + 1) * P

        with nc.Block() as block:
            @block.sync
            def _(sp):
                sp.dma_start(w_qk[:, :, :, :, :], ins["w_qk"].rearrange("g a (c p) m -> p g a c m", p=P)).then_inc(w_loaded, 16)
                sp.dma_start(lo_rows[:, :], ins["lo_rows"]).then_inc(w_loaded, 16)

            @block.gpsimd
            def _(pool):
                credit(pool, v_staged)
                pool.memset(v_now[:, :, :, :, :], 1.0).then_inc(padded, 1)
                pool.wait_ge(padded, 1)
                with pool.Fori(0, B) as b:
                    for g in range(NG):
                        pool.wait_ge(turned_back, reuse(group(b, g), NG))
                        pool.tensor_copy(v_now[:, g, :, :, 0:HD1],
                                         v_all[:, bass.ts(b, QT), g * HG * HD1:(g + 1) * HG * HD1]
                                         .rearrange("p q (j d) -> p q j d", j=HG)).then_inc(v_staged, 1)

            @block.tensor
            def _(pe):
                credit(pe, q_made, k_made, scored, turned, mixed, turned_back)

                def queries(b, g):
                    pe.wait_ge(normed, reuse(group(b, g), 2) if g else reuse(group(b, g), 1))
                    for c in range(DC):
                        m = pe.matmul(ps_q, w_qk[:, g, 0, c, :], xT[:, c, bass.ts(b, S)],
                                      start=(c == 0), stop=(c == DC - 1))
                    m.then_inc(q_made, 1)

                def keys_of(b, g):
                    pe.wait_ge(k_out, reuse(group(b, g), 1))
                    for c in range(DC):
                        m = pe.matmul(ps_k, w_qk[:, g, 1, c, :], xT[:, c, bass.ts(b, S)],
                                      start=(c == 0), stop=(c == DC - 1))
                    m.then_inc(k_made, 1)

                def scores(b, k):
                    g = k // GU
                    if k % GU == 0:
                        pe.wait_ge(q_out, done(group(b, g)))
                        pe.wait_ge(k_out, done(group(b, g)))
                    if k >= 3:
                        pe.wait_ge(maxed, done(unit(b, k) - 3))
                    r, q = k % HG * SLOT, tile(k) * P
                    to = ps_s[k % 3][:, 0:keys(k)]
                    pe.matmul(to, q_hi[r:r + SLOT, g % 2, q:q + P], k_split[r:r + SLOT, g % 2, 0:keys(k)],
                              start=True, stop=False)
                    pe.matmul(to, q_lo[r:r + HD1, g % 2, q:q + P], k_split[r:r + HD1, g % 2, 0:keys(k)],
                              start=False, stop=True).then_inc(scored, 1)

                def turn_probs(b, k):
                    pe.wait_ge(exped, done(unit(b, k)))
                    pe.wait_ge(copied[k % 2], reuse(pair(b, k), 1))
                    for j in range(tile(k) + 1):
                        m = pe.transpose(ps_t[k % 2][:, j * P:(j + 1) * P], probs[:, k % 2, j * P:(j + 1) * P],
                                         ident[:, :])
                    m.then_inc(turned, 1)

                def mixes(b, k):
                    g, q, r = k // GU, tile(k), k % HG * SLOT
                    if k % GU == 0:
                        pe.wait_ge(v_staged, done(group(b, g)))
                        pe.wait_ge(yT_out, reuse(group(b, g), 1))
                    pe.wait_ge(copied[k % 2], done(pair(b, k)))
                    for j in range(q + 1):
                        m = pe.matmul(ps_yT[r:r + SLOT, q * P:(q + 1) * P], v_now[:, g, j, k % HG, :],
                                      probsT[:, k % 2, j * P:(j + 1) * P], start=(j == 0), stop=(j == q))
                    m.then_inc(mixed, 1)

                def turn_back(b, g):
                    pe.wait_ge(yT_out, done(group(b, g)))
                    for q in range(QT):
                        m = pe.transpose(ps_q[:, q * P:(q + 1) * P], yT[:, q * P:(q + 1) * P], ident[:, :])
                    m.then_inc(turned_back, 1)

                pe.wait_ge(w_loaded, 32)
                with pe.Fori(0, B) as b:
                    queries(b, 0)
                    keys_of(b, 0)
                    scores(b, 0)
                    scores(b, 1)
                    for k in range(UNITS):
                        g = k // GU
                        if k + 2 < UNITS:
                            scores(b, k + 2)
                        turn_probs(b, k)
                        if k > 0:
                            mixes(b, k - 1)
                        if k % GU == 3 and g > 0:
                            turn_back(b, g - 1)
                        if k % GU == 7 and g + 1 < NG:
                            queries(b, g + 1)
                        if k % GU == 9 and g + 1 < NG:
                            keys_of(b, g + 1)
                    mixes(b, UNITS - 1)
                    turn_back(b, NG - 1)

            @block.scalar
            def _(act):
                credit(act, q_hi_out, k_masked_out, exped, copied[1], yT_out)

                def queries_high(b, g):
                    act.wait_ge(q_made, done(group(b, g)))
                    act.mul(q_hi[:, g % 2, :], ps_q, scale).then_inc(q_hi_out, 1)

                def keys_masked(b, g):
                    act.wait_ge(k_made, done(group(b, g)))
                    act.wait_ge(k_out, reuse(group(b, g), 1))
                    act.mul(k_masked[:, :], ps_k, lo_rows[:, 0:1]).then_inc(k_masked_out, 1)

                def exps(b, k):
                    n = unit(b, k)
                    act.wait_ge(maxed, done(n))
                    act.wait_ge(turned, reuse(n, 2))
                    act.activation(probs[:, k % 2, 0:keys(k)], neg_scores[:, k % 3, 0:keys(k)], ACT.Exp,
                                   bias=neg_max[:, k:k + 1], scale=-1.0).then_inc(exped, 1)

                def copy(b, k):
                    n = unit(b, k)
                    act.wait_ge(turned, done(n))
                    act.wait_ge(mixed, reuse(n, 2))
                    act.copy(probsT[:, k % 2, 0:keys(k)], ps_t[k % 2][:, 0:keys(k)]).then_inc(copied[1], 1)

                def copy_mixes(b, g):
                    act.wait_ge(mixed, done(unit(b, g * GU + GU - 1)))
                    act.wait_ge(turned_back, reuse(group(b, g), 1))
                    act.copy(yT[:, :], ps_yT).then_inc(yT_out, 1)

                act.wait_ge(w_loaded, 32)
                with act.Fori(0, B) as b:
                    queries_high(b, 0)
                    keys_masked(b, 0)
                    exps(b, 0)
                    for k in range(UNITS):
                        g = k // GU
                        if k + 1 < UNITS:
                            exps(b, k + 1)
                        if k % GU == 1 and g > 0:
                            copy_mixes(b, g - 1)
                        if k % 2:
                            copy(b, k)
                        if k % GU == 8 and g + 1 < NG:
                            queries_high(b, g + 1)
                        if k % GU == 10 and g + 1 < NG:
                            keys_masked(b, g + 1)
                    copy_mixes(b, NG - 1)

            @block.vector
            def _(dve):
                credit(dve, q_out, k_out, maxed, copied[0], normed)

                def queries_low(b, g):
                    dve.wait_ge(q_hi_out, done(group(b, g)))
                    dve.scalar_tensor_tensor(q_lo[:, g % 2, :], ps_q, scale, q_hi[:, g % 2, :].bitcast(F32),
                                             ALU.mult, ALU.subtract).then_inc(q_out, 1)

                def keys_split(b, g):
                    dve.wait_ge(k_masked_out, done(group(b, g)))
                    dve.tensor_tensor(k_split[:, g % 2, :], ps_k, k_masked[:, :].bitcast(F32),
                                      ALU.subtract).then_inc(k_out, 1)

                def maxes(b, k):
                    n = unit(b, k)
                    dve.wait_ge(scored, done(n))
                    dve.wait_ge(exped, reuse(n, 3))
                    dve.memset(carrier[:, k:k + 1], 0.0)
                    at = (QT - 1 - tile(k)) * P
                    dve.tensor_tensor_reduce(neg_scores[:, k % 3, 0:keys(k)], ps_s[k % 3][:, 0:keys(k)],
                                             biases[:, head(k), at:at + keys(k)], -1.0, 3.0e38, ALU.add, ALU.min,
                                             neg_max[:, k:k + 1]).then_inc(maxed, 1)

                def copy(b, k):
                    n = unit(b, k)
                    dve.wait_ge(turned, done(n))
                    dve.wait_ge(mixed, reuse(n, 2))
                    dve.tensor_copy(probsT[:, k % 2, 0:keys(k)], ps_t[k % 2][:, 0:keys(k)]).then_inc(copied[0], 1)

                def norms(b, g):
                    m = group(b, g)
                    dve.wait_ge(turned_back, done(m))
                    dve.reciprocal(recip[:, :, :], mix[:, :, HD1:HD1 + 1]).then_inc(recips, 1)
                    dve.wait_ge(recips, m + 1)
                    out = Y_all[:, bass.ts(b, QT), g, :].rearrange("p q (j d) -> p q j d", j=HG)
                    dve.tensor_tensor(out, mix[:, :, 0:HD1].rearrange("p (q j) d -> p q j d", j=HG),
                                      recip[:, :, :].to_broadcast([P, GU, HD1])
                                      .rearrange("p (q j) d -> p q j d", j=HG), ALU.mult).then_inc(normed, 1)

                with dve.Fori(0, B) as b:
                    queries_low(b, 0)
                    keys_split(b, 0)
                    maxes(b, 0)
                    maxes(b, 1)
                    for k in range(UNITS):
                        g = k // GU
                        if k + 2 < UNITS:
                            maxes(b, k + 2)
                        if k % 2 == 0:
                            copy(b, k)
                        if k % GU == 5 and g > 0:
                            norms(b, g - 1)
                        if k % GU == 8 and g + 1 < NG:
                            queries_low(b, g + 1)
                        if k % GU == 10 and g + 1 < NG:
                            keys_split(b, g + 1)
                    norms(b, NG - 1)


def capacity_route(nc, x, ident, eps, banks, dispatched, slots, gates, ins):
    with ExitStack() as ctx:
        sb = lambda n, s, d=F32: ctx.enter_context(nc.sbuf_tensor(n, s, d))
        sem = phase_semaphores(nc, ctx, "capacity_route_")
        norm = Norm(nc, ctx, "n4", x, ident, banks[0:2], eps)
        ps_l, ps_before, ps_total = banks[2:4], banks[4], banks[5]
        w_g = sb("w_g", [P, DC, E1])
        xn_all = sb("xn_all", [P, NT, D])
        logits = sb("logits1", [P, NT, E1])
        top = sb("top1", [P, NT, 8])
        which = sb("which", [P, NT, 8], U32)
        which_f = sb("which_f", [P, NT, 2])
        expert_int = sb("expert_int", [P, E1], mybir.dt.int32)
        expert = sb("expert", [P, E1])
        onehot = sb("onehot", [P, 2, NT, E1])
        both = sb("both", [P, NT, E1])
        earlier = sb("earlier", [P, P])
        ones = sb("ones", [P, P])
        before = sb("before", [P, NT, E1])
        totals = sb("totals", [P, 2, NT, E1])
        placed = sb("placed", [P, 2, NT, E1])
        shifted = sb("shifted1", [P, NT, E1])
        total = sb("total1", [P, NT, 1])
        position = sb("position", [P, 2, NT])
        kept = sb("kept", [P, 2, NT])
        slot_f = sb("slot_f", [P, 2, NT])
        send = sb("send", [P, 2, NT], U32)
        w_loaded, logit_out, made = sem("w_loaded"), sem("logit_out"), sem("made")
        topped, step, counted, exped, sent = sem("topped"), sem("step"), sem("counted"), sem("exped"), sem("sent")

        with nc.Block() as block:
            @block.sync
            def _(sp):
                sp.dma_start(w_g[:, :, :], ins["w_g"].rearrange("(c p) k -> p c k", p=P)).then_inc(w_loaded, 16)

            @block.gpsimd
            def _(pool):
                credit(pool, norm.copied)
                pool.memset(ones[:, :], 1.0).then_inc(made, 1)
                pool.iota(expert_int[:, :], pattern=[[1, E1]], base=0, channel_multiplier=0).then_inc(made, 1)
                pool.wait_ge(made, 2)
                pool.tensor_copy(expert[:, :], expert_int[:, :]).then_inc(made, 1)
                pool.affine_select(out=earlier[:, :], in_=ones[:, :], compare_op=ALU.is_gt, fill=0.0, base=0,
                                   pattern=[[1, P]], channel_multiplier=-1).then_inc(made, 1)

                def copy(t, u):
                    pool.wait_ge(norm.xn_done, done(t))
                    pool.tensor_copy(xn_all[:, t, :], norm.xn[:, u, :]).then_inc(norm.copied, 1)

                tiles(pool, copy)
                pool.wait_ge(norm.copied, done(NT - 1))
                pool.wait_ge(step, 9)
                for t in range(NT):
                    for i in range(2):
                        pool.indirect_dma_start(dispatched[:, :], bass.IndirectOffsetOnAxis(ap=send[:, i, t:t + 1], axis=0),
                                                xn_all[:, t, :], None, bounds_check=E1 * CAP - 1,
                                                oob_is_err=False).then_inc(sent, 16)
                pool.wait_ge(sent, 16 * 2 * NT)

            @block.scalar
            def _(act):
                credit(act, norm.xnT_done)
                norm.scalar_std(act)
                tiles(act, lambda t, u: norm.scalar_tile(act, t, u))
                act.wait_ge(step, 1)
                act.activation(shifted[:, :, :], shifted[:, :, :], ACT.Exp).then_inc(exped, 1)

            @block.vector
            def _(dve):
                credit(dve, norm.xn_done, logit_out)
                norm.vector_stats(dve)

                def logit(t, u):
                    dve.wait_ge(norm.used, done(t))
                    dve.tensor_copy(logits[:, t, :], ps_l[u][:, 0:E1]).then_inc(logit_out, 1)

                ahead(dve, lambda t, u: norm.vector_tile(dve, t, u, copied=True), logit)
                dve.wait_ge(logit_out, done(NT - 1))
                for t in range(NT):
                    dve.max(top[:, t, :], logits[:, t, :]).then_inc(topped, 1)
                dve.wait_ge(topped, NT)
                dve.tensor_tensor(shifted[:, :, :], logits[:, :, :], top[:, :, 0:1].to_broadcast([P, NT, E1]),
                                  ALU.subtract).then_inc(step, 1)
                for t in range(NT):
                    dve.max_index(which[:, t, :], top[:, t, :], logits[:, t, :]).then_inc(topped, 1)
                dve.wait_ge(topped, 2 * NT)
                dve.tensor_copy(which_f[:, :, :], which[:, :, 0:2]).then_inc(step, 1)
                dve.wait_ge(step, 2)
                dve.wait_ge(made, 4)
                for i in range(2):
                    dve.tensor_tensor(onehot[:, i, :, :], which_f[:, :, i:i + 1].to_broadcast([P, NT, E1]),
                                      expert[:, :].unsqueeze(1).to_broadcast([P, NT, E1]), ALU.is_equal).then_inc(step, 1)
                dve.wait_ge(step, 4)
                dve.tensor_tensor(both[:, :, :], onehot[:, 0, :, :], onehot[:, 1, :, :], ALU.add).then_inc(step, 1)
                dve.wait_ge(counted, 1)
                dve.memset(totals[:, 0, 0, :], 0.0)
                dve.tensor_copy(totals[:, 0, 1:NT, :],
                                ps_total[:, 0:(NT - 1) * E1].rearrange("p (t e) -> p t e", e=E1)).then_inc(topped, 1)
                n, at, lag = 2 * NT + 1, 0, 1
                dve.wait_ge(topped, n)
                while lag < NT:
                    dve.tensor_copy(totals[:, 1 - at, 0:lag, :], totals[:, at, 0:lag, :])
                    dve.tensor_tensor(totals[:, 1 - at, lag:NT, :], totals[:, at, lag:NT, :],
                                      totals[:, at, 0:NT - lag, :], ALU.add).then_inc(topped, 1)
                    n, at, lag = n + 1, 1 - at, 2 * lag
                    dve.wait_ge(topped, n)
                dve.tensor_tensor(before[:, :, :], ps_before[:, 0:NT * E1].rearrange("p (t e) -> p t e", e=E1),
                                  totals[:, at, :, :], ALU.add).then_inc(step, 1)
                dve.wait_ge(step, 6)
                for i in range(2):
                    dve.tensor_tensor(placed[:, i, :, :], onehot[:, i, :, :], before[:, :, :], ALU.mult).then_inc(topped, 1)
                dve.wait_ge(topped, n + 2)
                dve.tensor_reduce(position[:, :, :], placed[:, :, :, :], AX.X, ALU.add).then_inc(step, 1)
                dve.wait_ge(step, 7)
                dve.tensor_scalar(kept[:, :, :], position[:, :, :], float(CAP), None, ALU.is_lt).then_inc(topped, 1)
                dve.scalar_tensor_tensor(out=slot_f[:, :, :], in0=which_f[:, :, :].rearrange("p t i -> p i t"),
                                         scalar=float(CAP), in1=position[:, :, :], op0=ALU.mult, op1=ALU.add) \
                    .then_inc(topped, 1)
                dve.wait_ge(topped, n + 4)
                dve.tensor_tensor(slot_f[:, :, :], slot_f[:, :, :], kept[:, :, :], ALU.mult).then_inc(topped, 1)
                dve.tensor_scalar(position[:, :, :], kept[:, :, :], -float(2 * E1 * CAP), float(2 * E1 * CAP),
                                  ALU.mult, ALU.add).then_inc(topped, 1)
                dve.wait_ge(topped, n + 6)
                dve.tensor_copy(slots[:, :, :], slot_f[:, :, :]).then_inc(step, 1)
                dve.tensor_tensor(send[:, :, :], slot_f[:, :, :], position[:, :, :], ALU.add).then_inc(step, 1)
                dve.wait_ge(exped, 1)
                dve.tensor_reduce(total[:, :, 0], shifted[:, :, :], AX.X, ALU.add).then_inc(topped, 1)
                dve.wait_ge(topped, n + 7)
                dve.reciprocal(total[:, :, :], total[:, :, :]).then_inc(topped, 1)
                for i in range(2):
                    dve.tensor_tensor(placed[:, i, :, :], onehot[:, i, :, :], shifted[:, :, :], ALU.mult).then_inc(topped, 1)
                dve.wait_ge(topped, n + 10)
                dve.tensor_reduce(gates[:, :, :], placed[:, :, :, :], AX.X, ALU.add).then_inc(topped, 1)
                dve.wait_ge(topped, n + 11)
                dve.tensor_tensor(gates[:, :, :], gates[:, :, :], kept[:, :, :], ALU.mult).then_inc(topped, 1)
                dve.wait_ge(topped, n + 12)
                dve.tensor_tensor(gates[:, :, :], gates[:, :, :],
                                  total[:, :, 0].unsqueeze(1).to_broadcast([P, 2, NT]), ALU.mult)

            @block.tensor
            def _(pe):
                credit(pe, norm.turned, norm.used)
                pe.wait_ge(w_loaded, 16)

                def route(t, u):
                    pe.wait_ge(norm.xnT_done, done(t))
                    pe.wait_ge(logit_out, reuse(t, 2))
                    for c in range(DC):
                        m = pe.matmul(ps_l[u][:, 0:E1], norm.xnT[:, u, c, :], w_g[:, c, :],
                                      start=(c == 0), stop=(c == DC - 1))
                    m.then_inc(norm.used, 1)

                ahead(pe, lambda t, u: norm.tensor_turn(pe, t, u), route)
                pe.wait_ge(step, 5)
                pe.wait_ge(made, 4)
                rows = both[:, :, :].rearrange("p t e -> p (t e)")
                pe.matmul(ps_before[:, 0:NT * E1], earlier[:, :], rows, start=True, stop=True)
                pe.matmul(ps_total[:, 0:NT * E1], ones[:, :], rows, start=True, stop=True).then_inc(counted, 1)


def capacity_experts(nc, ident, banks, dispatched, returned, ins):
    with ExitStack() as ctx:
        sb = lambda n, s: ctx.enter_context(nc.sbuf_tensor(n, s, F32))
        sem = phase_semaphores(nc, ctx, "capacity_")
        FC = F1 // P
        HALF = CAP // 2
        w1 = sb("w1", [P, 2, DC, F1])
        w2 = sb("w2", [P, 2, FC, D])
        rows = sb("rows1", [P, 2, CT, D])
        rowsT = sb("rowsT", [P, 2, DC, CAP])
        hidden = sb("hidden1", [P, FC, CAP])
        outs = sb("outs", [P, 2, CT, D])
        ps_t, ps_h, ps_o = banks[0:2], banks[2:6], banks[6:8]
        w1_loaded = [sem(f"w1_loaded{u}") for u in range(2)]
        w2_loaded = [sem(f"w2_loaded{u}") for u in range(2)]
        rows_loaded = [sem(f"rows_loaded{u}") for u in range(2)]
        stored, outs_free = sem("stored"), sem("outs_free")
        turned, rowsT_done, up_done = sem("turned"), sem("rowsT_done"), sem("up_done")
        relu_left, relu_right, down_done, out_done = sem("relu_left"), sem("relu_right"), sem("down_done"), sem("out_done")

        def turns(eng, turn):
            with eng.Fori(0, E1 // 2) as ee:
                for u in range(2):
                    turn(2 * ee + u, ee, u)

        with nc.Block() as block:
            @block.sync
            def _(sp):
                def load(e, ee, u):
                    sp.wait_ge(turned, reuse(e * CT + CT - 1, 2 * CT))
                    sp.dma_start(rows[:, u, :, :], dispatched[bass.ds(e * CAP, CAP), :]
                                 .rearrange("(t p) d -> p t d", p=P)).then_inc(rows_loaded[u], 16)
                    sp.wait_ge(up_done, reuse(e * FC + FC - 1, 2 * FC))
                    sp.dma_start(w1[:, u, :, :], ins["w1"][bass.ds(e, 1)].rearrange("a (c p) f -> p (a c) f", p=P)) \
                        .then_inc(w1_loaded[u], 16)
                    sp.wait_ge(down_done, reuse(e * CT + CT - 1, 2 * CT))
                    sp.dma_start(w2[:, u, :, :], ins["w2"][bass.ds(e, 1)].rearrange("a (c p) d -> p (a c) d", p=P)) \
                        .then_inc(w2_loaded[u], 16)

                turns(sp, load)

            @block.gpsimd
            def _(pool):
                credit(pool, outs_free)

                def store(e, ee, u):
                    pool.wait_ge(out_done, done(e * CT + CT - 1))
                    pool.dma_start(returned[bass.ds(e * CAP, CAP), :].rearrange("(t p) d -> p t d", p=P),
                                   outs[:, u, :, :]).then_inc(stored, 16)
                    pool.wait_ge(stored, 16 * (e + 1))
                    pool.sem_inc(outs_free, 1)

                turns(pool, store)

            @block.tensor
            def _(pe):
                credit(pe, turned, up_done, down_done)

                def turn_rows(e, ee, u):
                    pe.wait_ge(rows_loaded[u], 16 * (ee + 1))
                    for t in range(CT):
                        n = e * CT + t
                        pe.wait_ge(rowsT_done, reuse(n, 2))
                        for c in range(DC):
                            m = pe.transpose(ps_t[t % 2][:, c * P:(c + 1) * P], rows[:, u, t, c * P:(c + 1) * P],
                                             ident[:, :])
                        m.then_inc(turned, 1)

                def up(e, ee, u):
                    pe.wait_ge(w1_loaded[u], 16 * (ee + 1))
                    pe.wait_ge(rowsT_done, done(e * CT + CT - 1))
                    for f in range(FC):
                        n = e * FC + f
                        pe.wait_ge(relu_left, reuse(n, 2))
                        pe.wait_ge(relu_right, reuse(n, 2))
                        for i in range(2):
                            for c in range(DC):
                                m = pe.matmul(ps_h[2 * (f % 2) + i][:, 0:HALF], w1[:, u, c, f * P:(f + 1) * P],
                                              rowsT[:, u, c, i * HALF:(i + 1) * HALF],
                                              start=(c == 0), stop=(c == DC - 1))
                        m.then_inc(up_done, 1)

                def down(e, ee, u):
                    pe.wait_ge(w2_loaded[u], 16 * (ee + 1))
                    pe.wait_ge(relu_left, done(e * FC + FC - 1))
                    pe.wait_ge(relu_right, done(e * FC + FC - 1))
                    for t in range(CT):
                        n = e * CT + t
                        pe.wait_ge(out_done, reuse(n, 2))
                        for f in range(FC):
                            m = pe.matmul(ps_o[t % 2][:, 0:D], hidden[:, f, t * P:(t + 1) * P], w2[:, u, f, :],
                                          start=(f == 0), stop=(f == FC - 1))
                        m.then_inc(down_done, 1)

                def turn(e, ee, u):
                    turn_rows(e, ee, u)
                    up(e, ee, u)
                    down(e, ee, u)

                turns(pe, turn)

            @block.scalar
            def _(act):
                credit(act, relu_left)

                def turn(e, ee, u):
                    for f in range(FC):
                        act.wait_ge(up_done, done(e * FC + f))
                        if f == 0:
                            act.wait_ge(down_done, reuse(e * CT, 1))
                        act.activation(hidden[:, f, 0:HALF], ps_h[2 * (f % 2)][:, 0:HALF], ACT.Relu).then_inc(relu_left, 1)

                turns(act, turn)

            @block.vector
            def _(dve):
                credit(dve, rowsT_done, relu_right, out_done)

                def turn(e, ee, u):
                    for t in range(CT):
                        n = e * CT + t
                        dve.wait_ge(turned, done(n))
                        if t == 0:
                            dve.wait_ge(up_done, reuse(e * FC, 1))
                        dve.tensor_copy(rowsT[:, u, :, t * P:(t + 1) * P],
                                        ps_t[t % 2][:, 0:D].rearrange("p (c k) -> p c k", c=DC)).then_inc(rowsT_done, 1)
                    for f in range(FC):
                        dve.wait_ge(up_done, done(e * FC + f))
                        if f == 0:
                            dve.wait_ge(down_done, reuse(e * CT, 1))
                        dve.tensor_scalar(hidden[:, f, HALF:CAP], ps_h[2 * (f % 2) + 1][:, 0:HALF], 0.0, None,
                                          ALU.max).then_inc(relu_right, 1)
                    for t in range(CT):
                        n = e * CT + t
                        dve.wait_ge(down_done, done(n))
                        if t == 0:
                            dve.wait_ge(outs_free, reuse(e, 2))
                        dve.tensor_copy(outs[:, u, t, :], ps_o[t % 2][:, 0:D]).then_inc(out_done, 1)

                turns(dve, turn)


def combine(nc, x, returned, slots, gates, out):
    with ExitStack() as ctx:
        sem = phase_semaphores(nc, ctx, "combine_")
        first = ctx.enter_context(nc.sbuf_tensor("first", [P, NT, D], F32))
        second = ctx.enter_context(nc.sbuf_tensor("second", [P, NT, D], F32))
        RING = 8
        fetched = [[sem(f"fetched{i}_{t}") for t in range(RING)] for i in range(2)]
        half, summed, stored = sem("half"), sem("summed"), sem("stored")

        with nc.Block() as block:
            @block.gpsimd
            def _(pool):
                for t in range(NT):
                    if t >= RING:
                        pool.wait_ge(summed, t - RING + 1)
                    for i, rows in ((0, first), (1, second)):
                        pool.indirect_dma_start(rows[:, t, :], None, returned[:, :],
                                                bass.IndirectOffsetOnAxis(ap=slots[:, i, t:t + 1], axis=0),
                                                bounds_check=E1 * CAP - 1, oob_is_err=False) \
                            .then_inc(fetched[i][t % RING], 16)

            @block.vector
            def _(dve):
                for t in range(NT):
                    dve.wait_ge(fetched[0][t % RING], 16 * (t // RING + 1))
                    dve.scalar_tensor_tensor(out=x[:, t, :], in0=first[:, t, :], scalar=gates[:, 0, t:t + 1],
                                             in1=x[:, t, :], op0=ALU.mult, op1=ALU.add).then_inc(half, 1)
                    dve.wait_ge(half, t + 1)
                    dve.wait_ge(fetched[1][t % RING], 16 * (t // RING + 1))
                    dve.scalar_tensor_tensor(out=x[:, t, :], in0=second[:, t, :], scalar=gates[:, 1, t:t + 1],
                                             in1=x[:, t, :], op0=ALU.mult, op1=ALU.add).then_inc(summed, 1)

            @block.sync
            def _(sp):
                outv = out.rearrange("b (t p) d -> p (b t) d", p=P)
                for g in range(NT // 2):
                    sp.wait_ge(summed, 2 * g + 2)
                    sp.dma_start(outv[:, 2 * g:2 * g + 2, :], x[:, 2 * g:2 * g + 2, :]).then_inc(stored, 16)
                sp.wait_ge(stored, 16 * (NT // 2))


def two_layers(nc, ins, out):
    with ExitStack() as ctx:
        sb = lambda n, s, d=F32: ctx.enter_context(nc.sbuf_tensor(n, s, d))
        x = sb("x", [P, NT, D])
        ident = sb("ident", [P, P])
        eps = sb("eps", [P, 1])
        psum = ctx.enter_context(nc.psum_tensor("psum", [P, 8 * 512], F32))
        banks = [psum[:, k * 512:(k + 1) * 512] for k in range(8)]
        comb_dram = nc.dram_tensor("comb_dram", [E0 + 2, NT * P], F32, kind="Internal").ap()
        dispatched = nc.dram_tensor("dispatched_dram", [E1 * CAP, D], F32, kind="Internal").ap()
        returned = nc.dram_tensor("returned_dram", [E1 * CAP, D], F32, kind="Internal").ap()

        with ExitStack() as latent:
            sl = lambda n, s: latent.enter_context(nc.sbuf_tensor(n, s, F32))
            U_all = sl("U_all", [P, NT, H0, KV])
            N_all = sl("N_all", [P, H0 // 2, D])
            bias_out = sl("bias_out", [1, D])
            c_aug = sl("c_aug", [P, NT, KA])
            cT = sl("cT", [KA, B * S])
            cqT = sl("cqT", [P, 2, B * S])
            A_all = sl("A_all", [P, H0, 2, KA])
            latent_prepare(nc, x, ident, eps, banks, c_aug, cT, cqT, A_all, N_all, bias_out, ins)
            latent_attention(nc, ident, banks, c_aug, cT, cqT, A_all, U_all, dispatched)
            project_out(nc, "out0", x, ident, psum, U_all[:, :, :, :].rearrange("p t h k -> p t (h k)"),
                        H0 * KV // P, N_all, bias_out)

        with ExitStack() as mixture:
            xT_hi, xT_lo = (mixture.enter_context(nc.sbuf_tensor(n, [P, DC, B * S], F32R)) for n in ("xT_hi", "xT_lo"))
            experts_prepare(nc, x, ident, eps, banks, xT_hi, xT_lo, comb_dram, ins)
            experts(nc, x, psum, xT_hi, xT_lo, comb_dram, ins)

        with ExitStack() as alibi:
            sl = lambda n, s: alibi.enter_context(nc.sbuf_tensor(n, s, F32))
            xT = sl("xT1", [P, DC, B * S])
            v_all = sl("v_all", [P, NT, D])
            biases = sl("biases", [P, H1, S])
            Y_all = sl("Y_all", [P, NT, NG, HG * HD1])
            w_out1 = sl("w_out1", [P, DC, D])
            alibi_prepare(nc, x, ident, eps, banks, xT, v_all, biases, w_out1, ins)
            alibi_attention(nc, ident, banks, xT, v_all, biases, Y_all, ins)
            project_out(nc, "out1", x, ident, psum, Y_all[:, :, :, :].rearrange("p t g k -> p t (g k)"), DC, w_out1)

        slots = sb("slots", [P, 2, NT], U32)
        gates = sb("gates", [P, 2, NT])
        capacity_route(nc, x, ident, eps, banks, dispatched, slots, gates, ins)
        capacity_experts(nc, ident, banks, dispatched, returned, ins)
        combine(nc, x, returned, slots, gates, out)


def layout(**w):
    a = {n: np.asarray(v) for n, v in w.items()}
    at, f0 = "L0_attn_", "L0_ffn_"
    out = {"hidden": a[at + "hidden_states"]}
    out["w_dkv"], out["w_dq"] = a[at + "W_DKV_w"].T, a[at + "W_DQ_w"].T
    out["b_dkv"], out["b_dq"], out["b_o"] = a[at + "W_DKV_b"], a[at + "W_DQ_b"], a[at + "W_O_b"]
    for k in ("UQ", "UK", "UV"):
        out["w_" + k.lower()] = np.concatenate([a[f"{at}W_{k}_w"], a[f"{at}W_{k}_b"][:, None]], 1)
    out["w_o"] = a[at + "W_O_w"].T
    out["w_router"] = np.concatenate([a[f0 + "router_w"], a[f0 + "shared_expert_gate_w"]], 0).T
    gate_up = a[f0 + "gate_up_proj"].reshape(E0, 2, I0, D)
    shared = np.stack([a[f0 + "shared_gate_w"], a[f0 + "shared_up_w"]])[None]
    gate_up = np.concatenate([gate_up, shared, np.zeros_like(shared)], 0)
    out["w_gu0"] = gate_up.reshape(E0 // 2 + 1, 2, 2, I0, D).transpose(0, 2, 4, 1, 3).reshape(E0 // 2 + 1, 2, D, P)
    down = np.concatenate([a[f0 + "down_proj"], a[f0 + "shared_down_w"][None],
                           np.zeros_like(a[f0 + "shared_down_w"][None])], 0)
    out["w_d0"] = down.transpose(0, 2, 1).reshape(E0 // 2 + 1, P, D)
    qkv = a["L1_attn_W_qkv"]
    qk = qkv[:, 0:2 * D].reshape(D, 2, NG, HG, HD1).transpose(2, 1, 0, 3, 4)
    out["w_qk"] = np.concatenate([qk, qk], -1).reshape(NG, 2, D, P)
    out["lo_rows"] = (np.arange(P) % SLOT >= HD1).astype(np.float32)[:, None]
    out["w_v"], out["w_out1"] = qkv[:, 2 * D:], a["L1_attn_W_o"]
    out["w_g"], out["w1"], out["w2"] = a["L1_ffn_Wg"], a["L1_ffn_w1"], a["L1_ffn_w2"]
    return {n: np.ascontiguousarray(v) for n, v in out.items()}


def kernel(**inputs):
    import concourse.bacc as bacc
    from concourse.bass_utils import run_bass_kernel_spmd

    nc = bacc.Bacc("TRN2", target_bir_lowering=False, num_devices=1)
    arrays = layout(**inputs)
    ins = {n: nc.dram_tensor("in_" + n, a.shape, mybir.dt.from_np(a.dtype), kind="ExternalInput").ap()
           for n, a in arrays.items()}
    out = nc.dram_tensor("out", (B, S, D), F32, kind="ExternalOutput").ap()
    two_layers(nc, ins, out)
    r = run_bass_kernel_spmd(nc, [{"in_" + n: a for n, a in arrays.items()}], core_ids=[0])
    return r.results[0]["out"]
```

```python
from contextlib import ExitStack

import numpy as np

import concourse.bass as bass
import concourse.mybir as mybir
from concourse.alu_op_type import AluOpType as ALU

F32 = mybir.dt.float32
F32R = mybir.dt.float32r
U32 = mybir.dt.uint32
ACT = mybir.ActivationFunctionType
AX = mybir.AxisListType

P = 128
B, S, D = 4, 512, 256
NT = B * S // P
QT = S // P
DC = D // P
EPS = 1e-5

H0, HD0, KV, QC = 16, 128, 64, 192
KA = KV + 1
SPLIT = 97

E0, I0 = 64, 64
TOP0 = 8

H1, HD1 = 16, 16
HG = 4
NG = H1 // HG
SLOT = 32

E1, F1 = 8, 1024
CAP = 640
CT = CAP // P
NEG = -1.0e30

CREDIT = 16
RING = 4


def done(n):
    return n + 1 + CREDIT


def reuse(n, depth):
    return n - depth + 1 + CREDIT


def credit(eng, *sems):
    for s in sems:
        eng.sem_inc(s, CREDIT)


def phase_semaphores(nc, ctx, prefix=""):
    taken = []

    def give_back():
        nc.clear_and_free_semaphores(taken)
        nc.all_engine_barrier()

    ctx.callback(give_back)

    def sem(name):
        taken.append(nc.alloc_semaphore(prefix + name))
        return taken[-1]

    return sem


def identity_matrix(pool, ident, made):
    pool.memset(ident[:, :], 0.0).then_inc(made, 1)
    pool.wait_ge(made, 1)
    pool.affine_select(out=ident[:, :], in_=ident[:, :], compare_op=ALU.not_equal, fill=1.0, base=0,
                       pattern=[[-1, P]], channel_multiplier=1).then_inc(made, 1)


class Norm:

    def __init__(self, nc, ctx, name, x, ident, ps_t, eps):
        sb = lambda n, s: ctx.enter_context(nc.sbuf_tensor(f"{name}_{n}", s, F32))
        sem = phase_semaphores(nc, ctx, name + "_")
        self.x, self.ident, self.ps_t, self.eps = x, ident, ps_t, eps
        self.stats = sb("stats", [P, NT, 6])
        self.meanvar = sb("meanvar", [P, NT, 2])
        self.std = sb("std", [P, NT])
        self.rstd = sb("rstd", [P, NT])
        self.xn = sb("xn", [P, RING, D])
        self.xnT = sb("xnT", [P, RING, DC, P])
        self.x_ready = sem("x_ready")
        self.stats_done = sem("stats_done")
        self.meanvar_done = sem("meanvar_done")
        self.std_done = sem("std_done")
        self.rstd_done = sem("rstd_done")
        self.xn_done = sem("xn_done")
        self.turned = sem("turned")
        self.xnT_done = sem("xnT_done")
        self.used = sem("used")
        self.copied = sem("copied")

    def vector_stats(self, dve):
        for t in range(NT):
            dve.bn_stats(self.stats[:, t, :], self.x[:, t, :]).then_inc(self.stats_done, 1)
        for t in range(NT):
            dve.wait_ge(self.stats_done, t + 1)
            dve.bn_aggr(self.meanvar[:, t, :], self.stats[:, t, :]).then_inc(self.meanvar_done, 1)
        dve.wait_ge(self.std_done, 1)
        dve.reciprocal(self.rstd[:, :], self.std[:, :]).then_inc(self.rstd_done, 1)
        dve.wait_ge(self.rstd_done, 1)

    def scalar_std(self, act):
        act.wait_ge(self.meanvar_done, NT)
        act.activation(self.std[:, :], self.meanvar[:, :, 1], ACT.Sqrt,
                       bias=self.eps[:, 0:1]).then_inc(self.std_done, 1)

    def vector_tile(self, dve, t, u, copied=False):
        dve.wait_ge(self.turned, reuse(t, RING))
        if copied:
            dve.wait_ge(self.copied, reuse(t, RING))
        dve.tensor_scalar(self.xn[:, u, :], self.x[:, t, :], self.meanvar[:, t, 0:1],
                          self.rstd[:, bass.ts(t, 1)], ALU.subtract, ALU.mult).then_inc(self.xn_done, 1)

    def tensor_turn(self, pe, t, u):
        pe.wait_ge(self.xn_done, done(t))
        pe.wait_ge(self.xnT_done, reuse(t, 2))
        for c in range(DC):
            m = pe.transpose(self.ps_t[u % 2][:, c * P:(c + 1) * P], self.xn[:, u, c * P:(c + 1) * P],
                             self.ident[:, :])
        m.then_inc(self.turned, 1)

    def scalar_tile(self, act, t, u, copied=False):
        act.wait_ge(self.turned, done(t))
        if copied:
            act.wait_ge(self.copied, reuse(t, RING))
        act.wait_ge(self.used, reuse(t, RING))
        act.copy(self.xnT[:, u, :, :], self.ps_t[u % 2][:, 0:D].rearrange("p (c k) -> p c k", c=DC)) \
            .then_inc(self.xnT_done, 1)


def tiles(eng, step, ring=2):
    with eng.Fori(0, NT // ring) as tt:
        for u in range(ring):
            step(ring * tt + u, u)


def ahead(eng, first, second, ring=2, lead=1):
    for t in range(lead):
        first(t, t)
    with eng.Fori(0, NT // ring - 1) as tt:
        for u in range(ring):
            first(ring * tt + u + lead, (u + lead) % ring)
            second(ring * tt + u, u)
    for u in range(ring):
        if u + lead < ring:
            first(NT - ring + u + lead, u + lead)
        second(NT - ring + u, u)


def latent_prepare(nc, x, ident, eps, banks, c_rows, c_first, c_second, cqT, A_all, N_all, bias_out, ins):
    with ExitStack() as ctx:
        sb = lambda n, s: ctx.enter_context(nc.sbuf_tensor(n, s, F32))
        sem = phase_semaphores(nc, ctx, "latent_prepare_")
        w_dkv = sb("w_dkv", [P, DC, KV])
        w_dq = sb("w_dq", [P, DC, QC])
        b_dkv_row = sb("b_dkv_row", [1, KV])
        b_dkv_col = sb("b_dkv_col", [KV, 1])
        b_dq = sb("b_dq", [P, 2])
        w_uq = sb("w_uq", [P, H0, QC + 1])
        w_uk = sb("w_uk", [P, H0, KA])
        w_uv = sb("w_uv", [P, H0, KA])
        w_o = sb("w_o", [P, H0, D])
        b_o = sb("b_o", [1, D])
        ones_row = sb("ones_row", [1, P])
        norm = Norm(nc, ctx, "n1", x, ident, banks[0:2], eps)
        ps_cq, ps_a, ps_c = banks[2:4], banks[4:6], banks[6:8]
        x_loaded, small_loaded, uqk_loaded, uvo_loaded = (
            sem(n) for n in ("x_loaded", "small_loaded", "uqk_loaded", "uvo_loaded"))
        made, consts = sem("made"), sem("consts")
        a_mm, a_out, n_mm, n_out = (sem(n) for n in ("a_mm", "a_out", "n_mm", "n_out"))
        zeroed, c_hi_done, c_out, cq_out = sem("zeroed"), sem("c_hi_done"), sem("c_out"), sem("cq_out")

        with nc.Block() as block:
            @block.sync
            def _(sp):
                xv = ins["hidden"].rearrange("b (t p) d -> p (b t) d", p=P)
                for g in range(4):
                    sp.dma_start(x[:, 4 * g:4 * g + 4, :], xv[:, 4 * g:4 * g + 4, :]).then_inc(x_loaded, 16)
                sp.dma_start(w_uq[:, :, :], ins["w_uq"].rearrange("(h p) k -> p h k", p=P)).then_inc(uqk_loaded, 16)
                sp.dma_start(w_uk[:, :, :], ins["w_uk"].rearrange("(h p) k -> p h k", p=P)).then_inc(uqk_loaded, 16)

            @block.scalar
            def _(act):
                small = [(w_dkv[:, :, :], ins["w_dkv"].rearrange("(c p) k -> p c k", p=P)),
                         (w_dq[:, :, :], ins["w_dq"].rearrange("(c p) k -> p c k", p=P)),
                         (b_dkv_row[:, :], ins["b_dkv"].rearrange("(a k) -> a k", a=1)),
                         (b_dkv_col[:, :], ins["b_dkv"].rearrange("(k a) -> k a", a=1)),
                         (b_dq[:, 0:1], ins["b_dq"][0:P].rearrange("(k a) -> k a", a=1)),
                         (b_dq[0:QC - P, 1:2], ins["b_dq"][P:QC].rearrange("(k a) -> k a", a=1)),
                         (b_o[:, :], ins["b_o"].rearrange("(a k) -> a k", a=1))]
                for to, of in small:
                    act.dma_start(to, of).then_inc(small_loaded, 16)
                act.dma_start(w_uv[:, :, :], ins["w_uv"].rearrange("(h p) k -> p h k", p=P)).then_inc(uvo_loaded, 16)
                act.dma_start(w_o[:, :, :], ins["w_o"].rearrange("(h p) k -> p h k", p=P)).then_inc(uvo_loaded, 16)
                credit(act, norm.xnT_done, cq_out)
                act.wait_ge(consts, 2)
                norm.scalar_std(act)
                scale = float(1.0 / np.sqrt(np.float32(HD0)))
                act.wait_ge(consts, 3)
                for j in range(H0 // 2):
                    act.wait_ge(a_mm, j + 1)
                    v = ps_a[j % 2][:, 0:4 * KA].rearrange("p (h c k) -> p h c k", h=2, c=2)
                    act.mul(A_all[:, 2 * j:2 * j + 2, 0, :], v[:, :, 0, :], scale).then_inc(a_out, 1)
                    act.mul(A_all[0:KA, 2 * j:2 * j + 2, 1, :], v[0:KA, :, 1, :], scale).then_inc(a_out, 1)
                act.wait_ge(small_loaded, 16 * 7)

                def step(t, u):
                    norm.scalar_tile(act, t, u)

                def latents(t, u):
                    act.wait_ge(norm.used, done(t))
                    m = ps_cq[u % 2]
                    act.activation(cqT[:, 0, bass.ts(t, P)], m[:, 0:P], ACT.Identity, bias=b_dq[:, 0:1])
                    act.activation(cqT[0:QC - P, 1, bass.ts(t, P)], m[0:QC - P, P:2 * P], ACT.Identity,
                                   bias=b_dq[0:QC - P, 1:2]).then_inc(cq_out, 1)

                ahead(act, step, latents, RING, 2)

            @block.gpsimd
            def _(pool):
                pool.memset(ones_row[:, :], 1.0).then_inc(consts, 1)
                pool.memset(eps[:, :], EPS).then_inc(consts, 1)
                pool.memset(A_all[:, :, :, :], 0.0).then_inc(consts, 1)
                identity_matrix(pool, ident, made)

            @block.vector
            def _(dve):
                credit(dve, norm.xn_done, c_out)
                dve.memset(c_first[KV:SPLIT, :].bitcast(F32), 0.0).then_inc(zeroed, 1)
                dve.wait_ge(zeroed, 1)
                dve.memset(c_first[KV:KA, :].bitcast(F32), 1.0)
                dve.memset(c_first[SPLIT - 1:SPLIT, :].bitcast(F32), 1.0)
                dve.memset(cqT[QC - P:QC - P + 1, 1, :], 1.0)
                dve.wait_ge(x_loaded, 64)
                norm.vector_stats(dve)
                for j in range(H0 // 2):
                    dve.wait_ge(n_mm, j + 1)
                    dve.tensor_copy(N_all[:, j, :], ps_a[j % 2][:, 0:D]).then_inc(n_out, 1)
                dve.wait_ge(n_mm, H0 // 2 + 1)
                dve.tensor_copy(bias_out[:, :], ps_a[0][0:1, 0:D]).then_inc(n_out, 1)

                def latents(t, u):
                    dve.wait_ge(norm.used, done(t))
                    m = ps_c[u % 2]
                    dve.tensor_scalar(c_first[0:KV, bass.ts(t, P)], m[0:KV, KV:KV + P], b_dkv_col[:, 0:1],
                                      None, ALU.add).then_inc(c_hi_done, 1)
                    dve.tensor_copy(c_rows[:, t, :], m[:, 0:KV])
                    dve.wait_ge(c_hi_done, t + 1)
                    dve.tensor_copy(c_second[0:KV, bass.ts(t, P)], c_first[0:KV, bass.ts(t, P)].bitcast(F32))
                    dve.scalar_tensor_tensor(c_second[KV:2 * KV, bass.ts(t, P)], m[0:KV, KV:KV + P],
                                             b_dkv_col[:, 0:1], c_first[0:KV, bass.ts(t, P)].bitcast(F32),
                                             ALU.add, ALU.subtract).then_inc(c_out, 1)

                ahead(dve, lambda t, u: norm.vector_tile(dve, t, u), latents, RING, 2)

            @block.tensor
            def _(pe):
                credit(pe, norm.turned, norm.used)
                pe.wait_ge(uqk_loaded, 32)
                for j in range(H0 // 2):
                    if j >= 2:
                        pe.wait_ge(a_out, 2 * (j - 1))
                    v = ps_a[j % 2][:, 0:4 * KA].rearrange("p (h c k) -> p h c k", h=2, c=2)
                    for i in range(2):
                        h = 2 * j + i
                        pe.matmul(v[:, i, 0, :], w_uq[:, h, 0:P], w_uk[:, h, :], start=True, stop=True)
                        m = pe.matmul(v[0:KA, i, 1, :], w_uq[:, h, P:QC + 1], w_uk[:, h, :],
                                      start=True, stop=True)
                    m.then_inc(a_mm, 1)
                pe.wait_ge(uvo_loaded, 32)
                pe.wait_ge(a_out, H0)
                for j in range(H0 // 2):
                    if j >= 2:
                        pe.wait_ge(n_out, j - 1)
                    for i in range(2):
                        h = 2 * j + i
                        m = pe.matmul(ps_a[j % 2][i * KV:(i + 1) * KV, 0:D], w_uv[:, h, 0:KV], w_o[:, h, :],
                                      start=True, stop=True)
                    m.then_inc(n_mm, 1)
                pe.wait_ge(n_out, H0 // 2)
                pe.wait_ge(small_loaded, 16 * 7)
                pe.wait_ge(consts, 1)
                for h in range(H0):
                    pe.matmul(ps_a[0][0:1, 0:D], w_uv[:, h, KV:KA], w_o[:, h, :], start=(h == 0), stop=False)
                pe.matmul(ps_a[0][0:1, 0:D], ones_row[:, 0:1], b_o[:, :], start=False, stop=True).then_inc(n_mm, 1)
                pe.wait_ge(made, 2)

                def latents(t, u):
                    pe.wait_ge(norm.xnT_done, done(t))
                    pe.wait_ge(c_out, reuse(t, 2))
                    pe.wait_ge(cq_out, reuse(t, 2))
                    m, mq = ps_c[u % 2], ps_cq[u % 2]
                    xs = norm.xnT
                    for c in range(DC):
                        pe.matmul(m[:, 0:KV], xs[:, u, c, :], w_dkv[:, c, :], start=(c == 0), stop=False)
                    pe.matmul(m[:, 0:KV], ones_row[:, :], b_dkv_row[:, :], start=False, stop=True)
                    for to, w in ((m[0:KV, KV:KV + P], w_dkv[:, :, :]), (mq[:, 0:P], w_dq[:, :, 0:P]),
                                  (mq[0:QC - P, P:2 * P], w_dq[:, :, P:QC])):
                        for c in range(DC):
                            mm = pe.matmul(to, w[:, c, :], xs[:, u, c, :], start=(c == 0), stop=(c == DC - 1))
                    mm.then_inc(norm.used, 1)

                ahead(pe, lambda t, u: norm.tensor_turn(pe, t, u), latents, RING, 2)


def latent_attention(nc, ident, banks, c_rows, c_first, c_second, cqT, A_all, UT_all, dispatched):
    with ExitStack() as ctx:
        sb = lambda n, s, d=F32: ctx.enter_context(nc.sbuf_tensor(n, s, d))
        sem = phase_semaphores(nc, ctx, "latent_")
        HU = 2 * P
        A_now = sb("A_now", [P, 2, KA])
        q_raw = sb("q_raw", [KA, S])
        q_first = sb("q_first", [SPLIT, 2, S], F32R)
        q_second = sb("q_second", [P, 2, S], F32R)
        c_parts = sb("c_parts", [P, QT, P], F32R)
        neg_max = sb("neg_max", [P, 2 * QT])
        sums = sb("sums", [P, 2 * QT])
        inverses = sb("inverses", [P, 2 * QT])
        probs = sb("probs", [P, QT, S])
        probsT_hi = sb("probsT_hi", [P, 2, QT, HU], F32R)
        probsT_lo = sb("probsT_lo", [P, 2, QT, HU], F32R)
        u_part = sb("u_part", [KV, S])
        c_now = sb("c_now", [P, QT, KV])
        zeros = sb("zeros", [P, CT * D])
        ps_s, ps_t, ps_u, ps_q = banks[0:4], banks[4:6], banks[6], banks[7]
        A_staged, q_made, q_out, q_split = sem("A_staged"), sem("q_made"), sem("q_out"), sem("q_split")
        q_again_out, bias_split = sem("q_again_out"), sem("bias_split")
        filled, c_now_done, c_hi_done, c_staged = sem("filled"), sem("c_now_done"), sem("c_hi_done"), sem("c_staged")
        scored, maxed, exped, turned = sem("scored"), sem("maxed"), sem("exped"), sem("turned")
        hi_done, lo_done = sem("hi_done"), sem("lo_done")
        inverted, scaled = sem("inverted"), sem("scaled")
        mixed, part_out, U_out = sem("mixed"), sem("part_out"), sem("U_out")
        zero_set, cleared = sem("zero_set"), sem("cleared")


        def pairs(eng, b, pair):
            pair(b, 0, True)
            with eng.Fori(1, H0 // 2 - 1) as j:
                pair(b, 2 * j, False)
            pair(b, H0 - 2, False)

        def unit(b, h, q):
            return (b * H0 + h) * QT + q

        def half(b, h, i):
            return (b * H0 + h) * 2 + i

        with nc.Block() as block:
            @block.sync
            def _(sp):
                sp.wait_ge(zero_set, 1)
                for e in range(E1):
                    sp.dma_start(dispatched[e * CAP:(e + 1) * CAP, :].rearrange("(p r) d -> p (r d)", p=P),
                                 zeros[:, :]).then_inc(cleared, 16)
                sp.wait_ge(cleared, 16 * E1)

            @block.gpsimd
            def _(pool):
                credit(pool, A_staged, q_split, c_now_done, c_staged, scaled)

                def stage(m, h):
                    pool.wait_ge(q_made, reuse(m, 1))
                    pool.tensor_copy(A_now[:, :, :], A_all[:, bass.ds(h, 1), :, :]
                                     .rearrange("p a c k -> p (a c) k")).then_inc(A_staged, 1)

                def split(m, u):
                    pool.wait_ge(q_out, done(m))
                    pool.tensor_tensor(q_second[0:KV, u, :], q_raw[0:KV, :], q_first[0:KV, u, :].bitcast(F32),
                                       ALU.subtract).then_inc(q_split, 1)

                def scale(b, h, u, q):
                    n = unit(b, h, q)
                    pool.wait_ge(inverted, done(n))
                    i = u * QT + q
                    pool.tensor_tensor(probs[:, q, :], probs[:, q, :],
                                       inverses[:, i:i + 1].to_broadcast([P, S]), ALU.mult).then_inc(scaled, 1)

                def pair(b, h0):
                    for u in range(2):
                        h = h0 + u
                        for q in range(QT):
                            if q < 2:
                                scale(b, h, u, q + 2)
                            else:
                                scale(b, h + 1, 1 - u, q - 2)
                            if q == 2:
                                stage(b * H0 + h + 3, (h + 3) % H0)
                            if q == 3:
                                split(b * H0 + h + 2, u)

                stage(0, 0)
                pool.memset(zeros[:, :], 0.0).then_inc(zero_set, 1)
                pool.tensor_copy(c_now[:, :, :], c_rows[:, 0:QT, :]).then_inc(c_now_done, 1)
                with pool.Fori(1, 3) as h:
                    stage(h, h)
                for u in range(2):
                    split(u, u)
                scale(0, 0, 0, 0)
                scale(0, 0, 0, 1)
                with pool.Fori(0, B) as b:
                    pool.wait_ge(c_hi_done, done(b))
                    pool.tensor_tensor(c_parts[:, :, KV:P], c_now[:, :, :], c_parts[:, :, 0:KV].bitcast(F32),
                                       ALU.subtract).then_inc(c_staged, 1)
                    with pool.Fori(0, H0 // 2) as j:
                        pair(b, 2 * j)
                    pool.tensor_copy(c_now[:, :, :], c_rows[:, bass.ts((b + 1) % B, QT), :]).then_inc(c_now_done, 1)

            @block.tensor
            def _(pe):
                credit(pe, q_made, scored, turned, mixed)

                def keys_of(b, h):
                    return bass.ts((b + 1) % B if isinstance(h, int) and h >= H0 else b, S)

                def queries(b, h, u):
                    m = b * H0 + h
                    pe.wait_ge(A_staged, done(m))
                    pe.wait_ge(q_again_out, reuse(m, 1))
                    pe.matmul(ps_q[0:KA, :], A_now[:, 0, :], cqT[:, 0, keys_of(b, h)], start=True, stop=False)
                    pe.matmul(ps_q[0:KA, :], A_now[0:KA, 1, :], cqT[0:KA, 1, keys_of(b, h)],
                              start=False, stop=True).then_inc(q_made, 1)

                def scores(b, h, u, q):
                    if q == 0:
                        pe.wait_ge(q_split, done(b * H0 + h))
                        pe.wait_ge(bias_split, done(b * H0 + h))
                        pe.wait_ge(q_again_out, done(b * H0 + h))
                    pe.wait_ge(exped, reuse(unit(b, h, q), 4))
                    pe.matmul(ps_s[q], q_first[:, u, q * P:(q + 1) * P], c_first[:, keys_of(b, h)],
                              start=True, stop=False)
                    pe.matmul(ps_s[q], q_second[:, u, q * P:(q + 1) * P], c_second[:, keys_of(b, h)],
                              start=False, stop=True).then_inc(scored, 1)

                def turn(b, h, q):
                    n = unit(b, h, q)
                    pe.wait_ge(scaled, done(n))
                    pe.wait_ge(lo_done, reuse(n, 2))
                    for k in range(QT):
                        m = pe.transpose(ps_t[q % 2][:, k * P:(k + 1) * P], probs[:, q, k * P:(k + 1) * P],
                                         ident[:, :])
                    m.then_inc(turned, 1)

                def mixes(b, h, i):
                    if i == 0:
                        pe.wait_ge(U_out, reuse(b * H0 + h, 1))
                    pe.wait_ge(lo_done, done(unit(b, h, 2 * i + 1)))
                    to = ps_u[:, i * HU:(i + 1) * HU]
                    for k in range(QT):
                        m = pe.matmul(to, c_parts[:, k, :], probsT_hi[:, i, k, :], start=(k == 0), stop=(k == QT - 1))
                        if k < QT - 1:
                            pe.matmul(to[0:KV, :], c_parts[:, k, 0:KV], probsT_lo[:, i, k, :], start=False, stop=False)
                        if k == QT - 2:
                            pe.matmul(to[0:KV, :], c_parts[:, k + 1, 0:KV], probsT_lo[:, i, k + 1, :],
                                      start=False, stop=False)
                    m.then_inc(mixed, 1)

                def pair(b, h0, first):
                    for u in range(2):
                        h = h0 + u
                        for q in range(QT):
                            turn(b, h, q)
                            if q == 0:
                                scores(b, h, u, 3)
                            else:
                                scores(b, h + 1, 1 - u, q - 1)
                            if q == 0 and (u == 1 or not first):
                                mixes(b, h - 1, 1)
                            if q == 1:
                                queries(b, h + 2, u)
                            if q == 2:
                                if first and u == 0:
                                    pe.wait_ge(c_staged, done(b))
                                mixes(b, h, 0)

                queries(0, 0, 0)
                queries(0, 1, 1)
                for q in range(3):
                    scores(0, 0, 0, q)
                with pe.Fori(0, B) as b:
                    pairs(pe, b, pair)
                    mixes(b, H0 - 1, 1)

            @block.scalar
            def _(act):
                credit(act, q_out, q_again_out, exped, hi_done, c_hi_done, part_out)

                def queries(b, h, u):
                    m = b * H0 + h
                    act.wait_ge(q_made, done(m))
                    act.wait_ge(q_split, reuse(m, 1))
                    act.wait_ge(bias_split, reuse(m, 1))
                    act.copy(q_raw[:, :], ps_q[0:KA, :])

                def queries_high(u):
                    act.copy(q_first[0:KA, u, :], ps_q[0:KA, :]).then_inc(q_out, 1)

                def queries_again(u):
                    act.copy(q_second[KV:2 * KV, u, :], ps_q[0:KV, :]).then_inc(q_again_out, 1)

                def exps(b, h, u, q):
                    n = unit(b, h, q)
                    act.wait_ge(maxed, done(n))
                    act.wait_ge(turned, reuse(n, 4))
                    i = u * QT + q
                    act.activation(probs[:, q, :], ps_s[q], ACT.Exp, bias=neg_max[:, i:i + 1],
                                   accum_out=sums[:, i:i + 1]).then_inc(exped, 1)

                def high(b, h, q):
                    n = unit(b, h, q)
                    i = q // 2
                    act.wait_ge(turned, done(n))
                    if q % 2 == 0:
                        act.wait_ge(mixed, reuse(half(b, h, i), 2))
                    act.copy(probsT_hi[:, i, :, (q % 2) * P:(q % 2 + 1) * P],
                             ps_t[q % 2].rearrange("p (k n) -> p k n", k=QT)).then_inc(hi_done, 1)

                def part(b, h):
                    act.wait_ge(mixed, done(half(b, h, 1)))
                    act.wait_ge(U_out, reuse(b * H0 + h, 1))
                    act.copy(u_part[:, :], ps_u[KV:2 * KV, :]).then_inc(part_out, 1)

                def pair(b, h0, first):
                    for u in range(2):
                        h = h0 + u
                        for q in range(QT):
                            if q < 2:
                                exps(b, h, u, q + 2)
                            else:
                                exps(b, h + 1, 1 - u, q - 2)
                            if q == 1 and (u == 1 or not first):
                                part(b, h - 1)
                            high(b, h, q)
                            if q == 0:
                                queries_again(1 - u)
                            if q == 2:
                                queries(b, h + 2, u)
                            if q == 3:
                                queries_high(u)

                act.wait_ge(filled, 1)
                for u in range(2):
                    queries(0, u, u)
                    queries_high(u)
                    if u == 0:
                        queries_again(u)
                exps(0, 0, 0, 0)
                exps(0, 0, 0, 1)
                with act.Fori(0, B) as b:
                    act.wait_ge(c_now_done, done(b))
                    act.wait_ge(mixed, reuse(half(b, 0, 0), 1))
                    act.copy(c_parts[:, :, 0:KV], c_now[:, :, :]).then_inc(c_hi_done, 1)
                    pairs(act, b, pair)
                    part(b, H0 - 1)

            @block.vector
            def _(dve):
                credit(dve, bias_split, maxed, inverted, lo_done, U_out)
                dve.memset(q_first[KV:SPLIT, :, :].bitcast(F32), 0.0).then_inc(filled, 1)

                def split_bias(b, h, u):
                    m = b * H0 + h
                    dve.wait_ge(q_out, done(m))
                    dve.tensor_tensor(q_first[SPLIT - 1:SPLIT, u, :], q_raw[KV:KA, :],
                                      q_first[KV:KA, u, :].bitcast(F32), ALU.subtract).then_inc(bias_split, 1)

                def maxes(b, h, u, q):
                    dve.wait_ge(scored, done(unit(b, h, q)))
                    dve.tensor_reduce(neg_max[:, u * QT + q:u * QT + q + 1], ps_s[q], AX.X, ALU.max,
                                      negate=True).then_inc(maxed, 1)

                def low(b, h, q):
                    n = unit(b, h, q)
                    i = q // 2
                    dve.wait_ge(hi_done, done(n))
                    if q % 2 == 0:
                        dve.wait_ge(mixed, reuse(half(b, h, i), 2))
                    at = slice((q % 2) * P, (q % 2 + 1) * P)
                    dve.tensor_tensor(probsT_lo[:, i, :, at], ps_t[q % 2].rearrange("p (k n) -> p k n", k=QT),
                                      probsT_hi[:, i, :, at].bitcast(F32), ALU.subtract).then_inc(lo_done, 1)

                def inverse(b, h, u, q):
                    dve.wait_ge(exped, done(unit(b, h, q)))
                    i = u * QT + q
                    dve.reciprocal(inverses[:, i:i + 1], sums[:, i:i + 1]).then_inc(inverted, 1)

                def add(b, h, u):
                    dve.wait_ge(part_out, done(b * H0 + h))
                    dve.tensor_tensor(UT_all[u * KV:(u + 1) * KV, bass.ts(b * (H0 // 2) + (h - u) // 2, S)],
                                      ps_u[0:KV, :], u_part[:, :], ALU.add).then_inc(U_out, 1)

                def pair(b, h0, first):
                    for u in range(2):
                        h = h0 + u
                        for q in range(QT):
                            if q > 0:
                                low(b, h, q - 1)
                            elif u == 1 or not first:
                                low(b, h - 1, QT - 1)
                            if q < 2:
                                inverse(b, h, u, q + 2)
                            else:
                                inverse(b, h + 1, 1 - u, q - 2)
                            if q == 0:
                                maxes(b, h, u, 3)
                            else:
                                maxes(b, h + 1, 1 - u, q - 1)
                            if q == 1 and (u == 1 or not first):
                                add(b, h - 1, 1 - u)
                            if q == 0:
                                split_bias(b, h + 1, 1 - u)

                split_bias(0, 0, 0)
                for q in range(3):
                    maxes(0, 0, 0, q)
                inverse(0, 0, 0, 0)
                inverse(0, 0, 0, 1)
                with dve.Fori(0, B) as b:
                    pairs(dve, b, pair)
                    low(b, H0 - 1, QT - 1)
                    add(b, H0 - 1, 1)


def latent_out(nc, x, psum, UT_all, w, bias_row):
    with ExitStack() as ctx:
        sb = lambda n, s: ctx.enter_context(nc.sbuf_tensor(f"out0_{n}", s, F32))
        sem = phase_semaphores(nc, ctx, "out0_")
        HP = H0 // 2
        mixes = sb("mixes", [P, 2, HP, P])
        ones_row = sb("ones_row", [1, P])
        ps_o = [psum[:, u * 512:u * 512 + D] for u in range(2)]
        ones_set, staged, projected, added = sem("ones_set"), sem("staged"), sem("projected"), sem("added")

        with nc.Block() as block:
            @block.gpsimd
            def _(pool):
                credit(pool, staged)
                pool.memset(ones_row[:, :], 1.0).then_inc(ones_set, 1)
                with pool.Fori(0, B) as b:
                    for q in range(QT):
                        u = q % 2
                        pool.wait_ge(projected, reuse(b * QT + q, 2))
                        v = UT_all[:, bass.ts(b, HP * S)].rearrange("p (k n) -> p k n", k=HP)
                        pool.tensor_copy(mixes[:, u, :, :], v[:, :, q * P:(q + 1) * P]).then_inc(staged, 1)

            @block.tensor
            def _(pe):
                credit(pe, projected)
                pe.wait_ge(ones_set, 1)

                def project(t, u):
                    pe.wait_ge(staged, done(t))
                    pe.wait_ge(added, reuse(t, 2))
                    for k in range(HP):
                        pe.matmul(ps_o[u], mixes[:, u, k, :], w[:, k, :], start=(k == 0), stop=False)
                    pe.matmul(ps_o[u], ones_row[:, :], bias_row[:, :], start=False, stop=True).then_inc(projected, 1)

                tiles(pe, project)

            @block.vector
            def _(dve):
                credit(dve, added)

                def add(t, u):
                    dve.wait_ge(projected, done(t))
                    dve.tensor_tensor(x[:, t, :], ps_o[u], x[:, t, :], ALU.add).then_inc(added, 1)

                tiles(dve, add)


def project_out(nc, name, x, ident, psum, mixes, chunks, w, bias_row=None):
    with ExitStack() as ctx:
        sb = lambda n, s: ctx.enter_context(nc.sbuf_tensor(f"{name}_{n}", s, F32))
        sem = phase_semaphores(nc, ctx, name + "_")
        W = chunks * P
        rows = sb("rows", [P, 2, W])
        turned_rows = sb("turned_rows", [P, 2, W])
        ones_row = sb("ones_row", [1, P])
        half = min(W, 512)
        wide = W > 512
        ps_t = [[psum[:, (2 * u + i) * 512:(2 * u + i) * 512 + half] for i in range(1 + wide)] for u in range(2)]
        ps_o = [psum[:, (4 + u) * 512:(4 + u) * 512 + D] for u in range(2)]
        ones_set, staged, turned = sem("ones_set"), sem("staged"), sem("turned")
        copied, copied_right, projected, added = sem("copied"), sem("copied_right"), sem("projected"), sem("added")

        with nc.Block() as block:
            @block.gpsimd
            def _(pool):
                credit(pool, staged)
                pool.memset(ones_row[:, :], 1.0).then_inc(ones_set, 1)

                def stage(t, u):
                    pool.wait_ge(turned, reuse(t, 2))
                    pool.tensor_copy(rows[:, u, :], mixes[:, t, :]).then_inc(staged, 1)

                tiles(pool, stage)

            @block.tensor
            def _(pe):
                credit(pe, turned, projected)
                pe.wait_ge(ones_set, 1)

                def turn(t, u):
                    pe.wait_ge(staged, done(t))
                    pe.wait_ge(copied, reuse(t, 2))
                    if wide:
                        pe.wait_ge(copied_right, reuse(t, 2))
                    for k in range(chunks):
                        m = pe.transpose(ps_t[u][k // 4][:, (k % 4) * P:(k % 4 + 1) * P],
                                         rows[:, u, k * P:(k + 1) * P], ident[:, :])
                    m.then_inc(turned, 1)

                def project(t, u):
                    pe.wait_ge(copied, done(t))
                    if wide:
                        pe.wait_ge(copied_right, done(t))
                    pe.wait_ge(added, reuse(t, 2))
                    for k in range(chunks):
                        m = pe.matmul(ps_o[u], turned_rows[:, u, k * P:(k + 1) * P], w[:, k, :],
                                      start=(k == 0), stop=(k == chunks - 1 and bias_row is None))
                    if bias_row is not None:
                        m = pe.matmul(ps_o[u], ones_row[:, :], bias_row[:, :], start=False, stop=True)
                    m.then_inc(projected, 1)

                ahead(pe, turn, project)

            @block.scalar
            def _(act):
                credit(act, copied)

                def copy(t, u):
                    act.wait_ge(turned, done(t))
                    act.wait_ge(projected, reuse(t, 2))
                    act.copy(turned_rows[:, u, 0:half], ps_t[u][0]).then_inc(copied, 1)

                tiles(act, copy)

            @block.vector
            def _(dve):
                credit(dve, copied_right, added)

                def copy(t, u):
                    if wide:
                        dve.wait_ge(turned, done(t))
                        dve.wait_ge(projected, reuse(t, 2))
                        dve.tensor_copy(turned_rows[:, u, half:W], ps_t[u][1]).then_inc(copied_right, 1)

                def add(t, u):
                    dve.wait_ge(projected, done(t))
                    dve.tensor_tensor(x[:, t, :], ps_o[u], x[:, t, :], ALU.add).then_inc(added, 1)

                ahead(dve, copy, add)


def experts_prepare(nc, x, ident, eps, banks, xT_hi, xT_lo, comb_dram, ins):
    with ExitStack() as ctx:
        sb = lambda n, s: ctx.enter_context(nc.sbuf_tensor(n, s, F32))
        sem = phase_semaphores(nc, ctx, "experts_prepare_")
        norm = Norm(nc, ctx, "n2", x, ident, banks[0:2], eps)
        ps_l = banks[2:4]
        EA = E0 + 2
        w_r = sb("w_r", [P, DC, E0 + 1])
        logits = sb("logits", [P, NT, E0 + 1])
        top = sb("top", [P, NT, 8])
        rest = sb("rest", [P, NT, E0])
        shifted = sb("shifted", [P, NT, E0])
        chosen = sb("chosen", [P, NT, E0])
        total = sb("total", [P, NT, 1])
        comb = sb("comb", [P, NT, EA])
        combT = sb("combT", [EA, NT * P])
        w_loaded, hi_done = sem("w_loaded"), sem("hi_done")
        logit_out, max_done, rest_done, step_done = sem("logit_out"), sem("max_done"), sem("rest_done"), sem("step_done")
        exp_done, comb_done = sem("exp_done"), sem("comb_done")
        comb_turned, combT_done, stored = sem("comb_turned"), sem("combT_done"), sem("stored")

        with nc.Block() as block:
            @block.sync
            def _(sp):
                sp.dma_start(w_r[:, :, :], ins["w_router"].rearrange("(c p) k -> p c k", p=P)).then_inc(w_loaded, 16)
                sp.wait_ge(combT_done, NT // 4)
                sp.dma_start(comb_dram[:, :], combT[:, :]).then_inc(stored, 16)
                sp.wait_ge(stored, 16)

            @block.gpsimd
            def _(pool):
                credit(pool, norm.copied)

                def copy(t, u):
                    pool.wait_ge(norm.xnT_done, done(t))
                    pool.tensor_copy(xT_hi[:, :, bass.ts(t, P)], norm.xnT[:, u, :, :]).then_inc(hi_done, 1)
                    pool.wait_ge(hi_done, t + 1)
                    pool.tensor_tensor(xT_lo[:, :, bass.ts(t, P)], norm.xnT[:, u, :, :],
                                       xT_hi[:, :, bass.ts(t, P)].bitcast(F32), ALU.subtract).then_inc(norm.copied, 1)

                tiles(pool, copy, RING)

            @block.scalar
            def _(act):
                credit(act, norm.xnT_done)
                norm.scalar_std(act)
                tiles(act, lambda t, u: norm.scalar_tile(act, t, u, copied=True), RING)
                act.wait_ge(step_done, 2)
                act.activation(shifted[:, :, :], shifted[:, :, :], ACT.Exp).then_inc(exp_done, 1)
                act.activation(comb[:, :, E0:E0 + 1], logits[:, :, E0:E0 + 1], ACT.Sigmoid).then_inc(exp_done, 1)
                for g in range(NT // 4):
                    act.wait_ge(comb_turned, g + 1)
                    act.copy(combT[:, g * 512:(g + 1) * 512], banks[4 + g][0:EA, :]).then_inc(combT_done, 1)

            @block.vector
            def _(dve):
                credit(dve, norm.xn_done, logit_out)
                norm.vector_stats(dve)

                def logit(t, u):
                    dve.wait_ge(norm.used, done(t))
                    dve.tensor_copy(logits[:, t, :], ps_l[u % 2][:, 0:E0 + 1]).then_inc(logit_out, 1)

                ahead(dve, lambda t, u: norm.vector_tile(dve, t, u), logit, RING, 2)
                dve.wait_ge(logit_out, done(NT - 1))
                dve.memset(comb[:, :, E0 + 1:EA], 0.0).then_inc(step_done, 1)
                for t in range(NT):
                    dve.max(top[:, t, :], logits[:, t, 0:E0]).then_inc(max_done, 1)
                dve.wait_ge(max_done, NT)
                dve.tensor_tensor(shifted[:, :, :], logits[:, :, 0:E0], top[:, :, 0:1].to_broadcast([P, NT, E0]),
                                  ALU.subtract).then_inc(step_done, 1)
                for t in range(NT):
                    dve.match_replace(rest[:, t, :], top[:, t, :], logits[:, t, 0:E0], -3.0e38).then_inc(rest_done, 1)
                dve.wait_ge(rest_done, NT)
                dve.tensor_tensor(chosen[:, :, :], rest[:, :, :], logits[:, :, 0:E0],
                                  ALU.not_equal).then_inc(step_done, 1)
                dve.wait_ge(step_done, 3)
                dve.wait_ge(exp_done, 1)
                dve.tensor_tensor(chosen[:, :, :], chosen[:, :, :], shifted[:, :, :], ALU.mult).then_inc(step_done, 1)
                dve.wait_ge(step_done, 4)
                dve.tensor_reduce(total[:, :, 0], chosen[:, :, :], AX.X, ALU.add).then_inc(step_done, 1)
                dve.wait_ge(step_done, 5)
                dve.reciprocal(total[:, :, :], total[:, :, :]).then_inc(step_done, 1)
                dve.wait_ge(step_done, 6)
                dve.tensor_tensor(comb[:, :, 0:E0], chosen[:, :, :], total[:, :, :].to_broadcast([P, NT, E0]),
                                  ALU.mult).then_inc(comb_done, 1)

            @block.tensor
            def _(pe):
                credit(pe, norm.turned, norm.used)
                pe.wait_ge(w_loaded, 16)

                def route(t, u):
                    pe.wait_ge(norm.xnT_done, done(t))
                    pe.wait_ge(logit_out, reuse(t, 2))
                    for c in range(DC):
                        m = pe.matmul(ps_l[u % 2][:, 0:E0 + 1], norm.xnT[:, u, c, :], w_r[:, c, :],
                                      start=(c == 0), stop=(c == DC - 1))
                    m.then_inc(norm.used, 1)

                ahead(pe, lambda t, u: norm.tensor_turn(pe, t, u), route, RING, 2)
                pe.wait_ge(comb_done, 1)
                pe.wait_ge(exp_done, 2)
                for t in range(NT):
                    m = pe.transpose(banks[4 + t // 4][0:EA, (t % 4) * P:(t % 4 + 1) * P], comb[:, t, :], ident[:, :])
                    if t % 4 == 3:
                        m.then_inc(comb_turned, 1)


def experts(nc, x, psum, xT_hi, xT_lo, comb_dram, ins):
    with ExitStack() as ctx:
        sb = lambda n, s, d=F32: ctx.enter_context(nc.sbuf_tensor(n, s, d))
        sem = phase_semaphores(nc, ctx, "experts_")
        PR = 4
        TURNS = E0 // 2 // PR
        UNITS = PR * B
        GU = 2 * DC * P
        w_raw = sb("w_raw", [P, PR, GU + D])
        w_hi = sb("w_hi", [P, PR, GU + D], F32R)
        w_lo = sb("w_lo", [P, PR, GU + D], F32R)
        weight = sb("weight", [P, 4, S])
        gate = sb("gate", [P, 2, S])
        scaled = sb("scaled", [P, 2, S])
        hidden = sb("hidden", [P, 2, S])
        hidden_hi = sb("hidden_hi", [P, 4, S], F32R)
        hidden_lo = sb("hidden_lo", [P, 4, S], F32R)
        ps_g = [psum[:, u * 512:(u + 1) * 512] for u in range(2)]
        ps_u = [psum[:, (2 + u) * 512:(3 + u) * 512] for u in range(2)]
        ps_o = [psum[:, (4 + 2 * u) * 512:(6 + 2 * u) * 512] for u in range(2)]
        w_loaded = [sem(f"w_loaded{p}") for p in range(PR)]
        weight_loaded = [sem(f"weight_loaded{k}") for k in range(4)]
        w_hi_done, w_split = sem("w_hi_done"), sem("w_split")
        gu_done, silu_done, scaled_done, hidden_done = (
            sem(n) for n in ("gu_done", "silu_done", "scaled_done", "hidden_done"))
        hi_done, lo_done = sem("hi_done"), sem("lo_done")
        down_done, added = sem("down_done"), sem("added")

        def unit(g, k):
            return B + g * UNITS + k

        def split(g, p):
            return 1 + g * PR + p

        def loads(g, p):
            return 32 * g + (64 if p == PR - 1 else 32)

        def splits_in_turn(g, last, split_pair):
            def at(k):
                if k < 2:
                    split_pair(g, k + 2, unit(g, k) - 2)
                elif k >= UNITS - 2 and not last:
                    split_pair(g + 1, k - (UNITS - 2), unit(g, k) - 2)
            return at

        with nc.Block() as block:
            @block.sync
            def _(sp):
                def load_weights(p, pair):
                    sp.dma_start(w_raw[:, p, 0:GU].rearrange("p (g c m) -> p g c m", g=2, c=DC),
                                 ins["w_gu0"][pair].rearrange("g (c k) m -> k g c m", k=P)).then_inc(w_loaded[p], 16)
                    sp.dma_start(w_raw[:, p, GU:GU + D], ins["w_d0"][pair]).then_inc(w_loaded[p], 16)

                def load_weight(n, k, pair, b):
                    sp.wait_ge(scaled_done, reuse(n, 4))
                    for i in range(2):
                        sp.dma_start(weight[i * I0:(i + 1) * I0, k % 4, :],
                                     comb_dram[bass.ds(2 * pair + i, 1), b * S:(b + 1) * S].to_broadcast([I0, S])) \
                            .then_inc(weight_loaded[k % 4], 16)

                def turn(g, last):
                    for k in range(UNITS):
                        if 2 <= k < 2 + PR and not last:
                            sp.wait_ge(w_split, done(split(g, k - 2)))
                            load_weights(k - 2, (g + 1) * PR + k - 2)
                        if k + 4 < UNITS:
                            load_weight(unit(g, k) + 4, k + 4, g * PR + k % PR, (k + 4) // PR)
                        elif not last:
                            load_weight(unit(g, k) + 4, k + 4, (g + 1) * PR + k % PR, 0)

                load_weights(PR - 1, E0 // 2)
                for p in range(PR - 1):
                    load_weights(p, p)
                for b in range(B):
                    load_weight(b, b, E0 // 2, b)
                sp.wait_ge(w_split, done(0))
                load_weights(PR - 1, PR - 1)
                for p in range(PR):
                    load_weight(B + p, p, p, 0)
                with sp.Fori(0, TURNS - 1) as g:
                    turn(g, False)
                turn(TURNS - 1, True)

            @block.tensor
            def _(pe):
                credit(pe, gu_done, down_done)

                def gates_ups(n, p, b, u):
                    pe.wait_ge(silu_done, reuse(n, 2))
                    pe.wait_ge(hidden_done, reuse(n, 2))
                    parts = ((w_hi, xT_hi), (w_hi, xT_lo), (w_lo, xT_hi))
                    for i, to in ((0, ps_g[u]), (1, ps_u[u])):
                        for w, xs in parts:
                            for c in range(DC):
                                at = (i * DC + c) * P
                                m = pe.matmul(to, w[:, p, at:at + P], xs[:, c, b * S:(b + 1) * S],
                                              start=(w is w_hi and xs is xT_hi and c == 0),
                                              stop=(w is w_lo and c == DC - 1))
                    m.then_inc(gu_done, 1)

                def down(n, p, b, u, first, last, add):
                    pe.wait_ge(lo_done, done(n))
                    if first:
                        pe.wait_ge(added, reuse(add, 2))
                    for q in range(QT):
                        for j, (hs, w) in enumerate(((hidden_hi, w_hi), (hidden_hi, w_lo), (hidden_lo, w_hi))):
                            m = pe.matmul(ps_o[b % 2][:, q * D:(q + 1) * D], hs[:, u, q * P:(q + 1) * P],
                                          w[:, p, GU:GU + D], start=(first and q % 2 == 0 and j == 0),
                                          stop=(last and j == 2), skip_group_check=True)
                    m.then_inc(down_done, 1)

                pe.wait_ge(w_split, done(0))
                for b in range(B):
                    gates_ups(b, PR - 1, b, b % 2)
                    if b > 1:
                        down(b - 2, PR - 1, b - 2, b - 2, True, True, b - 2)
                for b in range(B - 2, B):
                    down(b, PR - 1, b, b, True, True, b)

                def turn(g, first):
                    for k in range(UNITS):
                        b, p = k // PR, k % PR
                        if b == 0:
                            pe.wait_ge(w_split, done(split(g, p)))
                        gates_ups(unit(g, k), p, b, k % 2)
                        if k >= 2:
                            down_k(g, k - 2)
                        elif not first:
                            down_k(g - 1, UNITS + k - 2)

                def down_k(g, k):
                    b, p = k // PR, k % PR
                    down(unit(g, k), p, b, k % 4, p == 0, p == PR - 1, B + g * B + b)

                turn(0, True)
                with pe.Fori(1, TURNS) as g:
                    turn(g, False)
                for k in range(UNITS - 2, UNITS):
                    down_k(TURNS - 1, k)

            @block.scalar
            def _(act):
                credit(act, silu_done, hi_done, w_hi_done)

                def silu(n, u):
                    act.wait_ge(gu_done, done(n))
                    act.wait_ge(scaled_done, reuse(n, 2))
                    act.activation(gate[:, u, :], ps_g[u], ACT.Silu).then_inc(silu_done, 1)

                def high(n, u, v):
                    act.wait_ge(hidden_done, done(n))
                    act.wait_ge(down_done, reuse(n, 4))
                    act.copy(hidden_hi[:, v, :], hidden[:, u, :]).then_inc(hi_done, 1)

                def split_pair(g, p, used):
                    act.wait_ge(w_loaded[p], loads(g, p))
                    act.wait_ge(down_done, done(used))
                    act.copy(w_hi[:, p, :], w_raw[:, p, :]).then_inc(w_hi_done, 1)

                act.wait_ge(w_loaded[PR - 1], 32)
                act.copy(w_hi[:, PR - 1, :], w_raw[:, PR - 1, :]).then_inc(w_hi_done, 1)
                for b in range(B):
                    silu(b, b % 2)
                    if b > 0:
                        high(b - 1, (b - 1) % 2, b - 1)
                    if b < 2:
                        act.wait_ge(w_loaded[b], 32)
                        act.copy(w_hi[:, b, :], w_raw[:, b, :]).then_inc(w_hi_done, 1)
                high(B - 1, (B - 1) % 2, B - 1)

                def turn(g, last):
                    split_at = splits_in_turn(g, last, split_pair)
                    for k in range(UNITS):
                        silu(unit(g, k), k % 2)
                        if k > 0:
                            high(unit(g, k) - 1, (k - 1) % 2, (k - 1) % 4)
                        split_at(k)
                    high(unit(g, UNITS - 1), 1, 3)

                with act.Fori(0, TURNS - 1) as g:
                    turn(g, False)
                turn(TURNS - 1, True)

            @block.gpsimd
            def _(pool):
                credit(pool, scaled_done, w_split)

                def scale(n, u, buffer, loads):
                    pool.wait_ge(silu_done, done(n))
                    pool.wait_ge(weight_loaded[buffer], 16 * loads)
                    pool.wait_ge(hidden_done, reuse(n, 2))
                    pool.tensor_tensor(scaled[:, u, :], gate[:, u, :], weight[:, buffer, :],
                                       ALU.mult).then_inc(scaled_done, 1)

                def low(n, p):
                    pool.wait_ge(w_hi_done, done(n))
                    pool.tensor_tensor(w_lo[:, p, :], w_raw[:, p, :], w_hi[:, p, :].bitcast(F32),
                                       ALU.subtract).then_inc(w_split, 1)

                low(0, PR - 1)
                for b in range(B):
                    scale(b, b % 2, b, 2)
                    if b < 2:
                        low(split(0, b), b)

                def turn(g, last):
                    split_at = splits_in_turn(g, last, lambda g, p, used: low(split(g, p), p))
                    for k in range(UNITS):
                        scale(unit(g, k), k % 2, k % 4, 2 * (g * (UNITS // 4) + k // 4 + 2))
                        split_at(k)

                with pool.Fori(0, TURNS - 1) as g:
                    turn(g, False)
                turn(TURNS - 1, True)

            @block.vector
            def _(dve):
                credit(dve, hidden_done, lo_done, added)

                def hide(n, u, v):
                    dve.wait_ge(scaled_done, done(n))
                    dve.wait_ge(lo_done, reuse(n, 2))
                    dve.tensor_tensor(hidden[:, u, :], ps_u[u], scaled[:, u, :], ALU.mult).then_inc(hidden_done, 1)

                def low(n, u, v):
                    dve.wait_ge(hi_done, done(n))
                    dve.tensor_tensor(hidden_lo[:, v, :], hidden[:, u, :], hidden_hi[:, v, :].bitcast(F32),
                                      ALU.subtract).then_inc(lo_done, 1)

                def add(n, b):
                    dve.wait_ge(down_done, done(n))
                    xb = x[:, b * QT:(b + 1) * QT, :].rearrange("p t d -> p (t d)")
                    dve.tensor_tensor(xb, ps_o[b % 2], xb, ALU.add).then_inc(added, 1)

                for b in range(B):
                    hide(b, b % 2, b)
                    if b > 0:
                        low(b - 1, (b - 1) % 2, b - 1)
                    if b > 2:
                        add(b - 3, b - 3)
                low(B - 1, 1, B - 1)
                for b in range(B - 3, B):
                    add(b, b)

                def turn(g, first):
                    for k in range(UNITS):
                        hide(unit(g, k), k % 2, k % 4)
                        if k > 0:
                            low(unit(g, k) - 1, (k - 1) % 2, (k - 1) % 4)
                        if k % PR == 2 and (k > 2 or not first):
                            add(unit(g, k) - 3, (k // PR - 1) % B)
                    low(unit(g, UNITS - 1), 1, 3)

                turn(0, True)
                with dve.Fori(1, TURNS) as g:
                    turn(g, False)
                add(unit(TURNS - 1, UNITS - 1), B - 1)


def alibi_prepare(nc, x, ident, eps, banks, xT, v_all, biases, w_out, ins):
    with ExitStack() as ctx:
        sb = lambda n, s, d=F32: ctx.enter_context(nc.sbuf_tensor(n, s, d))
        sem = phase_semaphores(nc, ctx, "alibi_prepare_")
        norm = Norm(nc, ctx, "n3", x, ident, banks[0:2], eps)
        ps_v = banks[2:4]
        w_v = sb("w_v", [P, DC, D])
        distance_int = sb("distance_int", [P, S], mybir.dt.int32)
        distance = sb("distance", [P, S])
        w_loaded, w_out_loaded, v_out, far = sem("w_loaded"), sem("w_out_loaded"), sem("v_out"), sem("far")

        with nc.Block() as block:
            @block.sync
            def _(sp):
                sp.dma_start(w_v[:, :, :], ins["w_v"].rearrange("(c p) k -> p c k", p=P)).then_inc(w_loaded, 16)
                sp.dma_start(w_out[:, :, :], ins["w_out1"].rearrange("(c p) k -> p c k", p=P)).then_inc(w_out_loaded, 16)
                sp.wait_ge(w_out_loaded, 16)

            @block.gpsimd
            def _(pool):
                credit(pool, norm.copied)
                pool.iota(distance_int[:, :], pattern=[[1, S]], base=-(QT - 1) * P, channel_multiplier=-1).then_inc(far, 1)
                pool.wait_ge(far, 1)
                pool.tensor_copy(distance[:, :], distance_int[:, :]).then_inc(far, 1)
                pool.wait_ge(far, 2)
                pool.affine_select(out=distance[:, :], in_=distance[:, :], compare_op=ALU.is_ge, fill=NEG,
                                   base=(QT - 1) * P, pattern=[[-1, S]], channel_multiplier=1).then_inc(far, 1)

                def copy(t, u):
                    pool.wait_ge(norm.xnT_done, done(t))
                    pool.tensor_copy(xT[:, :, bass.ts(t, P)], norm.xnT[:, u, :, :]).then_inc(norm.copied, 1)

                tiles(pool, copy, RING)

            @block.scalar
            def _(act):
                credit(act, norm.xnT_done)
                norm.scalar_std(act)
                tiles(act, lambda t, u: norm.scalar_tile(act, t, u, copied=True), RING)

            @block.vector
            def _(dve):
                credit(dve, norm.xn_done, v_out)
                norm.vector_stats(dve)

                def values(t, u):
                    dve.wait_ge(norm.used, done(t))
                    dve.tensor_copy(v_all[:, t, :], ps_v[u % 2][:, 0:D]).then_inc(v_out, 1)

                ahead(dve, lambda t, u: norm.vector_tile(dve, t, u), values, RING, 2)
                dve.wait_ge(far, 3)
                slopes = np.float32(2.0) ** (np.float32(-8.0) / np.arange(1, H1 + 1, dtype=np.float32))
                for h in range(H1):
                    dve.tensor_scalar(biases[:, h, :], distance[:, :], float(slopes[h]), None, ALU.mult)

            @block.tensor
            def _(pe):
                credit(pe, norm.turned, norm.used)
                pe.wait_ge(w_loaded, 16)

                def values(t, u):
                    pe.wait_ge(norm.xnT_done, done(t))
                    pe.wait_ge(v_out, reuse(t, 2))
                    for c in range(DC):
                        m = pe.matmul(ps_v[u % 2][:, 0:D], norm.xnT[:, u, c, :], w_v[:, c, :],
                                      start=(c == 0), stop=(c == DC - 1))
                    m.then_inc(norm.used, 1)

                ahead(pe, lambda t, u: norm.tensor_turn(pe, t, u), values, RING, 2)


def alibi_attention(nc, ident, banks, xT, v_all, biases, Y_all, ins):
    with ExitStack() as ctx:
        sb = lambda n, s, d=F32: ctx.enter_context(nc.sbuf_tensor(n, s, d))
        sem = phase_semaphores(nc, ctx, "alibi_")
        GU = QT * HG
        UNITS = NG * GU
        w_qk = sb("w_qk", [P, NG, 2, DC, P])
        lo_rows = sb("lo_rows", [P, 1])
        q_hi = sb("q_hi", [P, 2, S], F32R)
        q_lo = sb("q_lo", [P, 2, S], F32R)
        k_masked = sb("k_masked", [P, S], F32R)
        k_split = sb("k_split", [P, 2, S], F32R)
        v_now = sb("v_now", [P, NG, QT, HG, SLOT])
        neg_scores = sb("neg_scores", [P, 8, S])
        neg_max = sb("neg_max1", [P, UNITS])
        probs = sb("probs1", [P, 8, S])
        probsT = sb("probsT1", [P, 4, S])
        yT = sb("yT", [P, S])
        recip = sb("recip1", [P, GU, 1])
        carrier = sb("carrier", [1, UNITS])
        ps_s, ps_t, ps_yT = banks[0:4], banks[4:6], banks[6]
        ps_qk = banks[7]
        mix = ps_qk.rearrange("p (n k) -> p n k", n=GU)
        w_loaded, padded, v_staged = sem("w_loaded"), sem("padded"), sem("v_staged")
        q_made, k_made, q_hi_out, k_masked_out = sem("q_made"), sem("k_made"), sem("q_hi_out"), sem("k_masked_out")
        q_out, k_out = sem("q_out"), sem("k_out")
        scored, maxed, exped, turned = sem("scored"), sem("maxed"), sem("exped"), sem("turned")
        copied = [sem("copied_even"), sem("copied_odd")]
        mixed, yT_out, turned_back, recips, normed = (
            sem(n) for n in ("mixed", "yT_out", "turned_back", "recips", "normed"))
        scale = 1.0 / float(np.sqrt(HD1))

        def unit(b, k):
            return b * UNITS + k

        def pair(b, k):
            return b * (UNITS // 2) + k // 2

        def group(b, g):
            return b * NG + g


        def batch(b, g):
            return (b + 1) % B if g == NG else b

        def slot(k):
            return k % GU // QT

        def head(k):
            return k % UNITS // QT

        def tile(k):
            return (3, 0, 2, 1)[k % QT]

        def keys(k):
            return (tile(k) + 1) * P

        with nc.Block() as block:
            @block.sync
            def _(sp):
                sp.dma_start(w_qk[:, :, :, :, :], ins["w_qk"].rearrange("g a (c p) m -> p g a c m", p=P)).then_inc(w_loaded, 16)
                sp.dma_start(lo_rows[:, :], ins["lo_rows"]).then_inc(w_loaded, 16)

            @block.gpsimd
            def _(pool):
                credit(pool, v_staged)
                pool.memset(v_now[:, :, :, :, :], 1.0).then_inc(padded, 1)
                pool.wait_ge(padded, 1)
                with pool.Fori(0, B) as b:
                    for g in range(NG):
                        pool.wait_ge(turned_back, reuse(group(b, g), NG))
                        pool.tensor_copy(v_now[:, g, :, :, 0:HD1],
                                         v_all[:, bass.ts(b, QT), g * HG * HD1:(g + 1) * HG * HD1]
                                         .rearrange("p q (j d) -> p q j d", j=HG)).then_inc(v_staged, 1)

            @block.tensor
            def _(pe):
                credit(pe, q_made, k_made, scored, turned, mixed, turned_back)

                def chunk(b, g, i, c):
                    return pe.matmul(ps_qk, w_qk[:, g % NG, i, c, :], xT[:, c, bass.ts(batch(b, g), S)],
                                     start=(c == 0), stop=(c == DC - 1))

                def queries_start(b, g):
                    pe.wait_ge(normed, reuse(group(b, g), 2))
                    chunk(b, g, 0, 0)

                def queries_end(b, g):
                    chunk(b, g, 0, 1).then_inc(q_made, 1)

                def keys_start(b, g):
                    pe.wait_ge(q_out, done(group(b, g)))
                    chunk(b, g, 1, 0)

                def keys_end(b, g):
                    chunk(b, g, 1, 1).then_inc(k_made, 1)

                def scores(b, k):
                    g = k // GU
                    if k % GU == 0:
                        pe.wait_ge(k_out, done(group(b, g)))
                    pe.wait_ge(maxed, reuse(unit(b, k), 4))
                    r, q = slot(k) * SLOT, tile(k) * P
                    to = ps_s[k % 4][:, 0:keys(k)]
                    pe.matmul(to, q_hi[r:r + SLOT, g % 2, q:q + P], k_split[r:r + SLOT, g % 2, 0:keys(k)],
                              start=True, stop=False)
                    pe.matmul(to, q_lo[r:r + HD1, g % 2, q:q + P], k_split[r:r + HD1, g % 2, 0:keys(k)],
                              start=False, stop=True).then_inc(scored, 1)

                def turn_probs(b, k):
                    pe.wait_ge(exped, done(unit(b, k)))
                    pe.wait_ge(copied[k % 2], reuse(pair(b, k), 1))
                    for j in range(tile(k) + 1):
                        m = pe.transpose(ps_t[k % 2][:, j * P:(j + 1) * P], probs[:, k % 8, j * P:(j + 1) * P],
                                         ident[:, :])
                    m.then_inc(turned, 1)

                def mixes(b, k):
                    g, q, r = k // GU, tile(k), slot(k) * SLOT
                    if k % GU == 0:
                        pe.wait_ge(v_staged, done(group(b, g)))
                        pe.wait_ge(yT_out, reuse(group(b, g), 1))
                    pe.wait_ge(copied[k % 2], done(pair(b, k)))
                    for j in range(q + 1):
                        m = pe.matmul(ps_yT[r:r + SLOT, q * P:(q + 1) * P], v_now[:, g, j, slot(k), :],
                                      probsT[:, k % 4, j * P:(j + 1) * P], start=(j == 0), stop=(j == q))
                    m.then_inc(mixed, 1)

                def turn_back(b, g):
                    pe.wait_ge(yT_out, done(group(b, g)))
                    for q in range(QT):
                        m = pe.transpose(ps_qk[:, q * P:(q + 1) * P], yT[:, q * P:(q + 1) * P], ident[:, :])
                    m.then_inc(turned_back, 1)

                pe.wait_ge(w_loaded, 32)
                for step in (queries_start, queries_end, keys_start, keys_end):
                    step(0, 0)
                for k in range(3):
                    scores(0, k)
                with pe.Fori(0, B) as b:
                    for k in range(UNITS):
                        g = k // GU
                        turn_probs(b, k)
                        scores(b, k + 3)
                        if k > 1:
                            mixes(b, k - 2)
                        if k % GU == 3 and g > 0:
                            turn_back(b, g - 1)
                        if k % GU == 5:
                            queries_start(b, g + 1)
                            queries_end(b, g + 1)
                        if k % GU == 9:
                            keys_start(b, g + 1)
                            keys_end(b, g + 1)
                    mixes(b, UNITS - 2)
                    mixes(b, UNITS - 1)
                    turn_back(b, NG - 1)

            @block.scalar
            def _(act):
                credit(act, q_hi_out, k_masked_out, exped, copied[1], yT_out)

                def queries_high(b, g):
                    act.wait_ge(q_made, done(group(b, g)))
                    act.mul(q_hi[:, g % 2, :], ps_qk, scale).then_inc(q_hi_out, 1)

                def keys_masked(b, g):
                    act.wait_ge(k_made, done(group(b, g)))
                    act.wait_ge(k_out, reuse(group(b, g), 1))
                    act.mul(k_masked[:, :], ps_qk, lo_rows[:, 0:1]).then_inc(k_masked_out, 1)

                def exps(b, k):
                    n = unit(b, k)
                    act.wait_ge(maxed, done(n))
                    act.wait_ge(turned, reuse(n, 8))
                    i = k % UNITS
                    act.activation(probs[:, k % 8, 0:keys(k)], neg_scores[:, k % 8, 0:keys(k)], ACT.Exp,
                                   bias=neg_max[:, i:i + 1], scale=-1.0).then_inc(exped, 1)

                def copy(b, k):
                    n = unit(b, k)
                    act.wait_ge(turned, done(n))
                    act.wait_ge(mixed, reuse(n, 4))
                    act.copy(probsT[:, k % 4, 0:keys(k)], ps_t[k % 2][:, 0:keys(k)]).then_inc(copied[1], 1)

                def copy_mixes(b, g):
                    act.wait_ge(mixed, done(unit(b, g * GU + GU - 1)))
                    act.wait_ge(turned_back, reuse(group(b, g), 1))
                    act.copy(yT[:, :], ps_yT).then_inc(yT_out, 1)

                act.wait_ge(w_loaded, 32)
                queries_high(0, 0)
                keys_masked(0, 0)
                exps(0, 0)
                exps(0, 1)
                with act.Fori(0, B) as b:
                    for k in range(UNITS):
                        g = k // GU
                        exps(b, k + 2)
                        if k % GU == 2 and g > 0:
                            copy_mixes(b, g - 1)
                        if k % 2:
                            copy(b, k)
                        if k % GU == 7:
                            queries_high(b, g + 1)
                        if k % GU == 10:
                            keys_masked(b, g + 1)
                    copy_mixes(b, NG - 1)

            @block.vector
            def _(dve):
                credit(dve, q_out, k_out, maxed, copied[0], normed)

                def queries_low(b, g):
                    dve.wait_ge(q_hi_out, done(group(b, g)))
                    dve.scalar_tensor_tensor(q_lo[:, g % 2, :], ps_qk, scale, q_hi[:, g % 2, :].bitcast(F32),
                                             ALU.mult, ALU.subtract).then_inc(q_out, 1)

                def keys_split(b, g):
                    dve.wait_ge(k_masked_out, done(group(b, g)))
                    dve.tensor_tensor(k_split[:, g % 2, :], ps_qk, k_masked[:, :].bitcast(F32),
                                      ALU.subtract).then_inc(k_out, 1)

                def maxes(b, k):
                    n = unit(b, k)
                    dve.wait_ge(scored, done(n))
                    dve.wait_ge(exped, reuse(n, 8))
                    i = k % UNITS
                    dve.memset(carrier[:, i:i + 1], 0.0)
                    at = (QT - 1 - tile(k)) * P
                    dve.tensor_tensor_reduce(neg_scores[:, k % 8, 0:keys(k)], ps_s[k % 4][:, 0:keys(k)],
                                             biases[:, head(k), at:at + keys(k)], -1.0, 3.0e38, ALU.add, ALU.min,
                                             neg_max[:, i:i + 1]).then_inc(maxed, 1)

                def copy(b, k):
                    n = unit(b, k)
                    dve.wait_ge(turned, done(n))
                    dve.wait_ge(mixed, reuse(n, 4))
                    dve.tensor_copy(probsT[:, k % 4, 0:keys(k)], ps_t[k % 2][:, 0:keys(k)]).then_inc(copied[0], 1)

                def norms(b, g):
                    m = group(b, g)
                    dve.wait_ge(turned_back, done(m))
                    dve.reciprocal(recip[:, :, :], mix[:, :, HD1:HD1 + 1]).then_inc(recips, 1)
                    dve.wait_ge(recips, m + 1)
                    out = Y_all[:, bass.ts(b, QT), g, :].rearrange("p q (j d) -> p q j d", j=HG)
                    dve.tensor_tensor(out, mix[:, :, 0:HD1].rearrange("p (q j) d -> p q j d", j=HG),
                                      recip[:, :, :].to_broadcast([P, GU, HD1])
                                      .rearrange("p (q j) d -> p q j d", j=HG), ALU.mult).then_inc(normed, 1)

                queries_low(0, 0)
                keys_split(0, 0)
                for k in range(3):
                    maxes(0, k)
                with dve.Fori(0, B) as b:
                    for k in range(UNITS):
                        g = k // GU
                        if k % 2 == 0:
                            copy(b, k)
                        maxes(b, k + 3)
                        if k % GU == 5 and g > 0:
                            norms(b, g - 1)
                        if k % GU == 8:
                            queries_low(b, g + 1)
                        if k % GU == 11:
                            keys_split(b, g + 1)
                    norms(b, NG - 1)


def capacity_route(nc, x, ident, eps, banks, weights, dispatched, slots, gates, ins):
    with ExitStack() as ctx:
        sb = lambda n, s, d=F32: ctx.enter_context(nc.sbuf_tensor(n, s, d))
        sem = phase_semaphores(nc, ctx, "capacity_route_")
        norm = Norm(nc, ctx, "n4", x, ident, banks[0:2], eps)
        ps_l, ps_before, ps_total = banks[2:4], banks[4], banks[5]
        w_g = sb("w_g", [P, DC, E1])
        xn_all = sb("xn_all", [P, NT, D])
        logits = sb("logits1", [P, NT, E1])
        top = sb("top1", [P, NT, 8])
        which = sb("which", [P, NT, 8], U32)
        which_f = sb("which_f", [P, NT, 2])
        expert_int = sb("expert_int", [P, E1], mybir.dt.int32)
        expert = sb("expert", [P, E1])
        onehot = sb("onehot", [P, 2, NT, E1])
        both = sb("both", [P, NT, E1])
        earlier = sb("earlier", [P, P])
        ones = sb("ones", [P, P])
        before = sb("before", [P, NT, E1])
        totals = sb("totals", [P, 2, NT, E1])
        placed = sb("placed", [P, 2, NT, E1])
        shifted = sb("shifted1", [P, NT, E1])
        total = sb("total1", [P, NT, 1])
        position = sb("position", [P, 2, NT])
        kept = sb("kept", [P, 2, NT])
        slot_f = sb("slot_f", [P, 2, NT])
        send = sb("send", [P, 2, NT], U32)
        (w1, w1_hi, w1_lo), (w2, w2_hi, w2_lo) = weights
        first_loaded, first_hi = sem("first_loaded"), sem("first_hi")
        w_loaded, logit_out, made = sem("w_loaded"), sem("logit_out"), sem("made")
        topped, step, counted, exped, sent = sem("topped"), sem("step"), sem("counted"), sem("exped"), sem("sent")

        with nc.Block() as block:
            @block.sync
            def _(sp):
                sp.dma_start(w_g[:, :, :], ins["w_g"].rearrange("(c p) k -> p c k", p=P)).then_inc(w_loaded, 16)
                sp.dma_start(w1[:, :, :], ins["w1"][0].rearrange("(c p) f -> p c f", p=P)).then_inc(first_loaded, 16)
                sp.dma_start(w2[:, :, :], ins["w2"][0].rearrange("(c p) d -> p c d", p=P)).then_inc(first_loaded, 16)

            @block.gpsimd
            def _(pool):
                credit(pool, norm.copied)
                pool.memset(ones[:, :], 1.0).then_inc(made, 1)
                pool.iota(expert_int[:, :], pattern=[[1, E1]], base=0, channel_multiplier=0).then_inc(made, 1)
                pool.wait_ge(made, 2)
                pool.tensor_copy(expert[:, :], expert_int[:, :]).then_inc(made, 1)
                pool.affine_select(out=earlier[:, :], in_=ones[:, :], compare_op=ALU.is_gt, fill=0.0, base=0,
                                   pattern=[[1, P]], channel_multiplier=-1).then_inc(made, 1)

                def copy(t, u):
                    pool.wait_ge(norm.xn_done, done(t))
                    pool.tensor_copy(xn_all[:, t, :], norm.xn[:, u, :]).then_inc(norm.copied, 1)

                tiles(pool, copy, RING)
                pool.wait_ge(norm.copied, done(NT - 1))
                pool.wait_ge(step, 9)
                for t in range(NT):
                    for i in range(2):
                        pool.indirect_dma_start(dispatched[:, :], bass.IndirectOffsetOnAxis(ap=send[:, i, t:t + 1], axis=0),
                                                xn_all[:, t, :], None, bounds_check=E1 * CAP - 1,
                                                oob_is_err=False).then_inc(sent, 16)
                pool.wait_ge(sent, 16 * 2 * NT)

            @block.scalar
            def _(act):
                credit(act, norm.xnT_done)
                norm.scalar_std(act)
                tiles(act, lambda t, u: norm.scalar_tile(act, t, u), RING)
                act.wait_ge(step, 1)
                act.activation(shifted[:, :, :], shifted[:, :, :], ACT.Exp).then_inc(exped, 1)
                act.wait_ge(first_loaded, 32)
                act.copy(w1_hi[:, :, :], w1[:, :, :]).then_inc(first_hi, 1)
                act.copy(w2_hi[:, :, :], w2[:, :, :]).then_inc(first_hi, 1)

            @block.vector
            def _(dve):
                credit(dve, norm.xn_done, logit_out)
                norm.vector_stats(dve)

                def logit(t, u):
                    dve.wait_ge(norm.used, done(t))
                    dve.tensor_copy(logits[:, t, :], ps_l[u % 2][:, 0:E1]).then_inc(logit_out, 1)

                ahead(dve, lambda t, u: norm.vector_tile(dve, t, u, copied=True), logit, RING, 2)
                dve.wait_ge(logit_out, done(NT - 1))
                for t in range(NT):
                    dve.max(top[:, t, :], logits[:, t, :]).then_inc(topped, 1)
                dve.wait_ge(topped, NT)
                dve.tensor_tensor(shifted[:, :, :], logits[:, :, :], top[:, :, 0:1].to_broadcast([P, NT, E1]),
                                  ALU.subtract).then_inc(step, 1)
                for t in range(NT):
                    dve.max_index(which[:, t, :], top[:, t, :], logits[:, t, :]).then_inc(topped, 1)
                dve.wait_ge(topped, 2 * NT)
                dve.tensor_copy(which_f[:, :, :], which[:, :, 0:2]).then_inc(step, 1)
                dve.wait_ge(step, 2)
                dve.wait_ge(made, 4)
                for i in range(2):
                    dve.tensor_tensor(onehot[:, i, :, :], which_f[:, :, i:i + 1].to_broadcast([P, NT, E1]),
                                      expert[:, :].unsqueeze(1).to_broadcast([P, NT, E1]), ALU.is_equal).then_inc(step, 1)
                dve.wait_ge(step, 4)
                dve.tensor_tensor(both[:, :, :], onehot[:, 0, :, :], onehot[:, 1, :, :], ALU.add).then_inc(step, 1)
                dve.wait_ge(counted, 1)
                dve.memset(totals[:, 0, 0, :], 0.0)
                dve.tensor_copy(totals[:, 0, 1:NT, :],
                                ps_total[:, 0:(NT - 1) * E1].rearrange("p (t e) -> p t e", e=E1)).then_inc(topped, 1)
                n, at, lag = 2 * NT + 1, 0, 1
                dve.wait_ge(topped, n)
                while lag < NT:
                    dve.tensor_copy(totals[:, 1 - at, 0:lag, :], totals[:, at, 0:lag, :])
                    dve.tensor_tensor(totals[:, 1 - at, lag:NT, :], totals[:, at, lag:NT, :],
                                      totals[:, at, 0:NT - lag, :], ALU.add).then_inc(topped, 1)
                    n, at, lag = n + 1, 1 - at, 2 * lag
                    dve.wait_ge(topped, n)
                dve.tensor_tensor(before[:, :, :], ps_before[:, 0:NT * E1].rearrange("p (t e) -> p t e", e=E1),
                                  totals[:, at, :, :], ALU.add).then_inc(step, 1)
                dve.wait_ge(step, 6)
                for i in range(2):
                    dve.tensor_tensor(placed[:, i, :, :], onehot[:, i, :, :], before[:, :, :], ALU.mult).then_inc(topped, 1)
                dve.wait_ge(topped, n + 2)
                dve.tensor_reduce(position[:, :, :], placed[:, :, :, :], AX.X, ALU.add).then_inc(step, 1)
                dve.wait_ge(step, 7)
                dve.tensor_scalar(kept[:, :, :], position[:, :, :], float(CAP), None, ALU.is_lt).then_inc(topped, 1)
                dve.scalar_tensor_tensor(out=slot_f[:, :, :], in0=which_f[:, :, :].rearrange("p t i -> p i t"),
                                         scalar=float(CAP), in1=position[:, :, :], op0=ALU.mult, op1=ALU.add) \
                    .then_inc(topped, 1)
                dve.wait_ge(topped, n + 4)
                dve.tensor_tensor(slot_f[:, :, :], slot_f[:, :, :], kept[:, :, :], ALU.mult).then_inc(topped, 1)
                dve.tensor_scalar(position[:, :, :], kept[:, :, :], -float(2 * E1 * CAP), float(2 * E1 * CAP),
                                  ALU.mult, ALU.add).then_inc(topped, 1)
                dve.wait_ge(topped, n + 6)
                dve.tensor_copy(slots[:, :, :], slot_f[:, :, :]).then_inc(step, 1)
                dve.tensor_tensor(send[:, :, :], slot_f[:, :, :], position[:, :, :], ALU.add).then_inc(step, 1)
                dve.wait_ge(exped, 1)
                dve.tensor_reduce(total[:, :, 0], shifted[:, :, :], AX.X, ALU.add).then_inc(topped, 1)
                dve.wait_ge(topped, n + 7)
                dve.reciprocal(total[:, :, :], total[:, :, :]).then_inc(topped, 1)
                for i in range(2):
                    dve.tensor_tensor(placed[:, i, :, :], onehot[:, i, :, :], shifted[:, :, :], ALU.mult).then_inc(topped, 1)
                dve.wait_ge(topped, n + 10)
                dve.tensor_reduce(gates[:, :, :], placed[:, :, :, :], AX.X, ALU.add).then_inc(topped, 1)
                dve.wait_ge(topped, n + 11)
                dve.tensor_tensor(gates[:, :, :], gates[:, :, :], kept[:, :, :], ALU.mult).then_inc(topped, 1)
                dve.wait_ge(topped, n + 12)
                dve.tensor_tensor(gates[:, :, :], gates[:, :, :],
                                  total[:, :, 0].unsqueeze(1).to_broadcast([P, 2, NT]), ALU.mult)
                for n, (w, hi, lo) in enumerate(weights):
                    dve.wait_ge(first_hi, n + 1)
                    dve.tensor_tensor(lo[:, :, :], w[:, :, :], hi[:, :, :].bitcast(F32), ALU.subtract)

            @block.tensor
            def _(pe):
                credit(pe, norm.turned, norm.used)
                pe.wait_ge(w_loaded, 16)

                def route(t, u):
                    pe.wait_ge(norm.xnT_done, done(t))
                    pe.wait_ge(logit_out, reuse(t, 2))
                    for c in range(DC):
                        m = pe.matmul(ps_l[u % 2][:, 0:E1], norm.xnT[:, u, c, :], w_g[:, c, :],
                                      start=(c == 0), stop=(c == DC - 1))
                    m.then_inc(norm.used, 1)

                ahead(pe, lambda t, u: norm.tensor_turn(pe, t, u), route, RING, 2)
                pe.wait_ge(step, 5)
                pe.wait_ge(made, 4)
                rows = both[:, :, :].rearrange("p t e -> p (t e)")
                pe.matmul(ps_before[:, 0:NT * E1], earlier[:, :], rows, start=True, stop=True)
                pe.matmul(ps_total[:, 0:NT * E1], ones[:, :], rows, start=True, stop=True).then_inc(counted, 1)


def capacity_experts(nc, ident, banks, weights, dispatched, returned, ins):
    with ExitStack() as ctx:
        sb = lambda n, s, d=F32: ctx.enter_context(nc.sbuf_tensor(n, s, d))
        sem = phase_semaphores(nc, ctx, "capacity_")
        FC = F1 // P
        HALF = CAP // 2
        (w1, w1_hi, w1_lo), (w2, w2_hi, w2_lo) = weights
        rows = sb("rows1", [P, 2, CT, D])
        rows_hi, rows_lo = sb("rows_hi", [P, DC, CAP], F32R), sb("rows_lo", [P, DC, CAP], F32R)
        hidden_hi, hidden_lo = sb("hidden1_hi", [P, FC, CAP], F32R), sb("hidden1_lo", [P, FC, CAP], F32R)
        outs = sb("outs", [P, 2, CT, D])
        ps_t, ps_h, ps_o = banks[0:2], banks[2:6], banks[6:8]
        w1_loaded, w2_loaded = sem("w1_loaded"), sem("w2_loaded")
        w1_hi_done, w1_split, w2_hi_done, w2_split = (sem(n) for n in ("w1_hi_done", "w1_split", "w2_hi_done", "w2_split"))
        rows_loaded = [sem(f"rows_loaded{u}") for u in range(2)]
        stored, outs_free = sem("stored"), sem("outs_free")
        turned, rows_hi_done, rows_split, up_done = sem("turned"), sem("rows_hi_done"), sem("rows_split"), sem("up_done")
        left_hi, right_hi, hidden_split = sem("left_hi"), sem("right_hi"), sem("hidden_split")
        down_done, out_done = sem("down_done"), sem("out_done")
        PRODUCTS = ((0, 0), (0, 1), (1, 0))

        def turns(eng, turn):
            with eng.Fori(0, E1 // 2 - 1) as ee:
                for u in range(2):
                    turn(2 * ee + u, u, False)
            turn(E1 - 2, 0, False)
            turn(E1 - 1, 1, True)

        with nc.Block() as block:
            @block.sync
            def _(sp):
                def load_rows(e, u):
                    at = dispatched[bass.ds(e * CAP, CAP), :] if not isinstance(e, int) else dispatched[e * CAP:(e + 1) * CAP, :]
                    sp.dma_start(rows[:, u, :, :], at.rearrange("(t p) d -> p t d", p=P)).then_inc(rows_loaded[u], 16)

                def load_weights(e):
                    if isinstance(e, int):
                        of1, of2 = ins["w1"][e:e + 1], ins["w2"][e:e + 1]
                    else:
                        of1, of2 = ins["w1"][bass.ds(e, 1)], ins["w2"][bass.ds(e, 1)]
                    sp.wait_ge(w1_split, reuse(e, 1))
                    sp.dma_start(w1[:, :, :], of1.rearrange("a (c p) f -> p (a c) f", p=P)).then_inc(w1_loaded, 16)
                    sp.wait_ge(w2_split, reuse(e, 1))
                    sp.dma_start(w2[:, :, :], of2.rearrange("a (c p) d -> p (a c) d", p=P)).then_inc(w2_loaded, 16)

                def turn(e, u, last):
                    if not last:
                        sp.wait_ge(turned, reuse((e + 1) * CT + CT - 1, 2 * CT))
                        load_rows(e + 1, 1 - u)
                        load_weights(e + 1)

                load_rows(0, 0)
                turns(sp, turn)

            @block.gpsimd
            def _(pool):
                credit(pool, w1_split, w2_split, outs_free)
                for s in (w1_split, w2_split):
                    pool.sem_inc(s, 1)

                def split1(e):
                    pool.wait_ge(w1_hi_done, done(e))
                    pool.tensor_tensor(w1_lo[:, :, :], w1[:, :, :], w1_hi[:, :, :].bitcast(F32),
                                       ALU.subtract).then_inc(w1_split, 1)

                def split2(e):
                    pool.wait_ge(w2_hi_done, done(e))
                    pool.tensor_tensor(w2_lo[:, :, :], w2[:, :, :], w2_hi[:, :, :].bitcast(F32),
                                       ALU.subtract).then_inc(w2_split, 1)

                def turn(e, u, last):
                    if not last:
                        split1(e + 1)
                    pool.wait_ge(out_done, done(e * CT + CT - 1))
                    at = returned[bass.ds(e * CAP, CAP), :] if not isinstance(e, int) else returned[e * CAP:(e + 1) * CAP, :]
                    pool.dma_start(at.rearrange("(t p) d -> p t d", p=P), outs[:, u, :, :]).then_inc(stored, 16)
                    if not last:
                        split2(e + 1)
                    pool.wait_ge(stored, 16 * (e + 1))
                    pool.sem_inc(outs_free, 1)

                turns(pool, turn)

            @block.tensor
            def _(pe):
                credit(pe, turned, up_done, down_done)

                def turn_rows(e, u):
                    pe.wait_ge(rows_loaded[u], 16 + 8 * (e - u))
                    for t in range(CT):
                        n = e * CT + t
                        pe.wait_ge(rows_split, reuse(n, 2))
                        for c in range(DC):
                            m = pe.transpose(ps_t[t % 2][:, c * P:(c + 1) * P], rows[:, u, t, c * P:(c + 1) * P],
                                             ident[:, :])
                        m.then_inc(turned, 1)

                def up(e):
                    pe.wait_ge(w1_split, done(e))
                    pe.wait_ge(rows_split, done(e * CT + CT - 1))
                    ws, xs = (w1_hi, w1_lo), (rows_hi, rows_lo)
                    for f in range(FC):
                        pe.wait_ge(hidden_split, reuse(e * FC + f, 2))
                        for i in range(2):
                            for j, (jw, jx) in enumerate(PRODUCTS):
                                for c in range(DC):
                                    m = pe.matmul(ps_h[2 * (f % 2) + i][:, 0:HALF], ws[jw][:, c, f * P:(f + 1) * P],
                                                  xs[jx][:, c, i * HALF:(i + 1) * HALF],
                                                  start=(j == 0 and c == 0), stop=(j == 2 and c == DC - 1))
                        m.then_inc(up_done, 1)

                def down(e):
                    pe.wait_ge(w2_split, done(e))
                    pe.wait_ge(hidden_split, done(e * FC + FC - 1))
                    hs, ws = (hidden_hi, hidden_lo), (w2_hi, w2_lo)
                    for t in range(CT):
                        pe.wait_ge(out_done, reuse(e * CT + t, 2))
                        for f in range(FC):
                            for j, (jh, jw) in enumerate(PRODUCTS):
                                m = pe.matmul(ps_o[t % 2][:, 0:D], hs[jh][:, f, t * P:(t + 1) * P], ws[jw][:, f, :],
                                              start=(f == 0 and j == 0), stop=(f == FC - 1 and j == 2))
                        m.then_inc(down_done, 1)

                def turn(e, u, last):
                    up(e)
                    if not last:
                        turn_rows(e + 1, 1 - u)
                    down(e)

                turn_rows(0, 0)
                turns(pe, turn)

            @block.scalar
            def _(act):
                credit(act, w1_hi_done, w2_hi_done, rows_hi_done, left_hi)
                for s in (w1_hi_done, w2_hi_done):
                    act.sem_inc(s, 1)

                def high1(e):
                    act.wait_ge(w1_loaded, 16 * e)
                    act.wait_ge(up_done, reuse(e * FC + FC - 1, FC))
                    act.copy(w1_hi[:, :, :], w1[:, :, :]).then_inc(w1_hi_done, 1)

                def high2(e):
                    act.wait_ge(w2_loaded, 16 * e)
                    act.wait_ge(down_done, reuse(e * CT + CT - 1, CT))
                    act.copy(w2_hi[:, :, :], w2[:, :, :]).then_inc(w2_hi_done, 1)

                def rows_high(e):
                    for t in range(CT):
                        act.wait_ge(turned, done(e * CT + t))
                        act.copy(rows_hi[:, :, t * P:(t + 1) * P],
                                 ps_t[t % 2][:, 0:D].rearrange("p (c k) -> p c k", c=DC)).then_inc(rows_hi_done, 1)

                def turn(e, u, last):
                    for f in range(FC):
                        act.wait_ge(up_done, done(e * FC + f))
                        act.activation(hidden_hi[:, f, 0:HALF], ps_h[2 * (f % 2)][:, 0:HALF], ACT.Relu).then_inc(left_hi, 1)
                    if not last:
                        rows_high(e + 1)
                        high1(e + 1)
                        high2(e + 1)

                rows_high(0)
                turns(act, turn)

            @block.vector
            def _(dve):
                credit(dve, rows_split, right_hi, hidden_split, out_done)

                def rows_low(e):
                    for t in range(CT):
                        dve.wait_ge(rows_hi_done, done(e * CT + t))
                        at = slice(t * P, (t + 1) * P)
                        dve.tensor_tensor(rows_lo[:, :, at], ps_t[t % 2][:, 0:D].rearrange("p (c k) -> p c k", c=DC),
                                          rows_hi[:, :, at].bitcast(F32), ALU.subtract).then_inc(rows_split, 1)

                def low(f, i):
                    at = slice(i * HALF, (i + 1) * HALF)
                    return dve.scalar_tensor_tensor(hidden_lo[:, f, at], ps_h[2 * (f % 2) + i][:, 0:HALF], 0.0,
                                                    hidden_hi[:, f, at].bitcast(F32), ALU.max, ALU.subtract)

                def turn(e, u, last):
                    for f in range(FC):
                        n = e * FC + f
                        dve.wait_ge(up_done, done(n))
                        dve.tensor_scalar(hidden_hi[:, f, HALF:CAP], ps_h[2 * (f % 2) + 1][:, 0:HALF], 0.0, None,
                                          ALU.max).then_inc(right_hi, 1)
                        dve.wait_ge(left_hi, done(n))
                        low(f, 0)
                        dve.wait_ge(right_hi, done(n))
                        low(f, 1).then_inc(hidden_split, 1)
                    if not last:
                        rows_low(e + 1)
                    for t in range(CT):
                        dve.wait_ge(down_done, done(e * CT + t))
                        if t == 0:
                            dve.wait_ge(outs_free, reuse(e, 2))
                        dve.tensor_copy(outs[:, u, t, :], ps_o[t % 2][:, 0:D]).then_inc(out_done, 1)

                rows_low(0)
                turns(dve, turn)


def combine(nc, x, returned, slots, gates, out):
    with ExitStack() as ctx:
        sem = phase_semaphores(nc, ctx, "combine_")
        first = ctx.enter_context(nc.sbuf_tensor("first", [P, NT, D], F32))
        second = ctx.enter_context(nc.sbuf_tensor("second", [P, NT, D], F32))
        RING = 8
        fetched = [[sem(f"fetched{i}_{t}") for t in range(RING)] for i in range(2)]
        half, summed, stored = sem("half"), sem("summed"), sem("stored")

        with nc.Block() as block:
            @block.gpsimd
            def _(pool):
                for t in range(NT):
                    if t >= RING:
                        pool.wait_ge(summed, t - RING + 1)
                    for i, rows in ((0, first), (1, second)):
                        pool.indirect_dma_start(rows[:, t, :], None, returned[:, :],
                                                bass.IndirectOffsetOnAxis(ap=slots[:, i, t:t + 1], axis=0),
                                                bounds_check=E1 * CAP - 1, oob_is_err=False) \
                            .then_inc(fetched[i][t % RING], 16)

            @block.vector
            def _(dve):
                for t in range(NT):
                    dve.wait_ge(fetched[0][t % RING], 16 * (t // RING + 1))
                    dve.scalar_tensor_tensor(out=x[:, t, :], in0=first[:, t, :], scalar=gates[:, 0, t:t + 1],
                                             in1=x[:, t, :], op0=ALU.mult, op1=ALU.add).then_inc(half, 1)
                    dve.wait_ge(half, t + 1)
                    dve.wait_ge(fetched[1][t % RING], 16 * (t // RING + 1))
                    dve.scalar_tensor_tensor(out=x[:, t, :], in0=second[:, t, :], scalar=gates[:, 1, t:t + 1],
                                             in1=x[:, t, :], op0=ALU.mult, op1=ALU.add).then_inc(summed, 1)

            @block.sync
            def _(sp):
                outv = out.rearrange("b (t p) d -> p (b t) d", p=P)
                for g in range(NT // 2):
                    sp.wait_ge(summed, 2 * g + 2)
                    sp.dma_start(outv[:, 2 * g:2 * g + 2, :], x[:, 2 * g:2 * g + 2, :]).then_inc(stored, 16)
                sp.wait_ge(stored, 16 * (NT // 2))


def two_layers(nc, ins, out):
    with ExitStack() as ctx:
        sb = lambda n, s, d=F32: ctx.enter_context(nc.sbuf_tensor(n, s, d))
        x = sb("x", [P, NT, D])
        ident = sb("ident", [P, P])
        eps = sb("eps", [P, 1])
        psum = ctx.enter_context(nc.psum_tensor("psum", [P, 8 * 512], F32))
        banks = [psum[:, k * 512:(k + 1) * 512] for k in range(8)]
        comb_dram = nc.dram_tensor("comb_dram", [E0 + 2, NT * P], F32, kind="Internal").ap()
        dispatched = nc.dram_tensor("dispatched_dram", [E1 * CAP, D], F32, kind="Internal").ap()
        returned = nc.dram_tensor("returned_dram", [E1 * CAP, D], F32, kind="Internal").ap()

        with ExitStack() as latent:
            sl = lambda n, s, d=F32: latent.enter_context(nc.sbuf_tensor(n, s, d))
            UT_all = sl("UT_all", [P, B * (H0 // 2) * S])
            N_all = sl("N_all", [P, H0 // 2, D])
            bias_out = sl("bias_out", [1, D])
            c_rows = sl("c_rows", [P, NT, KV])
            c_first = sl("c_first", [SPLIT, B * S], F32R)
            c_second = sl("c_second", [P, B * S], F32R)
            cqT = sl("cqT", [P, 2, B * S])
            A_all = sl("A_all", [P, H0, 2, KA])
            latent_prepare(nc, x, ident, eps, banks, c_rows, c_first, c_second, cqT, A_all, N_all, bias_out, ins)
            latent_attention(nc, ident, banks, c_rows, c_first, c_second, cqT, A_all, UT_all, dispatched)
            latent_out(nc, x, psum, UT_all, N_all, bias_out)

        with ExitStack() as mixture:
            xT_hi, xT_lo = (mixture.enter_context(nc.sbuf_tensor(n, [P, DC, B * S], F32R)) for n in ("xT_hi", "xT_lo"))
            experts_prepare(nc, x, ident, eps, banks, xT_hi, xT_lo, comb_dram, ins)
            experts(nc, x, psum, xT_hi, xT_lo, comb_dram, ins)

        with ExitStack() as alibi:
            sl = lambda n, s: alibi.enter_context(nc.sbuf_tensor(n, s, F32))
            xT = sl("xT1", [P, DC, B * S])
            v_all = sl("v_all", [P, NT, D])
            biases = sl("biases", [P, H1, S])
            Y_all = sl("Y_all", [P, NT, NG, HG * HD1])
            w_out1 = sl("w_out1", [P, DC, D])
            alibi_prepare(nc, x, ident, eps, banks, xT, v_all, biases, w_out1, ins)
            alibi_attention(nc, ident, banks, xT, v_all, biases, Y_all, ins)
            project_out(nc, "out1", x, ident, psum, Y_all[:, :, :, :].rearrange("p t g k -> p t (g k)"), DC, w_out1)

        slots = sb("slots", [P, 2, NT], U32)
        gates = sb("gates", [P, 2, NT])
        with ExitStack() as capacity:
            weights = [[capacity.enter_context(nc.sbuf_tensor(n + part, shape, d))
                        for part, d in (("", F32), ("_hi", F32R), ("_lo", F32R))]
                       for n, shape in (("w1", [P, DC, F1]), ("w2", [P, F1 // P, D]))]
            capacity_route(nc, x, ident, eps, banks, weights, dispatched, slots, gates, ins)
            capacity_experts(nc, ident, banks, weights, dispatched, returned, ins)
        combine(nc, x, returned, slots, gates, out)


def layout(**w):
    a = {n: np.asarray(v) for n, v in w.items()}
    at, f0 = "L0_attn_", "L0_ffn_"
    out = {"hidden": a[at + "hidden_states"]}
    out["w_dkv"], out["w_dq"] = a[at + "W_DKV_w"].T, a[at + "W_DQ_w"].T
    out["b_dkv"], out["b_dq"], out["b_o"] = a[at + "W_DKV_b"], a[at + "W_DQ_b"], a[at + "W_O_b"]
    for k in ("UQ", "UK", "UV"):
        out["w_" + k.lower()] = np.concatenate([a[f"{at}W_{k}_w"], a[f"{at}W_{k}_b"][:, None]], 1)
    out["w_o"] = a[at + "W_O_w"].T
    out["w_router"] = np.concatenate([a[f0 + "router_w"], a[f0 + "shared_expert_gate_w"]], 0).T
    gate_up = a[f0 + "gate_up_proj"].reshape(E0, 2, I0, D)
    shared = np.stack([a[f0 + "shared_gate_w"], a[f0 + "shared_up_w"]])[None]
    gate_up = np.concatenate([gate_up, shared, np.zeros_like(shared)], 0)
    out["w_gu0"] = gate_up.reshape(E0 // 2 + 1, 2, 2, I0, D).transpose(0, 2, 4, 1, 3).reshape(E0 // 2 + 1, 2, D, P)
    down = np.concatenate([a[f0 + "down_proj"], a[f0 + "shared_down_w"][None],
                           np.zeros_like(a[f0 + "shared_down_w"][None])], 0)
    out["w_d0"] = down.transpose(0, 2, 1).reshape(E0 // 2 + 1, P, D)
    qkv = a["L1_attn_W_qkv"]
    qk = qkv[:, 0:2 * D].reshape(D, 2, NG, HG, HD1).transpose(2, 1, 0, 3, 4)
    out["w_qk"] = np.concatenate([qk, qk], -1).reshape(NG, 2, D, P)
    out["lo_rows"] = (np.arange(P) % SLOT >= HD1).astype(np.float32)[:, None]
    out["w_v"], out["w_out1"] = qkv[:, 2 * D:], a["L1_attn_W_o"]
    out["w_g"], out["w1"], out["w2"] = a["L1_ffn_Wg"], a["L1_ffn_w1"], a["L1_ffn_w2"]
    return {n: np.ascontiguousarray(v) for n, v in out.items()}


def kernel(**inputs):
    import concourse.bacc as bacc
    from concourse.bass_utils import run_bass_kernel_spmd

    nc = bacc.Bacc("TRN2", target_bir_lowering=False, num_devices=1)
    arrays = layout(**inputs)
    ins = {n: nc.dram_tensor("in_" + n, a.shape, mybir.dt.from_np(a.dtype), kind="ExternalInput").ap()
           for n, a in arrays.items()}
    out = nc.dram_tensor("out", (B, S, D), F32, kind="ExternalOutput").ap()
    two_layers(nc, ins, out)
    r = run_bass_kernel_spmd(nc, [{"in_" + n: a for n, a in arrays.items()}], core_ids=[0])
    return r.results[0]["out"]
```
